# Optimizing a Trainium2 kernel written in Bass

```python
import numpy as np
import jax
import jax.numpy as jnp

def _softmax(x, axis=-1):
    return jax.nn.softmax(x, axis=axis)

def _gelu(x):
    return jax.nn.gelu(x, approximate=True)

def _silu(x):
    return jax.nn.silu(x)

def _sigmoid(x):
    return jax.nn.sigmoid(x)

def _layernorm(x, axis=-1, eps=1e-05):
    m = jnp.mean(x, axis=axis, keepdims=True)
    v = jnp.var(x, axis=axis, keepdims=True)
    return (x - m) / jnp.sqrt(v + eps)

def _scatter_add(tgt, idx, src, axis=0):
    return tgt.at[idx].add(src)

def _segment_sum(src, seg, n):
    return jax.ops.segment_sum(src, seg, n)
kernel_name = 'mk_macaron_d2_jaxref_r8_6f1f97'

def setup_inputs(seed: int=0):
    np.random.seed(seed)
    _w = jnp.asarray

    def _L0_attn_setup():
        import jax, jax.numpy as jnp
        import numpy as np
        B, N, E, H = (1, 512, 256, 16)
        D = E // H
        DEGREE = 4
        LN_EPS = 1e-05
        ROPE_BASE = 10000.0

        def rope_cos_sin(n, d):
            inv_freq = 1.0 / ROPE_BASE ** (jnp.arange(0, d, 2, dtype=jnp.float32) / d)
            t = jnp.arange(n, dtype=jnp.float32)[:, None] * inv_freq[None, :]
            return (jnp.cos(t), jnp.sin(t))

        def apply_rope(x, cos, sin):
            x1, x2 = jnp.split(x, 2, axis=-1)
            c = cos[None, :, None, :]
            s = sin[None, :, None, :]
            return jnp.concatenate([x1 * c - x2 * s, x1 * s + x2 * c], axis=-1)

        def layernorm(x, scale, bias, eps=LN_EPS):
            m = jnp.mean(x, axis=-1, keepdims=True)
            v = jnp.var(x, axis=-1, keepdims=True)
            return (x - m) * jax.lax.rsqrt(v + eps) * scale + bias

        def polynomial_attention(q, k, v, degree, is_causal):
            a = jnp.einsum('bhnd,bhmd->bhnm', q, k) ** degree
            if is_causal:
                a = jnp.tril(a)
            denom = jnp.sum(a, axis=-1, keepdims=True)
            return jnp.einsum('bhnm,bhmd->bhnd', a / denom, v)
        key = jax.random.key(seed)
        k0, k1, k2 = jax.random.split(key, 3)
        x = jax.random.normal(k0, (B, N, E), dtype=jnp.float32)
        w_qkv = jax.random.normal(k1, (E, 3 * E), dtype=jnp.float32) * (1.0 / np.sqrt(E))
        w_out = jax.random.normal(k2, (E, E), dtype=jnp.float32) * (1.0 / np.sqrt(E))
        ln_scale = jnp.ones((D,), dtype=jnp.float32)
        ln_bias = jnp.zeros((D,), dtype=jnp.float32)
        return {'x': x, 'w_qkv': w_qkv, 'w_out': w_out, 'ln_scale': ln_scale, 'ln_bias': ln_bias}
    _L0_attn_in = _L0_attn_setup()

    def _L0_ffn_setup():
        import jax, jax.numpy as jnp
        import numpy as np
        NUM_EXPERTS = 8
        RANK = 16
        TOP_K = 2
        SCALING = 32.0 / RANK
        IN_F = 256
        OUT_F = 256
        key = jax.random.key(seed)
        k1, k2, k3, k4, k5 = jax.random.split(key, 5)
        B, T = (4, 256)
        x = jax.random.normal(k1, (B, T, IN_F), dtype=jnp.float32)
        bound_w = 1.0 / np.sqrt(IN_F)
        weight = jax.random.uniform(k2, (OUT_F, IN_F), jnp.float32, -bound_w, bound_w)
        lora_A = jax.random.uniform(k3, (NUM_EXPERTS, RANK, IN_F), jnp.float32, -bound_w, bound_w)
        lora_B = 0.02 * jax.random.normal(k4, (NUM_EXPERTS, OUT_F, RANK), dtype=jnp.float32)
        router_w = jax.random.uniform(k5, (NUM_EXPERTS, IN_F), jnp.float32, -bound_w, bound_w)
        return {'x': x, 'weight': weight, 'lora_A': lora_A, 'lora_B': lora_B, 'router_w': router_w}
    _L0_ffn_in = _L0_ffn_setup()

    def _L1_attn_setup():
        import jax, jax.numpy as jnp
        import numpy as np
        EMBED_DIM = 256
        NUM_HEADS = 16
        HEAD_DIM = EMBED_DIM // NUM_HEADS // 2
        DEPTH = 12
        LAMBDA_INIT = 0.8 - 0.6 * float(np.exp(-0.3 * DEPTH))
        EPS = 1e-05
        key = jax.random.key(seed)
        ks = jax.random.split(key, 9)
        B, T, E = (2, 256, EMBED_DIM)
        s = 0.02
        return {'x': jax.random.normal(ks[0], (B, T, E), jnp.float32), 'Wq': jax.random.normal(ks[1], (E, E), jnp.float32) * s, 'Wk': jax.random.normal(ks[2], (E, E), jnp.float32) * s, 'Wv': jax.random.normal(ks[3], (E, E), jnp.float32) * s, 'Wo': jax.random.normal(ks[4], (E, E), jnp.float32) * s, 'lambda_q1': jax.random.normal(ks[5], (HEAD_DIM,), jnp.float32) * 0.1, 'lambda_k1': jax.random.normal(ks[6], (HEAD_DIM,), jnp.float32) * 0.1, 'lambda_q2': jax.random.normal(ks[7], (HEAD_DIM,), jnp.float32) * 0.1, 'lambda_k2': jax.random.normal(ks[8], (HEAD_DIM,), jnp.float32) * 0.1, 'subln_weight': jnp.ones((2 * HEAD_DIM,), jnp.float32)}
    _L1_attn_in = _L1_attn_setup()

    def _L1_ffn_setup():
        import jax, jax.numpy as jnp
        import numpy as np
        from jax import lax
        DIM = 256
        INTER = 176
        N_EXPERTS = 32
        TOP_K = 6
        N_SHARED = 2
        CAPACITY = 256
        ROUTE_SCALE = 1.0

        def _gate(xf, gate_w):
            logits = xf @ gate_w.T
            scores = jax.nn.softmax(logits.astype(jnp.float32), axis=-1)
            top_w, top_i = lax.top_k(scores, TOP_K)
            return ((top_w * ROUTE_SCALE).astype(xf.dtype), top_i)

        def _moe(xf, gate_w, w1, w2, w3):
            T, D = xf.shape
            E, CAP = (N_EXPERTS, CAPACITY)
            top_w, top_i = _gate(xf, gate_w)
            e_flat = top_i.reshape(-1)
            t_flat = jnp.repeat(jnp.arange(T), TOP_K)
            w_flat = top_w.reshape(-1)
            order = jnp.argsort(e_flat)
            e_s, t_s, w_s = (e_flat[order], t_flat[order], w_flat[order])
            counts = jnp.zeros((E,), jnp.int32).at[e_s].add(1)
            starts = jnp.concatenate([jnp.zeros((1,), jnp.int32), jnp.cumsum(counts)[:-1]])
            pos = jnp.arange(T * TOP_K, dtype=jnp.int32) - starts[e_s]
            valid = pos < CAP
            buf_idx = jnp.where(valid, e_s * CAP + pos, E * CAP)
            xbuf = jnp.zeros((E * CAP + 1, D), xf.dtype).at[buf_idx].set(xf[t_s])
            xb = xbuf[:E * CAP].reshape(E, CAP, D)
            h = jax.nn.silu(jnp.einsum('ecd,edi->eci', xb, w1)) * jnp.einsum('ecd,edi->eci', xb, w3)
            ob = jnp.einsum('eci,eid->ecd', h, w2).reshape(E * CAP, D)
            ob = jnp.concatenate([ob, jnp.zeros((1, D), ob.dtype)], axis=0)
            y_pairs = ob[buf_idx] * w_s[:, None]
            y = jnp.zeros((T, D), xf.dtype).at[t_s].add(y_pairs)
            return y
        key = jax.random.key(seed)
        ks = jax.random.split(key, 9)
        B, S = (4, 256)
        si = INTER * N_SHARED
        inputs = {'x': jax.random.normal(ks[0], (B, S, DIM), jnp.float32), 'gate_w': jax.random.normal(ks[1], (N_EXPERTS, DIM), jnp.float32), 'w1': jax.random.normal(ks[2], (N_EXPERTS, DIM, INTER), jnp.float32) * DIM ** (-0.5), 'w2': jax.random.normal(ks[3], (N_EXPERTS, INTER, DIM), jnp.float32) * INTER ** (-0.5), 'w3': jax.random.normal(ks[4], (N_EXPERTS, DIM, INTER), jnp.float32) * DIM ** (-0.5), 'sw1': jax.random.normal(ks[5], (DIM, si), jnp.float32) * DIM ** (-0.5), 'sw2': jax.random.normal(ks[6], (si, DIM), jnp.float32) * si ** (-0.5), 'sw3': jax.random.normal(ks[7], (DIM, si), jnp.float32) * DIM ** (-0.5)}
        return inputs
    _L1_ffn_in = _L1_ffn_setup()
    _d = {'L0_attn_x': _L0_attn_in['x'], 'L0_attn_w_qkv': _L0_attn_in['w_qkv'], 'L0_attn_w_out': _L0_attn_in['w_out'], 'L0_attn_ln_scale': _L0_attn_in['ln_scale'], 'L0_attn_ln_bias': _L0_attn_in['ln_bias'], 'L0_ffn_weight': _L0_ffn_in['weight'], 'L0_ffn_lora_A': _L0_ffn_in['lora_A'], 'L0_ffn_lora_B': _L0_ffn_in['lora_B'], 'L0_ffn_router_w': _L0_ffn_in['router_w'], 'L1_attn_Wq': _L1_attn_in['Wq'], 'L1_attn_Wk': _L1_attn_in['Wk'], 'L1_attn_Wv': _L1_attn_in['Wv'], 'L1_attn_Wo': _L1_attn_in['Wo'], 'L1_attn_lambda_q1': _L1_attn_in['lambda_q1'], 'L1_attn_lambda_k1': _L1_attn_in['lambda_k1'], 'L1_attn_lambda_q2': _L1_attn_in['lambda_q2'], 'L1_attn_lambda_k2': _L1_attn_in['lambda_k2'], 'L1_attn_subln_weight': _L1_attn_in['subln_weight'], 'L1_ffn_gate_w': _L1_ffn_in['gate_w'], 'L1_ffn_w1': _L1_ffn_in['w1'], 'L1_ffn_w2': _L1_ffn_in['w2'], 'L1_ffn_w3': _L1_ffn_in['w3'], 'L1_ffn_sw1': _L1_ffn_in['sw1'], 'L1_ffn_sw2': _L1_ffn_in['sw2'], 'L1_ffn_sw3': _L1_ffn_in['sw3']}
    _x0 = _d['L0_attn_x']
    _d['L0_attn_x'] = jax.random.normal(jax.random.fold_in(jax.random.key(seed), 1), (2, 512, 256), dtype=_x0.dtype)
    del _x0
    return _d

def reference(L0_attn_x, L0_attn_w_qkv, L0_attn_w_out, L0_attn_ln_scale, L0_attn_ln_bias, L0_ffn_weight, L0_ffn_lora_A, L0_ffn_lora_B, L0_ffn_router_w, L1_attn_Wq, L1_attn_Wk, L1_attn_Wv, L1_attn_Wo, L1_attn_lambda_q1, L1_attn_lambda_k1, L1_attn_lambda_q2, L1_attn_lambda_k2, L1_attn_subln_weight, L1_ffn_gate_w, L1_ffn_w1, L1_ffn_w2, L1_ffn_w3, L1_ffn_sw1, L1_ffn_sw2, L1_ffn_sw3):

    def _L0_attn_ref(x, w_qkv, w_out, ln_scale, ln_bias):
        import jax, jax.numpy as jnp
        import numpy as np
        B, N, E, H = (1, 512, 256, 16)
        D = E // H
        DEGREE = 4
        LN_EPS = 1e-05
        ROPE_BASE = 10000.0

        def rope_cos_sin(n, d):
            inv_freq = 1.0 / ROPE_BASE ** (jnp.arange(0, d, 2, dtype=jnp.float32) / d)
            t = jnp.arange(n, dtype=jnp.float32)[:, None] * inv_freq[None, :]
            return (jnp.cos(t), jnp.sin(t))

        def apply_rope(x, cos, sin):
            x1, x2 = jnp.split(x, 2, axis=-1)
            c = cos[None, :, None, :]
            s = sin[None, :, None, :]
            return jnp.concatenate([x1 * c - x2 * s, x1 * s + x2 * c], axis=-1)

        def layernorm(x, scale, bias, eps=LN_EPS):
            m = jnp.mean(x, axis=-1, keepdims=True)
            v = jnp.var(x, axis=-1, keepdims=True)
            return (x - m) * jax.lax.rsqrt(v + eps) * scale + bias

        def polynomial_attention(q, k, v, degree, is_causal):
            a = jnp.einsum('bhnd,bhmd->bhnm', q, k) ** degree
            if is_causal:
                a = jnp.tril(a)
            denom = jnp.sum(a, axis=-1, keepdims=True)
            return jnp.einsum('bhnm,bhmd->bhnd', a / denom, v)
        b, n, e = x.shape
        proj = x @ w_qkv
        q, k, v = jnp.split(proj, 3, axis=-1)
        q = q.reshape(b, n, H, D)
        k = k.reshape(b, n, H, D)
        v = v.reshape(b, n, H, D)
        cos, sin = rope_cos_sin(n, D)
        q = apply_rope(q, cos, sin)
        k = apply_rope(k, cos, sin)
        q = q.transpose(0, 2, 1, 3)
        k = k.transpose(0, 2, 1, 3)
        v = v.transpose(0, 2, 1, 3)
        q = layernorm(q, ln_scale, ln_bias)
        k = layernorm(k, ln_scale, ln_bias)
        out = polynomial_attention(q, k, v, DEGREE, True)
        out = out.transpose(0, 2, 1, 3).reshape(b, n, e)
        out = out @ w_out
        return out

    def _L0_ffn_ref(x, weight, lora_A, lora_B, router_w):
        import jax, jax.numpy as jnp
        import numpy as np
        NUM_EXPERTS = 8
        RANK = 16
        TOP_K = 2
        SCALING = 32.0 / RANK
        IN_F = 256
        OUT_F = 256
        B, T, D = x.shape
        N = B * T
        base = jnp.einsum('btd,od->bto', x, weight)
        logits = jnp.einsum('btd,ed->bte', x, router_w)
        probs = jax.nn.softmax(logits, axis=-1)
        topk_vals, topk_idx = jax.lax.top_k(probs, TOP_K)
        topk_vals = topk_vals / topk_vals.sum(axis=-1, keepdims=True)
        w_dense = jnp.zeros((N, NUM_EXPERTS), dtype=x.dtype).at[jnp.arange(N)[:, None], topk_idx.reshape(N, TOP_K)].set(topk_vals.reshape(N, TOP_K))
        x_flat = x.reshape(N, D)
        Ax = jnp.einsum('nd,erd->ner', x_flat, lora_A)
        expert_out = jnp.einsum('ner,ne,eor->no', Ax, w_dense, lora_B) * SCALING
        return base + expert_out.reshape(B, T, OUT_F)

    def _L1_attn_ref(x, Wq, Wk, Wv, Wo, lambda_q1, lambda_k1, lambda_q2, lambda_k2, subln_weight):
        import jax, jax.numpy as jnp
        import numpy as np
        EMBED_DIM = 256
        NUM_HEADS = 16
        HEAD_DIM = EMBED_DIM // NUM_HEADS // 2
        DEPTH = 12
        LAMBDA_INIT = 0.8 - 0.6 * float(np.exp(-0.3 * DEPTH))
        EPS = 1e-05
        B, T, E = x.shape
        H, hd = (NUM_HEADS, HEAD_DIM)
        scaling = hd ** (-0.5)
        q = (x @ Wq.T).reshape(B, T, H, 2, hd)
        k = (x @ Wk.T).reshape(B, T, H, 2, hd)
        v = (x @ Wv.T).reshape(B, T, H, 2 * hd)
        q1, q2 = (q[:, :, :, 0], q[:, :, :, 1])
        k1, k2 = (k[:, :, :, 0], k[:, :, :, 1])
        p1 = jax.nn.softmax(jnp.einsum('bthd,bshd->bhts', q1, k1) * scaling, axis=-1)
        p2 = jax.nn.softmax(jnp.einsum('bthd,bshd->bhts', q2, k2) * scaling, axis=-1)
        attn1 = jnp.einsum('bhts,bshe->bthe', p1, v)
        attn2 = jnp.einsum('bhts,bshe->bthe', p2, v)
        lambda_1 = jnp.exp(jnp.sum(lambda_q1 * lambda_k1))
        lambda_2 = jnp.exp(jnp.sum(lambda_q2 * lambda_k2))
        lambda_full = lambda_1 - lambda_2 + LAMBDA_INIT
        attn = attn1 - lambda_full * attn2
        rms = jax.lax.rsqrt(jnp.mean(attn * attn, axis=-1, keepdims=True) + EPS)
        attn = attn * rms * subln_weight
        attn = attn * (1.0 - LAMBDA_INIT)
        attn = attn.reshape(B, T, H * 2 * hd)
        return attn @ Wo.T

    def _L1_ffn_ref(x, gate_w, w1, w2, w3, sw1, sw2, sw3):
        import jax, jax.numpy as jnp
        import numpy as np
        from jax import lax
        DIM = 256
        INTER = 176
        N_EXPERTS = 32
        TOP_K = 6
        N_SHARED = 2
        CAPACITY = 256
        ROUTE_SCALE = 1.0

        def _gate(xf, gate_w):
            logits = xf @ gate_w.T
            scores = jax.nn.softmax(logits.astype(jnp.float32), axis=-1)
            top_w, top_i = lax.top_k(scores, TOP_K)
            return ((top_w * ROUTE_SCALE).astype(xf.dtype), top_i)

        def _moe(xf, gate_w, w1, w2, w3):
            T, D = xf.shape
            E, CAP = (N_EXPERTS, CAPACITY)
            top_w, top_i = _gate(xf, gate_w)
            e_flat = top_i.reshape(-1)
            t_flat = jnp.repeat(jnp.arange(T), TOP_K)
            w_flat = top_w.reshape(-1)
            order = jnp.argsort(e_flat)
            e_s, t_s, w_s = (e_flat[order], t_flat[order], w_flat[order])
            counts = jnp.zeros((E,), jnp.int32).at[e_s].add(1)
            starts = jnp.concatenate([jnp.zeros((1,), jnp.int32), jnp.cumsum(counts)[:-1]])
            pos = jnp.arange(T * TOP_K, dtype=jnp.int32) - starts[e_s]
            valid = pos < CAP
            buf_idx = jnp.where(valid, e_s * CAP + pos, E * CAP)
            xbuf = jnp.zeros((E * CAP + 1, D), xf.dtype).at[buf_idx].set(xf[t_s])
            xb = xbuf[:E * CAP].reshape(E, CAP, D)
            h = jax.nn.silu(jnp.einsum('ecd,edi->eci', xb, w1)) * jnp.einsum('ecd,edi->eci', xb, w3)
            ob = jnp.einsum('eci,eid->ecd', h, w2).reshape(E * CAP, D)
            ob = jnp.concatenate([ob, jnp.zeros((1, D), ob.dtype)], axis=0)
            y_pairs = ob[buf_idx] * w_s[:, None]
            y = jnp.zeros((T, D), xf.dtype).at[t_s].add(y_pairs)
            return y
        shape = x.shape
        xf = x.reshape(-1, DIM)
        y = _moe(xf, gate_w, w1, w2, w3)
        shared = jax.nn.silu(xf @ sw1) * (xf @ sw3) @ sw2
        return (y + shared).reshape(shape)
    x = L0_attn_x
    x = x + 0.5 * _L0_ffn_ref(_layernorm(x, axis=-1), L0_ffn_weight, L0_ffn_lora_A, L0_ffn_lora_B, L0_ffn_router_w)
    x = x + _L0_attn_ref(_layernorm(x, axis=-1), L0_attn_w_qkv, L0_attn_w_out, L0_attn_ln_scale, L0_attn_ln_bias)
    x = x + 0.5 * _L0_ffn_ref(_layernorm(x, axis=-1), L0_ffn_weight, L0_ffn_lora_A, L0_ffn_lora_B, L0_ffn_router_w)
    x = x + 0.5 * _L1_ffn_ref(_layernorm(x, axis=-1), L1_ffn_gate_w, L1_ffn_w1, L1_ffn_w2, L1_ffn_w3, L1_ffn_sw1, L1_ffn_sw2, L1_ffn_sw3)
    x = x + _L1_attn_ref(_layernorm(x, axis=-1), L1_attn_Wq, L1_attn_Wk, L1_attn_Wv, L1_attn_Wo, L1_attn_lambda_q1, L1_attn_lambda_k1, L1_attn_lambda_q2, L1_attn_lambda_k2, L1_attn_subln_weight)
    x = x + 0.5 * _L1_ffn_ref(_layernorm(x, axis=-1), L1_ffn_gate_w, L1_ffn_w1, L1_ffn_w2, L1_ffn_w3, L1_ffn_sw1, L1_ffn_sw2, L1_ffn_sw3)
    return x

_drawn_inputs = setup_inputs


def setup_inputs(seed=0):
    import zlib

    import numpy as np

    out = dict(_drawn_inputs(seed))
    spreads = {'L0_attn_ln_scale': (1.0, 0.2),
     'L0_attn_ln_bias': (0.0, 0.1),
     'L1_attn_subln_weight': (1.0, 0.6)}
    factors = {'L1_attn_lambda_q1': 200.0,
     'L1_attn_lambda_k1': 8.0,
     'L1_attn_lambda_q2': 60.928,
     'L1_attn_lambda_k2': 55.92,
     'L1_attn_Wq': 4.029,
     'L1_attn_Wk': 4.186}
    for name, (base, spread) in spreads.items():
        noise = np.random.default_rng([zlib.crc32(name.encode()), seed]).standard_normal(out[name].shape)
        drawn = base * np.exp(spread * noise) if base else spread * noise
        out[name] = jnp.asarray(drawn.astype(out[name].dtype))
    for name, factor in factors.items():
        out[name] = (out[name] * factor).astype(out[name].dtype)
    return out
```

```python
from contextlib import ExitStack

import concourse.bass as bass
from concourse import mybir

F32 = mybir.dt.float32
BF16 = mybir.dt.bfloat16
U32 = mybir.dt.uint32
ALU = mybir.AluOpType
ACT = mybir.ActivationFunctionType
AX_X = mybir.AxisListType.X

P = 128
B, N, D = 2, 512, 256
T = B * N // P
TB = N // P
C = D // P
EPS = 1e-5
LE, RANK = 8, 16
FW = D + LE * RANK + LE
LPAD = 14
HD = 16
MU = 4
PROD = [(0, 0), (0, 1), (0, 2), (1, 0), (1, 1), (1, 2), (2, 0), (2, 1)]
LAMBDA_INIT = 0.8 - 0.6 * 2.718281828459045 ** (-0.3 * 12)
SCALE1 = 8.0 ** -0.5
NE, TOPK, CAP, INTER = 32, 6, 256, 176
IH = INTER // 2
EPAD = NE + 2
SI = 2 * INTER
ROW = D + 2
SLOTS = NE * CAP
NB = 4
SKIP = 65536.0


class Chain:

    def __init__(self, eng, sem):
        self.eng, self.sem, self.n = eng, sem, 0

    def link(self, ins):
        ins.then_inc(self.sem, 1)
        self.n += 1
        self.eng.wait_ge(self.sem, self.n)


def macaron_kernel(nc, d, out):
    ctx = ExitStack()
    with ctx:
        def sb(name, shape, dt=F32):
            return ctx.enter_context(nc.sbuf_tensor(name, shape, dt))

        def sem(name):
            return ctx.enter_context(nc.semaphore(name))

        parts = [nc.dram_tensor(f"parts{n}", [3, 2, D, B * N], BF16, kind="Internal").ap() for n in range(2)]
        xbuf = [nc.dram_tensor(f"xbuf{n}", [SLOTS, ROW], F32, kind="Internal").ap() for n in range(2)]
        y_dram = [nc.dram_tensor(f"y{n}", [B * N + 2 * P, D], F32, kind="Internal").ap() for n in range(2)]

        X = sb("X", [P, T, D])
        XN = sb("XN", [P, T, D])
        XT = sb("XT", [P, C, B * N])
        V = sb("V", [P, T, D])
        W13 = sb("W13", [P, NE * C * 2 * INTER])
        WF = sb("WF", [P, C, FW])
        LB = sb("LB", [P, D])
        WA = sb("WA", [P, C, 4 * D])
        SW13 = V[:, :, :].rearrange("p t d -> p (t d)")[:, 0:C * 2 * SI].rearrange("p (c n) -> p c n", c=C)
        SW2 = sb("SW2", [P, 3, D])
        GW = sb("GW", [P, C, NE])
        stack_mem = sb("stack_mem", [P, 8192])
        e_mem = sb("e_mem", [P, 4096])
        VA = sb("VA", [P, 2, TB, MU, 32])
        OS = sb("OS", [P, 2, N])
        ident = sb("ident", [P, P])
        trif = sb("trif", [P, P])
        identb = sb("identb", [P, P], BF16)
        mask = sb("mask", [P, P])
        tri = sb("tri", [P, P], BF16)
        ones = sb("ones", [P, P], BF16)
        slot0 = sb("slot0", [P, NE])
        tok = sb("tok", [P, T])
        empty = sb("empty", [P, 2, ROW])
        rope_c = sb("rope_c", [P, TB, HD])
        rope_s = sb("rope_s", [P, TB, HD])
        lnsb = sb("lnsb", [P, 2, HD])
        subw = sb("subw", [P, HD])
        lamv = sb("lamv", [P, 4, 8])
        lam = sb("lam", [P, 8])
        st = sb("st", [P, T, 6])
        mv = sb("mv", [P, T, 2])
        rv = sb("rv", [P, T])
        rstd = sb("rstd", [P, T])
        m4 = sb("m4", [P, 4])
        el = sb("el", [P, 4, LE])
        ep = sb("ep", [P, 4, LPAD])
        v8 = sb("v8", [P, T, 8])
        rep = sb("rep", [P, 4, 8])
        rpl = sb("rpl", [P, 4, LPAD])
        g4 = sb("g4", [P, 4, LE])
        s4 = sb("s4", [P, 4])
        hs1 = sb("hs1", [P, 2, 32])
        hs2 = sb("hs2", [P, 2, 32])
        hs3 = sb("hs3", [P, 2, 32])
        hs4 = sb("hs4", [P, 2, 32])
        rec = sb("rec", [P, 2, TB, MU])
        amap = sb("amap", [P, TB, MU, HD])
        nm = sb("nm", [P, 2, TB, MU])
        nmr = sb("nmr", [P, TB, MU])
        one = sb("one", [P, 1])
        turn = sb("turn", [P, 1])
        mp = sb("mp", [P, TB, 3, MU], BF16)
        mr = sb("mr", [3 * MU, N], BF16)
        m8 = sb("m8", [P, T])
        rs8 = sb("rs8", [P, T])
        pe_ = sb("pe", [P, T, EPAD])
        rep8 = sb("rep8", [P, T, 8])
        mkb = sb("mkb", [P, T, NE], BF16)
        s8 = sb("s8", [P, T, 8])
        s8z = sb("s8z", [P, T, 8])
        idx = sb("idx", [P, T, 8], U32)
        junk = sb("junk", [P, TOPK, NE])
        meta_w = sb("meta_w", [P, NB, 2])
        meta_i = sb("meta_i", [P, NB, 2], U32)
        PS = ctx.enter_context(nc.psum_tensor("PS", [P, 8, 512], F32))

        KS = [stack_mem[:, 2048 * r:2048 * r + 1024].bitcast(BF16).rearrange("p (m t) -> p m t", m=MU) for r in range(4)]
        QS = [stack_mem[:, 2048 * r + 1024:2048 * r + 2048].bitcast(BF16).rearrange("p (m t) -> p m t", m=MU) for r in range(4)]
        E = [e_mem[:, 2048 * r:2048 * r + 2048].rearrange("p (m t) -> p m t", m=MU) for r in range(2)]
        Y4 = [stack_mem[:, 512 * r:512 * r + 512] for r in range(4)]
        SQ = [stack_mem[:, 2048 + 512 * r:2560 + 512 * r] for r in range(2)]
        R1 = [stack_mem[:, 3072 + 512 * r:3584 + 512 * r] for r in range(2)]
        PT = stack_mem[:, 4096:4096 + 3072].bitcast(BF16).rearrange("p (c x t) -> p c x t", c=3, x=4)
        RT1 = [e_mem[:, 512 * r:512 * r + 512] for r in range(2)]
        RT2 = [e_mem[:, 1024 + 512 * r:1536 + 512 * r] for r in range(2)]
        ZS = e_mem[:, 2048:2048 + 512]
        ZF = e_mem[:, 2560:2560 + 512]
        Z = ZF.rearrange("p (t e r) -> p t e r", t=4, e=LE)
        at = [0]

        def take(mem, n):
            at[0] += n
            return mem[:, at[0] - n:at[0]]

        SRC = [take(stack_mem, TOPK * ROW).rearrange("p (k r) -> p k r", k=TOPK) for _ in range(2)]
        at[0] = 0
        XB = [take(stack_mem, 2 * ROW).rearrange("p (s r) -> p s r", s=2) for _ in range(NB)]
        W2E = [take(stack_mem, 512)[0:IH, :].rearrange("p (i n) -> p i n", i=2) for _ in range(NB)]
        XBT = [take(stack_mem, 512).rearrange("p (c s) -> p c s", c=C) for _ in range(2)]
        OB = [take(stack_mem, 512).rearrange("p (s n) -> p s n", s=2) for _ in range(NB)]
        at[0] = 0
        HSH = [take(e_mem, SI) for _ in range(2)]
        GSH = [take(e_mem, SI) for _ in range(2)]
        GTS = take(e_mem, 3 * P).rearrange("p (k t) -> p k t", k=3)
        GT = [take(e_mem, 512)[0:IH, :].rearrange("p (i s) -> p i s", i=2) for _ in range(2)]
        rpe = take(e_mem, T * EPAD).rearrange("p (t e) -> p t e", t=T)
        mk = take(e_mem, T * NE).rearrange("p (t e) -> p t e", t=T)
        wt = take(e_mem, T * NE).rearrange("p (t e) -> p t e", t=T)
        at[0] = 0
        HE = [[take(e_mem, INTER) for _ in range(2)] for _ in range(2)]
        GE = [[take(e_mem, INTER) for _ in range(2)] for _ in range(2)]
        rms = stack_mem[:, 0:4 * P].rearrange("p (k h) -> p k h", k=4)
        POS = PS[:, 5, 0:T * NE].rearrange("p (t e) -> p t e", t=T)
        MT = PS[0:3 * MU, 7, 0:N // 2].bitcast(BF16)
        LOG = PS[:, 4, 0:T * NE].rearrange("p (t e) -> p t e", t=T)

        names = """x_in ffw_in attn0_in attn1_in shared_in w13_in const_in x_back lam_in
        pool_const init_rows dve_self act_self pool_self final_store
        ln_var ln_rstd xn_ready xt_psum xt_ready
        ff_psum ff_shift ff_exp ff_z ff_zt_psum ff_zt ff_out ff_done
        a0_proj a0_v a0_rope a0_sum a0_mean a0_center a0_square a0_var a0_rstd a0_norm
        sp_psum sp_high sp_rest sp_parts sp_stored
        u0_scores u0_square u0_e u0_av u0_os u0_ot u0_rows u0_va
        att_ready wo_psum res_done
        a1_v_psum a1_v u1_max u1_maxed u1_split u1_mt u1_mr u1_mrow u1_scores u1_exp u1_av u1_os u1_ot u1_rows u1_va lam_sum lam_exp
        rms_in rms_var rms_rstd
        g_logits g_shift g_exp g_mask g_pos g_weight g_copy g_scatter0 g_scatter1
        s_h s_silu s_g s_gt_psum s_gt s_out s_y y_stored
        e_xb0 e_xb1 e_xb2 e_xb3 e_w20 e_w21 e_w22 e_w23 e_meta e_xbt_psum e_xbt e_h e_silu e_g e_gt_psum e_gt e_out e_ob y_added stack_pad pool_turn sw13_in u0_masked u0_rec u1_rec u1_diff sp_mid u1_sp""".split()
        S = {n: sem(n) for n in names}
        stk = [sem(f"stack_in{r}") for r in range(4)]

        block = ctx.enter_context(nc.Block())

        def bc(ap, shape, dim):
            return ap.unsqueeze(dim).broadcast_to(shape)

        LN_TURN = [0, 1, 3, 4, 5, 7]

        @block.sync
        def _(sp):
            sp.dma_start(X[:, :, :], d["x"].rearrange("(t p) d -> p t d", p=P)).then_inc(S["x_in"], 16)
            for dst, src in ((ident, "ident"), (mask, "mask"), (trif, "trif"), (slot0, "slot0"), (tok, "tok")):
                sp.dma_start(dst[:, :], d[src]).then_inc(S["const_in"], 16)
            sp.dma_start(WF[:, :, :], d["wf"]).then_inc(S["ffw_in"], 16)
            sp.dma_start(LB[:, :], d["lb"]).then_inc(S["ffw_in"], 16)
            for dst, src in ((rope_c, "rope_c"), (rope_s, "rope_s"), (empty, "empty")):
                sp.dma_start(dst[:, :, :], d[src]).then_inc(S["const_in"], 16)
            sp.dma_start(WA[:, :, :], d["wa0"]).then_inc(S["attn0_in"], 16)
            for j, name in enumerate(("ln_scale", "ln_bias")):
                sp.dma_start(lnsb[:, j, :], bc(d[name], [P, HD], 0)).then_inc(S["attn0_in"], 16)
            sp.dma_start(SW2[:, :, :], d["sw2"]).then_inc(S["shared_in"], 16)
            sp.dma_start(GW[:, :, :], d["gw"]).then_inc(S["shared_in"], 16)
            for j, name in enumerate(("lq1", "lk1", "lq2", "lk2")):
                sp.dma_start(lamv[:, j, :], bc(d[name], [P, 8], 0)).then_inc(S["lam_in"], 16)
            sp.dma_start(subw[:, :], bc(d["subln"], [P, HD], 0)).then_inc(S["lam_in"], 16)
            sp.wait_ge(S["const_in"], 16 * 8)
            for n in range(2):
                for s in range(2):
                    sp.dma_start(xbuf[n].rearrange("(e s p) r -> p e s r", s=2, p=P)[:, :, s, :],
                                 bc(empty[:, s, :], [P, NE, ROW], 1)).then_inc(S["init_rows"], 16)
                sp.dma_start(y_dram[n][B * N:, :].rearrange("(s p) d -> p s d", p=P), empty[:, :, 0:D])\
                    .then_inc(S["init_rows"], 16)
            q = NE * C * 2 * INTER // 4
            for j in range(4):
                sp.dma_start(W13[:, j * q:(j + 1) * q], d["w13"][:, j * q:(j + 1) * q]).then_inc(S["w13_in"], 16)

            def store_parts(n):
                for b in range(B):
                    sp.wait_ge(S["sp_parts"], 4 * B * n + 4 * (b + 1))
                    for c in range(3):
                        sp.dma_start(parts[n][c, :, :, b * N:(b + 1) * N].rearrange("x (h p) t -> p (x h) t", p=P),
                                     PT[:, c, :, :]).then_inc(S["sp_stored"], 16)
                sp.wait_ge(S["sp_stored"], 16 * 6 * (n + 1))

            def load_stack(n, slot, g, b, width):
                for j, (cq, ck) in enumerate(PROD):
                    for dst, x, c in ((QS, 0, cq), (KS, 1, ck)):
                        src = parts[n][c, x, bass.ds(g * (MU * width), MU * width), b * N:(b + 1) * N]
                        sp.dma_start(dst[slot][width * j:width * (j + 1), :, :],
                                     src.rearrange("(m i) t -> i m t", i=width)).then_inc(stk[slot], 16)

            def experts(n):
                def load(e, k, first=False):
                    if not (first and n == 0):
                        sp.wait_ge(S["e_meta"], n * NE + e - NB + 1)
                        sp.wait_ge(S["e_xbt_psum"], n * NE + e - NB + 1)
                        sp.wait_ge(S["e_out"], n * NE + e - NB + 1)
                    sp.dma_start(XB[k], xbuf[n][bass.ds(e * CAP, CAP), :].rearrange("(s p) r -> p s r", p=P))\
                        .then_inc(S[f"e_xb{k}"], 16)
                    sp.dma_start(W2E[k], d["w2"][bass.ds(e * IH, IH), :].rearrange("p (i n) -> p i n", i=2))\
                        .then_inc(S[f"e_w2{k}"], 16)
                for r in range(2):
                    sp.wait_ge(S[f"g_scatter{r}"], (n + 1) * 4 * TOPK * 16)
                for k in range(NB):
                    load(k, k, True)
                with sp.Fori(1, NE // NB) as h:
                    for k in range(NB):
                        load(NB * h + k, k)

            def store_tiles(n):
                for t in range(T):
                    sp.wait_ge(S["s_y"], n * T + t + 1)
                    sp.dma_start(y_dram[n][t * P:(t + 1) * P, :], X[:, t, :]).then_inc(S["y_stored"], 16)

            store_parts(0)
            load_stack(0, 0, 0, 0, HD)
            load_stack(0, 1, 0, 1, HD)
            with sp.Fori(1, 4) as g:
                for b in range(B):
                    sp.wait_ge(S["u0_scores"], 16 * g + 8 * b - 8)
                    load_stack(0, b, g, b, HD)
            sp.wait_ge(S["wo_psum"], 4)
            sp.dma_start(SW13, d["sw13"]).then_inc(S["sw13_in"], 16)
            sp.dma_start(WA[:, :, :], d["wa1"]).then_inc(S["attn1_in"], 16)
            store_tiles(0)
            experts(0)
            sp.wait_ge(S["y_added"], 16 * 2 * NE)
            sp.dma_start(X[:, :, :], y_dram[0][0:B * N, :].rearrange("(t p) d -> p t d", p=P))\
                .then_inc(S["x_back"], 16)
            store_parts(1)

            def max_rows(u, slot):
                sp.wait_ge(S["u1_mr"], u + 1)
                for c in range(3):
                    sp.dma_start(QS[slot][64 + c:65 + c, :, :], mr[MU * c:MU * c + MU, :]).then_inc(S["u1_mrow"], 16)
            for u in range(4):
                load_stack(1, u, u // 2, u % 2, 8)
            max_rows(0, 0)
            max_rows(1, 1)
            with sp.Fori(0, 3) as i:
                for r in range(4):
                    sp.wait_ge(S["u1_scores"], 32 * i + 8 * r + 8)
                    load_stack(1, r, 2 * i + 2 + r // 2, r % 2, 8)
                    max_rows(4 * i + r + 2, (r + 2) % 4)
            max_rows(14, 2)
            max_rows(15, 3)
            sp.wait_ge(S["wo_psum"], 8)
            sp.dma_start(SW13, d["sw13"]).then_inc(S["sw13_in"], 16)
            store_tiles(1)
            experts(1)
            sp.wait_ge(S["y_added"], 16 * 2 * NE * 2)
            sp.dma_start(out.rearrange("b n d -> (b n) d"), y_dram[1][0:B * N, :]).then_inc(S["final_store"], 16)
            sp.wait_ge(S["final_store"], 16)


        @block.tensor
        def _(pe):
            mm = nc.tensor.matmul

            def transposes(turn, ready, value):
                for tt in range(4):
                    pe.wait_ge(ready, value(tt))
                    for c in range(C):
                        for h in range(2):
                            t = 2 * tt + h
                            o = c * 256 + h * P
                            last = nc.tensor.transpose(PS[:, tt, o:o + P], XN[:, t, c * P:(c + 1) * P], ident[:, :])
                    last.then_inc(S["xt_psum"], 1)

            def ln_transposes(n):
                transposes(LN_TURN[n], S["xn_ready"], lambda tt: T * n + 2 * tt + 2)

            def xt(c, t):
                return XT[:, c, t * P:(t + 1) * P]

            def ffn(n):
                ln_transposes(2 * n)
                for g in range(2):
                    if g:
                        pe.wait_ge(S["ff_done"], 2 * n + 1)
                    for i in range(4):
                        t = 4 * g + i
                        if i % 2 == 0:
                            pe.wait_ge(S["xt_ready"], 4 * LN_TURN[2 * n] + t // 2 + 1)
                        for c in range(C):
                            last = mm(PS[:, 4 + i, 0:FW], xt(c, t), WF[:, c, :], start=(c == 0), stop=(c == C - 1))
                    last.then_inc(S["ff_psum"], 1)
                    pe.wait_ge(S["ff_z"], 2 * n + g + 1)
                    pe.wait_ge(S["xt_ready"], 4 * LN_TURN[2 * n] + 4)
                    for i in range(4):
                        last = nc.tensor.transpose(PS[:, 0, i * P:(i + 1) * P], ZF[:, i * P:(i + 1) * P], ident[:, :])
                    last.then_inc(S["ff_zt_psum"], 1)
                    pe.wait_ge(S["ff_zt"], 2 * n + g + 1)
                    for i in range(4):
                        last = mm(PS[:, 4 + i, 0:D], ZS[:, i * P:(i + 1) * P], LB[:, :],
                                  start=False, stop=True, skip_group_check=True)
                    last.then_inc(S["ff_out"], 1)

            def attention_out(k):
                if k:
                    transposes(6, S["att_ready"], lambda tt: 1)
                else:
                    transposes(2, S["u0_rows"], lambda tt: 8)
                for tt in range(4):
                    pe.wait_ge(S["xt_ready"], 4 * (2 + 4 * k) + tt + 1)
                    for h in range(2):
                        for c in range(C):
                            last = mm(PS[:, 4 + tt, h * D:(h + 1) * D], xt(c, 2 * tt + h), WA[:, c, 3 * D:],
                                      start=(c == 0), stop=(c == C - 1))
                    last.then_inc(S["wo_psum"], 1)

            def attn0():
                ln_transposes(1)
                pe.wait_ge(S["attn0_in"], 48)
                for s in range(T + 3):
                    if s < T:
                        pe.wait_ge(S["xt_ready"], 4 + s // 2 + 1)
                        if s >= 2:
                            pe.wait_ge(S["a0_rope"], s - 1)
                            pe.wait_ge(S["a0_v"], s - 1)
                        for o, lo, hi in ((4, 0, 2 * D), (5, 2 * D, 3 * D)):
                            for c in range(C):
                                last = mm(PS[:, o + 2 * (s % 2), 0:hi - lo], xt(c, s), WA[:, c, lo:hi],
                                          start=(c == 0), stop=(c == C - 1))
                        last.then_inc(S["a0_proj"], 1)
                    t = s - 3
                    if t >= 0:
                        pe.wait_ge(S["a0_norm"], t + 1)
                        pe.wait_ge(S["xt_ready"], 8)
                        if t >= 2:
                            pe.wait_ge(S["sp_rest"], t - 1)
                        for x in range(4):
                            last = nc.tensor.transpose(PS[:, t % 2, x * P:(x + 1) * P], Y4[t % 4][:, x * P:(x + 1) * P],
                                                       ident[:, :])
                        last.then_inc(S["sp_psum"], 1)

                def unit(g, b, first):
                    u = 2 * g + b
                    pe.wait_ge(stk[b], 256 * (g + 1))
                    pe.wait_ge(S["u0_va"], u + 1)
                    if not first:
                        pe.wait_ge(S["u0_os"], u - 1)

                    def av(j):
                        pe.wait_ge(S["u0_e"], 4 * u + j + 1)
                        for m in range(MU):
                            last = mm(PS[32 * m:32 * m + 32, 4 + b, j * P:N], VA[:, b, j, m, :],
                                      E[j % 2][:, m, 0:N - j * P], start=(j == 0), stop=(j == TB - 1),
                                      skip_group_check=True)
                        last.then_inc(S["u0_av"], 1)
                    for j in range(TB):
                        for hp in range(2):
                            if not (first and b == 0 and j == 0):
                                pe.wait_ge(S["u0_square"], 8 * u + 2 * j + hp - 1)
                            elif hp == 0:
                                pe.wait_ge(S["sp_rest"], T)
                                pe.wait_ge(S["sp_high"], T)
                                pe.wait_ge(S["a0_rope"], T)
                                pe.wait_ge(S["a0_v"], T)
                            for k in range(2):
                                m = 2 * hp + k
                                last = mm(PS[:, 2 * hp + k, 0:N - j * P], KS[b][:, m, j * P:(j + 1) * P],
                                          QS[b][:, m, j * P:N], start=True, stop=True)
                            last.then_inc(S["u0_scores"], 1)
                        if j:
                            av(j - 1)
                    av(TB - 1)
                    pe.wait_ge(S["u0_os"], u + 1)
                    if not first:
                        pe.wait_ge(S["u0_rows"], u - 1)
                    for i in range(TB):
                        last = nc.tensor.transpose(PS[:, 6 + b, i * P:(i + 1) * P], OS[:, b, i * P:(i + 1) * P], ident[:, :])
                    last.then_inc(S["u0_ot"], 1)
                unit(0, 0, True)
                unit(0, 1, True)
                with pe.Fori(1, 4) as g:
                    for b in range(B):
                        unit(g, b, False)
                attention_out(0)

            def route(n):
                ln_transposes(3 + 2 * n)
                pe.wait_ge(S["shared_in"], 32)
                pe.wait_ge(S["sw13_in"], 16 * (n + 1))
                pe.wait_ge(S["xt_ready"], 4 * LN_TURN[3 + 2 * n] + 4)
                for t in range(T):
                    for c in range(C):
                        last = mm(LOG[:, t, :], xt(c, t), GW[:, c, :], start=(c == 0), stop=(c == C - 1))
                last.then_inc(S["g_logits"], 1)

            def positions(n):
                pe.wait_ge(S["g_mask"], n + 1)
                for t in range(T):
                    for k in range(t + 1):
                        last = mm(POS[:, t, :], (ones if k < t else tri)[:, :], mkb[:, k, :],
                                  start=(k == 0), stop=(k == t))
                last.then_inc(S["g_pos"], 1)

            def shared(n):
                def first_half(t):
                    q = n * T + t
                    for k in range(2):
                        if t >= 2:
                            pe.wait_ge(S["s_g"], q - 1)
                        for c in range(C):
                            last = mm(PS[:, 2 * k + t % 2, 0:SI], xt(c, t), SW13[:, c, k * SI:(k + 1) * SI],
                                      start=(c == 0), stop=(c == C - 1))
                    last.then_inc(S["s_h"], 1)

                def second_half(t):
                    q = n * T + t
                    pe.wait_ge(S["s_g"], q + 1)
                    if t >= 1:
                        pe.wait_ge(S["s_gt"], q)
                    for k in range(3):
                        w = min(P, SI - k * P)
                        last = nc.tensor.transpose(PS[0:w, 6, k * P:(k + 1) * P], GSH[t % 2][:, k * P:k * P + w], ident[:, :])
                    last.then_inc(S["s_gt_psum"], 1)
                    pe.wait_ge(S["s_gt"], q + 1)
                    if t >= 1:
                        pe.wait_ge(S["s_y"], q)
                    for k in range(3):
                        w = min(P, SI - k * P)
                        last = mm(PS[:, 7, 0:D], GTS[0:w, k, :], SW2[0:w, k, :], start=(k == 0), stop=(k == 2))
                    last.then_inc(S["s_out"], 1)
                first_half(0)
                first_half(1)
                positions(n)
                for t in range(T):
                    second_half(t)
                    if t + 2 < T:
                        first_half(t + 2)

            def experts(n):
                def turn_x(e, k, h, fresh=False):
                    pe.wait_ge(S[f"e_xb{k}"], 16 * (NE // NB) * n + 16 * (h + 1))
                    if not fresh:
                        pe.wait_ge(S["e_xbt"], NE * n + e - 1)
                    for c in range(C):
                        for s in range(2):
                            last = nc.tensor.transpose(PS[:, k % 2, c * 256 + s * P:c * 256 + (s + 1) * P],
                                                       XB[k][:, s, c * P:(c + 1) * P], ident[:, :])
                    last.then_inc(S["e_xbt_psum"], 1)

                def up(e, k, s, fresh):
                    if s == 0:
                        pe.wait_ge(S["e_xbt"], NE * n + e + 1)
                    if not fresh:
                        pe.wait_ge(S["e_g"], 2 * (NE * n + e) + s - 3)
                    for c in range(C):
                        last = mm(PS[:, 2 + 2 * (k % 2) + s, 0:2 * INTER], XBT[k % 2][:, c, s * P:(s + 1) * P],
                                  W13[:, bass.ds(e * (C * 2 * INTER) + c * 2 * INTER, 2 * INTER)],
                                  start=(c == 0), stop=(c == C - 1))
                    last.then_inc(S["e_h"], 1)

                def turn_g(e, k, fresh):
                    pe.wait_ge(S["e_g"], 2 * (NE * n + e) + 2)
                    if not fresh:
                        pe.wait_ge(S["e_gt"], NE * n + e)
                    for i in range(2):
                        for s in range(2):
                            last = nc.tensor.transpose(PS[0:IH, 6, (2 * i + s) * P:(2 * i + s + 1) * P],
                                                       GE[k % 2][s][:, i * IH:(i + 1) * IH], ident[:, :])
                    last.then_inc(S["e_gt_psum"], 1)

                def down(e, k, h, fresh):
                    pe.wait_ge(S["e_gt"], NE * n + e + 1)
                    pe.wait_ge(S[f"e_w2{k}"], 16 * (NE // NB) * n + 16 * (h + 1))
                    if not fresh:
                        pe.wait_ge(S["e_ob"], NE * n + e)
                    for s in range(2):
                        for i in range(2):
                            last = mm(PS[:, 7, s * D:(s + 1) * D], GT[k % 2][:, i, s * P:(s + 1) * P], W2E[k][:, i, :],
                                      start=(i == 0), stop=(i == 1))
                    last.then_inc(S["e_out"], 1)

                def step(e, k, h, first=False, last=False):
                    before, after = k - 1 if k else NB - 1, (k + 1) % NB
                    up(e, k, 0, first and k < 2)
                    if not (first and k == 0):
                        turn_g(e - 1, before, first and k == 1)
                    up(e, k, 1, first and k < 2)
                    if not (last and k == NB - 1):
                        turn_x(e + 1, after, h + (k + 1) // NB, first and k == 0)
                    if not (first and k == 0):
                        down(e - 1, before, h if k else h - 1, first and k == 1)
                pe.wait_ge(S["w13_in"], 64)
                pe.wait_ge(S["s_y"], T * (n + 1))
                turn_x(0, 0, 0, True)
                for k in range(NB):
                    step(k, k, 0, first=True)
                with pe.Fori(1, NE // NB - 1) as h:
                    for k in range(NB):
                        step(NB * h + k, k, h)
                for k in range(NB):
                    step(NE - NB + k, k, NE // NB - 1, last=True)
                turn_g(NE - 1, NB - 1, False)
                down(NE - 1, NB - 1, NE // NB - 1, False)

            def attn1():
                ln_transposes(4)
                pe.wait_ge(S["attn1_in"], 16)
                pe.wait_ge(S["xt_ready"], 4 * 5 + 4)
                for r in range(8):
                    b, x, half = r // 4, r // 2 % 2, r % 2
                    if r >= 2:
                        pe.wait_ge(S["sp_rest"], T + r - 1)
                    for c in range(C):
                        last = mm(PS[:, 4 + r % 2, :], WA[:, c, x * D + half * P:x * D + (half + 1) * P],
                                  XT[:, c, b * N:(b + 1) * N], start=(c == 0), stop=(c == C - 1))
                    last.then_inc(S["sp_psum"], 1)
                for t in range(T):
                    if t >= 2:
                        pe.wait_ge(S["a1_v"], t - 1)
                    for c in range(C):
                        last = mm(PS[:, 6 + t % 2, 0:D], xt(c, t), WA[:, c, 2 * D:3 * D], start=(c == 0), stop=(c == C - 1))
                    last.then_inc(S["a1_v_psum"], 1)


                def row_scores(w, slot, i4, x, fresh=False):
                    i, m = x // MU, x % MU
                    if x == 0:
                        pe.wait_ge(stk[slot], (1024 if slot < 2 else 0) + 256 * (i4 + 1))
                    if not fresh:
                        pe.wait_ge(S["u1_maxed"], 16 * w + x - 1)
                    mm(PS[:, 4 + x % 2, :], QS[slot][0:64, m, i * P:(i + 1) * P], KS[slot][0:64, m, :],
                       start=True, stop=True).then_inc(S["u1_max"], 1)

                def turn_maxima(w, first=False):
                    pe.wait_ge(S["u1_split"], w + 1)
                    if not first:
                        pe.wait_ge(S["u1_rows"], w - 1)
                    for i in range(TB):
                        last = nc.tensor.transpose(MT[:, i * P:(i + 1) * P], mp[:, i, :, :].rearrange("p c m -> p (c m)"),
                                                   identb[:, :])
                    last.then_inc(S["u1_mt"], 1)

                def av(u, b, j):
                    pe.wait_ge(S["u1_exp"], 8 * u + 2 * j + 2)
                    for m in range(MU):
                        last = mm(PS[32 * m:32 * m + 32, 6, :], VA[:, b, j, m // 2, :], E[j % 2][:, m, :],
                                  start=(j == 0), stop=(j == TB - 1), skip_group_check=True)
                    last.then_inc(S["u1_av"], 1)

                def turn_rows(u, b):
                    pe.wait_ge(S["u1_os"], u + 1)
                    for i in range(TB):
                        last = nc.tensor.transpose(PS[:, 7, i * P:(i + 1) * P], OS[:, b, i * P:(i + 1) * P], ident[:, :])
                    last.then_inc(S["u1_ot"], 1)

                def unit(i4, u4, first=False, last=False):
                    u = 4 * i4 + u4
                    pe.wait_ge(S["u1_mrow"], 48 * u + 48)
                    pe.wait_ge(S["u1_va"], u + 1)
                    for j in range(TB):
                        if j == 2 and not (first and u4 == 0):
                            pe.wait_ge(S["u1_mr"], u + 1)
                            turn_rows(u - 1, (u4 + 1) % 2)
                        if j == 3 and not (last and u4 == 3):
                            turn_maxima(u + 1, first and u4 == 0)
                        for hp in range(2):
                            if not (first and u4 == 0 and j == 0):
                                pe.wait_ge(S["u1_exp"], 8 * u + 2 * j + hp - 1)
                            for k in range(2):
                                m = 2 * hp + k
                                mm_ = mm(PS[:, 2 * hp + k, :], KS[u4][0:67, m, j * P:(j + 1) * P], QS[u4][0:67, m, :],
                                         start=True, stop=True)
                            mm_.then_inc(S["u1_scores"], 1)
                            ahead = 1 if j < 2 else 2
                            if not (last and u4 + ahead > 3):
                                for k in range(2):
                                    row_scores(u + ahead, (u4 + ahead) % 4, i4 + (u4 + ahead) // 4,
                                               (4 * j + 2 * hp + k + 8) % 16)
                        if j:
                            if j == 1 and not (first and u4 == 0):
                                pe.wait_ge(S["u1_os"], u)
                            av(u, u4 % 2, j - 1)
                        elif not (first and u4 == 0):
                            av(u - 1, (u4 + 1) % 2, 3)
                pe.wait_ge(S["sp_rest"], T + 8)
                pe.wait_ge(S["a1_v"], T)
                pe.wait_ge(S["stack_pad"], 1)
                for x in range(16):
                    row_scores(0, 0, 0, x, x < 2)
                turn_maxima(0, True)
                for x in range(8):
                    row_scores(1, 1, 0, x)
                for u4 in range(4):
                    unit(0, u4, first=True)
                with pe.Fori(1, 3) as i4:
                    for u4 in range(4):
                        unit(i4, u4)
                for u4 in range(4):
                    unit(3, u4, last=True)
                av(15, 1, 3)
                pe.wait_ge(S["u1_rows"], 15)
                turn_rows(15, 1)
                attention_out(1)

            pe.wait_ge(S["const_in"], 16 * 8)
            pe.wait_ge(S["pool_const"], 4)
            pe.wait_ge(S["ffw_in"], 32)
            ffn(0)
            attn0()
            ffn(1)
            route(0)
            shared(0)
            experts(0)
            attn1()
            route(1)
            shared(1)
            experts(1)

        @block.vector
        def _(dve):
            ch = Chain(dve, S["dve_self"])
            v = nc.vector

            def layer_norm(n):
                for t in range(T):
                    last = v.bn_stats(st[:, t, :], X[:, t, :])
                ch.link(last)
                for t in range(T):
                    last = v.bn_aggr(mv[:, t, :], st[:, t, :])
                ch.link(last)
                ch.link(v.tensor_scalar(rv[:, :], mv[:, :, 1], EPS, None, ALU.add))
                v.reciprocal(rv[:, :], rv[:, :]).then_inc(S["ln_var"], 1)
                dve.wait_ge(S["ln_rstd"], n + 1)
                for t in range(T):
                    v.tensor_scalar(XN[:, t, :], X[:, t, :], mv[:, t, 0:1], rstd[:, t:t + 1],
                                    ALU.subtract, ALU.mult).then_inc(S["xn_ready"], 1)

            def ffn(n):
                layer_norm(2 * n)
                for g in range(2):
                    q = 2 * n + g
                    logits = PS[:, 4:8, D + LE * RANK:FW]
                    dve.wait_ge(S["ff_psum"], q + 1)
                    ch.link(v.tensor_reduce(m4[:, :], logits, AX_X, ALU.max))
                    v.tensor_tensor(el[:, :, :], logits, bc(m4[:, :], [P, 4, LE], 2), ALU.subtract)\
                        .then_inc(S["ff_shift"], 1)
                    dve.wait_ge(S["ff_exp"], q + 1)
                    for i in range(4):
                        last = v.max(out=v8[:, i, :], in_=ep[:, i, 0:LE])
                    ch.link(last)
                    ch.link(v.tensor_copy(rep[:, :, 0:2], v8[:, 0:4, 0:2]))
                    for i in range(4):
                        last = v.match_replace(rpl[:, i, :], rep[:, i, :], ep[:, i, :], 2.0)
                    ch.link(last)
                    ch.link(v.scalar_tensor_tensor(g4[:, :, :], rpl[:, :, 0:LE], 1.5, ep[:, :, 0:LE], ALU.is_gt, ALU.mult))
                    ch.link(v.tensor_reduce(s4[:, :], g4[:, :, :], AX_X, ALU.add))
                    ch.link(v.reciprocal(s4[:, :], s4[:, :]))
                    ch.link(v.scalar_tensor_tensor(g4[:, :, :], g4[:, :, :], 32.0 / RANK, bc(s4[:, :], [P, 4, LE], 2),
                                                   ALU.mult, ALU.mult))
                    v.tensor_tensor(Z, PS[:, 4:8, D:D + LE * RANK].rearrange("p t (e r) -> p t e r", e=LE),
                                    bc(g4[:, :, :], [P, 4, LE, RANK], 3), ALU.mult).then_inc(S["ff_z"], 1)
                    dve.wait_ge(S["ff_out"], q + 1)
                    x4 = X[:, 4 * g:4 * g + 4, :]
                    ins = v.scalar_tensor_tensor(x4, PS[:, 4:8, 0:D], 0.5, x4, ALU.mult, ALU.add)
                    ins.then_inc(S["ff_done"], 1)
                    dve.wait_ge(S["ff_done"], q + 1)

            def attention_out(k):
                for tt in range(4):
                    dve.wait_ge(S["wo_psum"], 4 * k + tt + 1)
                    x2 = X[:, 2 * tt:2 * tt + 2, :]
                    last = v.tensor_tensor(x2, PS[:, 4 + tt, :].rearrange("p (t d) -> p t d", t=2), x2, ALU.add)
                last.then_inc(S["res_done"], 1)
                dve.wait_ge(S["res_done"], k + 1)

            def attn0():
                layer_norm(1)
                dve.wait_ge(S["const_in"], 16 * 8)
                for s in range(T + 3):
                    if s < T:
                        r, i = s % 2, s % TB
                        dve.wait_ge(S["a0_proj"], s + 1)
                        if s >= 2:
                            dve.wait_ge(S["a0_sum"], s - 1)
                        qk = PS[:, 4 + 2 * r, :].rearrange("p (h x e) -> p h x e", x=2, e=HD // 2)
                        t2 = RT2[r].rearrange("p (h x e) -> p h x e", x=2, e=HD // 2)
                        v.tensor_tensor(RT1[r].rearrange("p (h e) -> p h e", e=HD),
                                        PS[:, 4 + 2 * r, :].rearrange("p (h e) -> p h e", e=HD),
                                        bc(rope_c[:, i, :], [P, 32, HD], 1), ALU.mult)
                        for x in range(2):
                            last = v.tensor_tensor(t2[:, :, x, :], qk[:, :, 1 - x, :],
                                                   bc(rope_s[:, i, x * 8:x * 8 + 8], [P, 32, 8], 1), ALU.mult)
                        last.then_inc(S["a0_rope"], 1)
                    t = s - 1
                    if 0 <= t < T:
                        r = t % 2
                        dve.wait_ge(S["a0_sum"], t + 1)
                        if t >= 2:
                            dve.wait_ge(S["a0_center"], t - 1)
                        ch.link(v.tensor_reduce(hs1[:, r, :], Y4[t % 4].rearrange("p (h e) -> p h e", e=HD), AX_X, ALU.add))
                        v.tensor_scalar(hs2[:, r, :], hs1[:, r, :], 1.0 / HD, None, ALU.mult).then_inc(S["a0_mean"], 1)
                    t = s - 2
                    if 0 <= t < T:
                        r = t % 2
                        dve.wait_ge(S["a0_square"], t + 1)
                        ch.link(v.tensor_reduce(hs3[:, r, :], SQ[r].rearrange("p (h e) -> p h e", e=HD), AX_X, ALU.add))
                        ch.link(v.tensor_scalar(hs3[:, r, :], hs3[:, r, :], 1.0 / HD, EPS, ALU.mult, ALU.add))
                        v.reciprocal(hs3[:, r, :], hs3[:, r, :]).then_inc(S["a0_var"], 1)
                    t = s - 3
                    if 0 <= t < T:
                        split(t, t % 2, t % 2, PT[:, 0, :, (t % TB) * P:(t % TB + 1) * P],
                              PS[:, t % 2, :].rearrange("p (x t) -> p x t", x=4), 4)

                def unit(g, b, first):
                    u = 2 * g + b
                    for j in range(TB):
                        dve.wait_ge(S["u0_square"], 8 * u + 2 * j + 2)
                        diag = E[j % 2][:, :, 0:P]
                        v.tensor_tensor(diag, diag, bc(mask[:, :], [P, MU, P], 1), ALU.mult).then_inc(S["u0_masked"], 1)
                        dve.wait_ge(S["u0_masked"], 4 * u + j + 1)
                        e = E[j % 2][:, :, 0:N - j * P]
                        v.tensor_tensor(e, e, e, ALU.mult).then_inc(S["u0_e"], 1)
                    dve.wait_ge(S["u0_ot"], u + 1)
                    ot = PS[:, 6 + b, :].rearrange("p (i m e) -> p i m e", i=TB, m=MU)
                    v.reciprocal(rec[:, b, :, :], ot[:, :, :, HD]).then_inc(S["u0_rec"], 1)
                    dve.wait_ge(S["u0_rec"], u + 1)
                    v.tensor_tensor(XN[:, TB * b:TB * b + TB, bass.ds(g * (MU * HD), MU * HD)]
                                    .rearrange("p i (m e) -> p i m e", m=MU), ot[:, :, :, 0:HD],
                                    bc(rec[:, b, :, :], [P, TB, MU, HD], 3), ALU.mult).then_inc(S["u0_rows"], 1)
                unit(0, 0, True)
                unit(0, 1, True)
                with dve.Fori(1, 4) as g:
                    for b in range(B):
                        unit(g, b, False)
                attention_out(0)

            def split(q, r, bank, high, psum, n):
                dve.wait_ge(S["sp_high"], q + 1)
                if q >= 2:
                    dve.wait_ge(S["sp_parts"], q - 1)
                out_ = R1[r].rearrange("p (x t) -> p x t", x=n)
                v.tensor_tensor(out_, psum, high, ALU.subtract).then_inc(S["sp_rest"], 1)

            def route(n):
                layer_norm(3 + 2 * n)
                probs = pe_[:, :, 0:NE]
                dve.wait_ge(S["g_logits"], n + 1)
                ch.link(v.tensor_reduce(m8[:, :], LOG, AX_X, ALU.max))
                v.tensor_tensor(probs, LOG, bc(m8[:, :], [P, T, NE], 2), ALU.subtract).then_inc(S["g_shift"], 1)
                dve.wait_ge(S["g_exp"], n + 1)
                for t in range(T):
                    v.max(out=v8[:, t, :], in_=pe_[:, t, 0:NE])
                ch.link(v.tensor_reduce(rs8[:, :], probs, AX_X, ALU.add))
                v.reciprocal(rs8[:, :], rs8[:, :])
                ch.link(v.tensor_copy(rep8[:, :, 0:TOPK], v8[:, :, 0:TOPK]))
                for t in range(T):
                    last = v.match_replace(rpe[:, t, :], rep8[:, t, :], pe_[:, t, :], 2.0)
                ch.link(last)
                v.tensor_scalar(mkb[:, :, :], rpe[:, :, 0:NE], 1.5, None, ALU.is_gt).then_inc(S["g_mask"], 1)
                v.tensor_scalar(mk[:, :, :], rpe[:, :, 0:NE], 1.5, None, ALU.is_gt)
                ch.link(v.tensor_tensor(wt[:, :, :], probs, bc(rs8[:, :], [P, T, NE], 2), ALU.mult))

            def place(n):
                dve.wait_ge(S["g_pos"], n + 1)
                ch.link(v.scalar_tensor_tensor(mk[:, :, :], POS, float(CAP), mk[:, :, :], ALU.is_lt, ALU.mult))
                v.tensor_tensor(rpe[:, :, 0:NE], POS, bc(slot0[:, :], [P, T, NE], 1), ALU.add)
                ch.link(v.tensor_tensor(wt[:, :, :], wt[:, :, :], mk[:, :, :], ALU.mult))
                ch.link(v.tensor_tensor(mk[:, :, :], rpe[:, :, 0:NE], mk[:, :, :], ALU.mult))
                for t in range(T):
                    last = v.max(out=s8[:, t, :], in_=mk[:, t, :])
                ch.link(last)
                ch.link(v.tensor_scalar(s8z[:, :, :], s8[:, :, :], 0.0, SKIP, ALU.is_equal, ALU.mult))
                if n:
                    dve.wait_ge(S["g_scatter0"], 4 * TOPK * 16)
                    dve.wait_ge(S["g_scatter1"], 4 * TOPK * 16)
                ch.link(v.scalar_tensor_tensor(idx[:, :, :], s8[:, :, :], -1.0, s8z[:, :, :], ALU.add, ALU.add))

            def weights(n, t):
                src = SRC[t % 2]
                if t >= 2:
                    dve.wait_ge(S[f"g_scatter{t % 2}"], (n * 4 + t // 2) * TOPK * 16)
                v.tensor_copy(src[:, :, D + 1:D + 2], bc(tok[:, t:t + 1], [P, TOPK, 1], 1))
                for k in range(TOPK):
                    last = v.scalar_tensor_tensor(junk[:, k, :], mk[:, t, :], s8[:, t, k:k + 1], wt[:, t, :],
                                                  ALU.is_equal, ALU.mult, accum_out=src[:, k, D:D + 1])
                last.then_inc(S["g_weight"], 1)
                dve.wait_ge(S["g_weight"], n * T + t + 1)

            def shared(n):
                def gate(t):
                    q = n * T + t
                    dve.wait_ge(S["s_silu"], q + 1)
                    if t >= 2:
                        dve.wait_ge(S["s_gt_psum"], q - 1)
                    v.tensor_tensor(GSH[t % 2], HSH[t % 2], PS[:, 2 + t % 2, 0:SI], ALU.mult).then_inc(S["s_g"], 1)

                def add(t):
                    dve.wait_ge(S["s_out"], n * T + t + 1)
                    v.scalar_tensor_tensor(X[:, t, :], PS[:, 7, 0:D], 0.5, X[:, t, :], ALU.mult, ALU.add)\
                        .then_inc(S["s_y"], 1)
                gate(0)
                place(n)
                weights(n, 0)
                gate(1)
                weights(n, 1)
                for t in range(T):
                    add(t)
                    if t + 2 < T:
                        gate(t + 2)
                        weights(n, t + 2)

            def experts(n):
                def turned(e, k, fresh=False):
                    dve.wait_ge(S["e_xbt_psum"], NE * n + e + 1)
                    if not fresh:
                        dve.wait_ge(S["e_h"], 2 * (NE * n + e) - 2)
                    v.tensor_copy(XBT[k % 2], PS[:, k % 2, :].rearrange("p (c s) -> p c s", c=C)).then_inc(S["e_xbt"], 1)

                def step(e, k, h, first=False, last=False):
                    dve.wait_ge(S[f"e_xb{k}"], 16 * (NE // NB) * n + 16 * (h + 1))
                    if not first:
                        dve.wait_ge(S["y_added"], 32 * (NE * n + e) - 32 * (NB - 1))
                        dve.wait_ge(S["e_ob"], NE * n + e - NB + 1)
                    v.tensor_scalar(meta_w[:, k, :], XB[k][:, :, D], 0.5, None, ALU.mult)
                    v.tensor_copy(meta_i[:, k, :], XB[k][:, :, D + 1]).then_inc(S["e_meta"], 1)
                    for s in range(2):
                        dve.wait_ge(S["e_silu"], 2 * (NE * n + e) + s + 1)
                        if not (first and k < 2):
                            dve.wait_ge(S["e_gt_psum"], NE * n + e - 1)
                        v.tensor_tensor(GE[k % 2][s], HE[k % 2][s], PS[:, 2 + 2 * (k % 2) + s, INTER:2 * INTER], ALU.mult)\
                            .then_inc(S["e_g"], 1)
                    if not (last and k == NB - 1):
                        turned(e + 1, k + 1, first and k == 0)
                turned(0, 0, True)
                for k in range(NB):
                    step(k, k, 0, first=True)
                with dve.Fori(1, NE // NB - 1) as h:
                    for k in range(NB):
                        step(NB * h + k, k, h)
                for k in range(NB):
                    step(NE - NB + k, k, NE // NB - 1, last=True)

            def attn1():
                dve.wait_ge(S["x_back"], 16)
                layer_norm(4)
                dve.wait_ge(S["lam_in"], 80)
                l4 = lamv[:, :, :].rearrange("p (a b) e -> p a b e", b=2)
                ch.link(v.tensor_tensor(lam[:, :], lamv[:, 0, :], lamv[:, 1, :], ALU.mult))
                ch.link(v.tensor_reduce(m4[:, 0:1], lam[:, :], AX_X, ALU.add))
                ch.link(v.tensor_tensor(lam[:, :], lamv[:, 2, :], lamv[:, 3, :], ALU.mult))
                v.tensor_reduce(m4[:, 1:2], lam[:, :], AX_X, ALU.add).then_inc(S["lam_sum"], 1)
                dve.wait_ge(S["lam_exp"], 1)
                ch.link(v.scalar_tensor_tensor(lam[:, 0:1], lam[:, 2:3], -LAMBDA_INIT, lam[:, 1:2], ALU.add, ALU.subtract))
                ch.link(v.tensor_scalar(subw[:, :], subw[:, :], 1.0 - LAMBDA_INIT, None, ALU.mult))
                for r in range(8):
                    x = r % 4
                    split(T + r, r % 2, 4 + r % 2, PT[:, 0, x:x + 1, :], PS[:, 4 + r % 2:5 + r % 2, :], 1)

                def maximum(w, par, x, fresh=False):
                    if x == 0 and not fresh:
                        dve.wait_ge(S["u1_split"], w - 1)
                    dve.wait_ge(S["u1_max"], 16 * w + x + 1)
                    v.tensor_reduce(nm[:, par, x // MU, x % MU:x % MU + 1], PS[:, 4 + x % 2, :], AX_X, ALU.max, negate=True)\
                        .then_inc(S["u1_maxed"], 1)

                def rows(u, b, g):
                    dve.wait_ge(S["u1_ot"], u + 1)
                    ot = PS[:, 7, :].rearrange("p (i m e) -> p i m e", i=TB, m=MU)
                    v.reciprocal(rec[:, b, :, :], ot[:, :, :, HD]).then_inc(S["u1_rec"], 1)
                    dve.wait_ge(S["u1_rec"], u + 1)
                    v.tensor_tensor(amap[:, :, :, :], ot[:, :, :, 0:HD], bc(rec[:, b, :, :], [P, TB, MU, HD], 3), ALU.mult)\
                        .then_inc(S["u1_rows"], 1)
                    dve.wait_ge(S["u1_rows"], u + 1)
                    two = amap[:, :, :, :].rearrange("p i (h x) e -> p i h x e", x=2)
                    v.scalar_tensor_tensor(XN[:, TB * b:TB * b + TB, bass.ds(g * 32, 32)]
                                           .rearrange("p i (h e) -> p i h e", h=2),
                                           two[:, :, :, 1, :], lam[:, 0:1], two[:, :, :, 0, :], ALU.mult, ALU.add)\
                        .then_inc(S["u1_diff"], 1)

                def unit(i4, u4, first=False, last=False):
                    u = 4 * i4 + u4
                    for j in range(TB):
                        ahead = 1 if j < 2 else 2
                        if not (last and u4 + ahead > 3):
                            for k in range(4):
                                maximum(u + ahead, (u4 + ahead) % 2, (4 * j + k + 8) % 16, False)
                        if j == 2 and not (first and u4 == 0):
                            rows(u - 1, (u4 + 1) % 2, 2 * i4 + (u4 - 1) // 2)
                for x in range(16):
                    maximum(0, 0, x, True)
                for x in range(8):
                    maximum(1, 1, x, True)
                for u4 in range(4):
                    unit(0, u4, first=True)
                with dve.Fori(1, 3) as i4:
                    for u4 in range(4):
                        unit(i4, u4)
                for u4 in range(4):
                    unit(3, u4, last=True)
                rows(15, 1, 7)
                dve.wait_ge(S["u1_diff"], 16)
                flat = XN[:, :, :].rearrange("p t d -> p (t d)")
                a, b_ = e_mem[:, 0:2048], e_mem[:, 2048:4096]
                v.tensor_scalar(a, flat, 4e18, -4e18, ALU.min, ALU.max)
                ch.link(v.tensor_scalar(b_, flat, 2.0 ** -40, 1e18, ALU.mult, ALU.min))
                ch.link(v.tensor_scalar(b_, b_, -1e18, None, ALU.max))
                v.tensor_tensor(a, a, a, ALU.mult)
                ch.link(v.tensor_tensor(b_, b_, b_, ALU.mult))
                v.tensor_reduce(rms[:, 0, :], a.rearrange("p (h e) -> p h e", e=HD), AX_X, ALU.add)
                ch.link(v.tensor_reduce(rms[:, 1, :], b_.rearrange("p (h e) -> p h e", e=HD), AX_X, ALU.add))
                v.tensor_scalar(rms[:, 2, :], rms[:, 1, :], 3.4028235e38 * 2.0 ** -80, None, ALU.is_le)
                v.tensor_scalar(rms[:, 0, :], rms[:, 0, :], 1.0 / HD, EPS, ALU.mult, ALU.add)
                ch.link(v.tensor_scalar(rms[:, 1, :], rms[:, 1, :], 1.0 / HD, 1e-30, ALU.mult, ALU.add))
                v.reciprocal(rms[:, 0:2, :], rms[:, 0:2, :]).then_inc(S["rms_var"], 1)
                dve.wait_ge(S["rms_rstd"], 1)
                ch.link(v.scalar_tensor_tensor(rms[:, 3, :], rms[:, 1, :], 2.0 ** -40, rms[:, 0, :], ALU.mult, ALU.min))
                ch.link(v.tensor_tensor(rms[:, 3, :], rms[:, 3, :], rms[:, 2, :], ALU.mult))
                x3 = flat.rearrange("p (h e) -> p h e", e=HD)
                ch.link(v.tensor_tensor(x3, x3, bc(rms[:, 3, :], [P, P, HD], 2), ALU.mult))
                v.tensor_tensor(x3, x3, bc(subw[:, :], [P, P, HD], 1), ALU.mult).then_inc(S["att_ready"], 1)
                attention_out(1)

            dve.wait_ge(S["x_in"], 16)
            dve.wait_ge(S["pool_const"], 4)
            ffn(0)
            attn0()
            ffn(1)
            route(0)
            shared(0)
            experts(0)
            attn1()
            route(1)
            shared(1)
            experts(1)

        @block.scalar
        def _(act):
            act_fn = nc.scalar.activation

            def evacuate_xt(turn):
                for tt in range(4):
                    act.wait_ge(S["xt_psum"], 4 * turn + tt + 1)
                    act_fn(XT[:, :, tt * 256:(tt + 1) * 256], PS[:, tt, :].rearrange("p (c t) -> p c t", c=C), ACT.Copy)\
                        .then_inc(S["xt_ready"], 1)

            def layer_norm(n):
                act.wait_ge(S["ln_var"], n + 1)
                act_fn(rstd[:, :], rv[:, :], ACT.Sqrt).then_inc(S["ln_rstd"], 1)
                evacuate_xt(LN_TURN[n])

            def ffn(n):
                layer_norm(2 * n)
                for g in range(2):
                    q = 2 * n + g
                    act.wait_ge(S["ff_shift"], q + 1)
                    act_fn(ep[:, :, 0:LE], el[:, :, :], ACT.Exp).then_inc(S["ff_exp"], 1)
                    act.wait_ge(S["ff_zt_psum"], q + 1)
                    act_fn(ZS, PS[:, 0, :], ACT.Copy).then_inc(S["ff_zt"], 1)

            def split_high(q, dst, psum):
                act.wait_ge(S["sp_psum"], q + 1)
                if q % 4 == 0 and q:
                    act.wait_ge(S["sp_stored"], 16 * 3 * (q // 4))
                act_fn(dst, psum, ACT.Copy).then_inc(S["sp_high"], 1)

            def attn0():
                layer_norm(1)
                for s in range(T + 3):
                    if s < T:
                        act.wait_ge(S["a0_proj"], s + 1)
                        act_fn(V[:, s, :], PS[:, 5 + 2 * (s % 2), 0:D], ACT.Copy).then_inc(S["a0_v"], 1)
                    t = s - 1
                    if 0 <= t < T:
                        act.wait_ge(S["a0_center"], t + 1)
                        if t >= 2:
                            act.wait_ge(S["a0_var"], t - 1)
                        act_fn(SQ[t % 2], Y4[t % 4], ACT.Square).then_inc(S["a0_square"], 1)
                    t = s - 2
                    if 0 <= t < T:
                        act.wait_ge(S["a0_var"], t + 1)
                        if t >= 2:
                            act.wait_ge(S["a0_norm"], t - 1)
                        act_fn(hs4[:, t % 2, :], hs3[:, t % 2, :], ACT.Sqrt).then_inc(S["a0_rstd"], 1)
                    t = s - 3
                    if 0 <= t < T:
                        split_high(t, PT[:, 0, :, (t % TB) * P:(t % TB + 1) * P],
                                   PS[:, t % 2, :].rearrange("p (x t) -> p x t", x=4))

                def unit(g, b, first):
                    u = 2 * g + b
                    for j in range(TB):
                        for hp in range(2):
                            act.wait_ge(S["u0_scores"], 8 * u + 2 * j + hp + 1)
                            if not (first and b == 0 and j < 2):
                                act.wait_ge(S["u0_av"], 4 * u + j - 1)
                            act_fn(E[j % 2][:, 2 * hp:2 * hp + 2, 0:N - j * P], PS[:, 2 * hp:2 * hp + 2, 0:N - j * P],
                                   ACT.Square).then_inc(S["u0_square"], 1)
                    act.wait_ge(S["u0_av"], 4 * u + 4)
                    if not first:
                        act.wait_ge(S["u0_ot"], u - 1)
                    act_fn(OS[:, b, :], PS[:, 4 + b, :], ACT.Copy).then_inc(S["u0_os"], 1)
                unit(0, 0, True)
                unit(0, 1, True)
                with act.Fori(1, 4) as g:
                    for b in range(B):
                        unit(g, b, False)
                evacuate_xt(2)

            def route(n):
                layer_norm(3 + 2 * n)
                act.wait_ge(S["g_shift"], n + 1)
                act_fn(pe_[:, :, 0:NE], pe_[:, :, 0:NE], ACT.Exp).then_inc(S["g_exp"], 1)

            def shared(n):
                def copy_rows(t):
                    if t >= 2:
                        act.wait_ge(S[f"g_scatter{t % 2}"], (n * 4 + t // 2) * TOPK * 16)
                    act_fn(SRC[t % 2][:, :, 0:D], bc(XN[:, t, :], [P, TOPK, D], 1), ACT.Copy).then_inc(S["g_copy"], 1)

                def silu(t):
                    q = n * T + t
                    act.wait_ge(S["s_h"], q + 1)
                    if t >= 2:
                        act.wait_ge(S["s_g"], q - 1)
                    act_fn(HSH[t % 2], PS[:, t % 2, 0:SI], ACT.Silu).then_inc(S["s_silu"], 1)
                silu(0)
                silu(1)
                copy_rows(0)
                copy_rows(1)
                for t in range(T):
                    q = n * T + t
                    act.wait_ge(S["s_gt_psum"], q + 1)
                    if t:
                        act.wait_ge(S["s_out"], q)
                    act_fn(GTS[:, 0:2, :], PS[:, 6, 0:2 * P].rearrange("p (k t) -> p k t", k=2), ACT.Copy)
                    act_fn(GTS[0:SI - 2 * P, 2, :], PS[0:SI - 2 * P, 6, 2 * P:3 * P], ACT.Copy).then_inc(S["s_gt"], 1)
                    if t + 2 < T:
                        silu(t + 2)
                        copy_rows(t + 2)

            def experts(n):
                def turned_g(e, k, fresh):
                    act.wait_ge(S["e_gt_psum"], NE * n + e + 1)
                    if not fresh:
                        act.wait_ge(S["e_out"], NE * n + e - 1)
                    act_fn(GT[k % 2], PS[0:IH, 6, :].rearrange("p (i s) -> p i s", i=2), ACT.Copy).then_inc(S["e_gt"], 1)

                def weigh(e, k, fresh):
                    act.wait_ge(S["e_out"], NE * n + e + 1)
                    act.wait_ge(S["e_meta"], NE * n + e + 1)
                    if not fresh:
                        act.wait_ge(S["y_added"], 32 * (NE * n + e) - 32 * (NB - 1))
                    for s in range(2):
                        last = act_fn(OB[k][:, s, :], PS[:, 7, s * D:(s + 1) * D], ACT.Copy, scale=meta_w[:, k, s:s + 1])
                    last.then_inc(S["e_ob"], 1)

                def step(e, k, first=False):
                    before = k - 1 if k else NB - 1
                    for s in range(2):
                        act.wait_ge(S["e_h"], 2 * (NE * n + e) + s + 1)
                        if not (first and k < 2):
                            act.wait_ge(S["e_g"], 2 * (NE * n + e) + s - 3)
                        act_fn(HE[k % 2][s], PS[:, 2 + 2 * (k % 2) + s, 0:INTER], ACT.Silu).then_inc(S["e_silu"], 1)
                        if not (first and k == 0):
                            if s == 0:
                                turned_g(e - 1, before, first and k < 3)
                            else:
                                weigh(e - 1, before, first)
                for k in range(NB):
                    step(k, k, True)
                with act.Fori(1, NE // NB) as h:
                    for k in range(NB):
                        step(NB * h + k, k)
                turned_g(NE - 1, NB - 1, False)
                weigh(NE - 1, NB - 1, False)

            def attn1():
                layer_norm(4)
                act.wait_ge(S["lam_sum"], 1)
                act_fn(lam[:, 1:3], m4[:, 0:2], ACT.Exp).then_inc(S["lam_exp"], 1)
                for r in range(8):
                    x = r % 4
                    split_high(T + r, PT[:, 0, x:x + 1, :], PS[:, 4 + r % 2:5 + r % 2, :])
                for t in range(T):
                    act.wait_ge(S["a1_v_psum"], t + 1)
                    act_fn(V[:, t, :], PS[:, 6 + t % 2, 0:D], ACT.Copy).then_inc(S["a1_v"], 1)

                def max_rows(w, first=False):
                    act.wait_ge(S["u1_mt"], w + 1)
                    if not first:
                        act.wait_ge(S["u1_mrow"], 48 * w)
                    act_fn(mr[:, :], MT, ACT.Copy).then_inc(S["u1_mr"], 1)

                def output(u, b, fresh=False):
                    act.wait_ge(S["u1_av"], 4 * u + 4)
                    if not fresh:
                        act.wait_ge(S["u1_ot"], u - 1)
                    act_fn(OS[:, b, :], PS[:, 6, :], ACT.Copy).then_inc(S["u1_os"], 1)

                def unit(i4, u4, first=False, last=False):
                    u = 4 * i4 + u4
                    for j in range(TB):
                        for hp in range(2):
                            act.wait_ge(S["u1_scores"], 8 * u + 2 * j + hp + 1)
                            if not (first and u4 == 0 and j < 2):
                                act.wait_ge(S["u1_av"], 4 * u + j - 1)
                            act_fn(E[j % 2][:, 2 * hp:2 * hp + 2, :], PS[:, 2 * hp:2 * hp + 2, :], ACT.Exp, scale=SCALE1)\
                                .then_inc(S["u1_exp"], 1)
                            if j == 3 and hp == 0 and not (last and u4 == 3):
                                max_rows(u + 1)
                        if j == 0 and not (first and u4 == 0):
                            output(u - 1, (u4 + 1) % 2, first and u4 <= 2)
                max_rows(0, True)
                for u4 in range(4):
                    unit(0, u4, first=True)
                with act.Fori(1, 3) as i4:
                    for u4 in range(4):
                        unit(i4, u4)
                for u4 in range(4):
                    unit(3, u4, last=True)
                output(15, 1)
                act.wait_ge(S["rms_var"], 1)
                act_fn(rms[:, 0:2, :], rms[:, 0:2, :], ACT.Sqrt).then_inc(S["rms_rstd"], 1)
                evacuate_xt(6)

            ffn(0)
            attn0()
            ffn(1)
            route(0)
            shared(0)
            experts(0)
            attn1()
            route(1)
            shared(1)
            experts(1)

        @block.gpsimd
        def _(pool):
            ch = Chain(pool, S["pool_self"])
            p = nc.gpsimd
            p.memset(ep[:, :, LE:LPAD], -1.0)
            p.memset(rep[:, :, 2:8], -1.0)
            p.memset(pe_[:, :, NE:EPAD], -1.0)
            p.memset(rep8[:, :, TOPK:8], -1.0)
            ch.link(p.memset(VA[:, :, :, :, :], 0.0))
            pool.wait_ge(S["const_in"], 16 * 8)
            p.tensor_copy(identb[:, :], ident[:, :])
            p.tensor_copy(tri[:, :], trif[:, :])
            p.memset(ones[:, :], 1.0)
            p.memset(one[:, :], 1.0)
            p.memset(VA[:, :, :, :, HD:HD + 1], 1.0).then_inc(S["pool_const"], 4)

            def split_low(q, r, mid, low, n):
                pool.wait_ge(S["sp_rest"], q + 1)
                if q % 4 == 0 and q:
                    pool.wait_ge(S["sp_stored"], 16 * 3 * (q // 4))
                rest = R1[r].rearrange("p (x t) -> p x t", x=n)
                p.tensor_copy(mid, rest).then_inc(S["sp_mid"], 1)
                pool.wait_ge(S["sp_mid"], q + 1)
                p.tensor_tensor(low, rest, mid, ALU.subtract).then_inc(S["sp_parts"], 1)

            def attn0():
                pool.wait_ge(S["attn0_in"], 48)
                for s in range(T + 3):
                    if s < T:
                        r = s % 2
                        pool.wait_ge(S["a0_rope"], s + 1)
                        if s >= 4:
                            pool.wait_ge(S["sp_psum"], s - 3)
                        p.tensor_tensor(Y4[s % 4], RT1[r], RT2[r], ALU.add).then_inc(S["a0_sum"], 1)
                    t = s - 1
                    if 0 <= t < T:
                        y = Y4[t % 4].rearrange("p (h e) -> p h e", e=HD)
                        pool.wait_ge(S["a0_mean"], t + 1)
                        p.tensor_tensor(y, y, bc(hs2[:, t % 2, :], [P, 32, HD], 2), ALU.subtract).then_inc(S["a0_center"], 1)
                    t = s - 2
                    if 0 <= t < T:
                        y = Y4[t % 4].rearrange("p (h e) -> p h e", e=HD)
                        pool.wait_ge(S["a0_rstd"], t + 1)
                        pool.wait_ge(S["a0_square"], t + 1)
                        ch.link(p.tensor_tensor(y, y, bc(hs4[:, t % 2, :], [P, 32, HD], 2), ALU.mult))
                        ch.link(p.tensor_tensor(y, y, bc(lnsb[:, 0, :], [P, 32, HD], 1), ALU.mult))
                        p.tensor_tensor(y, y, bc(lnsb[:, 1, :], [P, 32, HD], 1), ALU.add).then_inc(S["a0_norm"], 1)
                    t = s - 3
                    if 0 <= t < T:
                        cols = slice((t % TB) * P, (t % TB + 1) * P)
                        split_low(t, t % 2, PT[:, 1, :, cols], PT[:, 2, :, cols], 4)

                def stage_v(g, b, first):
                    if not first:
                        pool.wait_ge(S["u0_av"], 4 * (2 * g + b) - 4)
                    p.tensor_copy(VA[:, b, :, :, 0:HD], V[:, TB * b:TB * b + TB, bass.ds(g * (MU * HD), MU * HD)]
                                  .rearrange("p i (m e) -> p i m e", m=MU)).then_inc(S["u0_va"], 1)
                pool.wait_ge(S["a0_v"], T)
                stage_v(0, 0, True)
                stage_v(0, 1, True)
                with pool.Fori(1, 4) as g:
                    for b in range(B):
                        stage_v(g, b, False)

            def dispatch(n):
                pool.wait_ge(S["init_rows"], 96)
                for t in range(T):
                    pool.wait_ge(S["g_weight"], n * T + t + 1)
                    pool.wait_ge(S["g_copy"], n * T + t + 1)
                    for k in range(TOPK):
                        p.indirect_dma_start(xbuf[n], bass.IndirectOffsetOnAxis(ap=idx[:, t, k:k + 1], axis=0),
                                             SRC[t % 2][:, k, :], None, bounds_check=SLOTS - 1, oob_is_err=False)\
                            .then_inc(S[f"g_scatter{t % 2}"], 16)

            def experts(n):
                def add(e, k, first=False):
                    if not (first and n == 0):
                        pool.wait_ge(S["pool_turn"], NE * n + e)
                    pool.wait_ge(S["e_ob"], NE * n + e + 1)
                    if not first:
                        pool.wait_ge(S["y_added"], 32 * (NE * n + e))
                    p.tensor_tensor(turn[:, :], one[:, :], one[:, :], ALU.mult).then_inc(S["pool_turn"], 1)
                    for s in range(2):
                        p.indirect_dma_start(y_dram[n], bass.IndirectOffsetOnAxis(ap=meta_i[:, k, s:s + 1], axis=0),
                                             OB[k][:, s, :], None, bounds_check=B * N + 2 * P - 1, oob_is_err=True,
                                             compute_op=ALU.add).then_inc(S["y_added"], 16)
                pool.wait_ge(S["y_stored"], 16 * T * (n + 1))
                for k in range(NB):
                    add(k, k, k == 0)
                with pool.Fori(1, NE // NB) as h:
                    for k in range(NB):
                        add(NB * h + k, k)

            def attn1():
                for r in range(8):
                    x = r % 4
                    split_low(T + r, r % 2, PT[:, 1, x:x + 1, :], PT[:, 2, x:x + 1, :], 1)
                pool.wait_ge(S["sp_stored"], 16 * 12)
                for r in range(4):
                    last = p.memset(KS[r][64:96, :, :], 1.0)
                last.then_inc(S["stack_pad"], 1)
                pool.wait_ge(S["stack_pad"], 1)

                def stage_v(u, b, g, fresh):
                    if not fresh:
                        pool.wait_ge(S["u1_av"], 4 * u - 4)
                    src = V[:, TB * b:TB * b + TB, bass.ds(g * 32, 32)].rearrange("p i (m e) -> p i m e", m=2)
                    p.tensor_tensor(VA[:, b, :, 0:2, 0:HD], src, one[:, :].unsqueeze(2).unsqueeze(3).broadcast_to([P, TB, 2, HD]), ALU.mult).then_inc(S["u1_va"], 1)

                def split_maxima(w, par, first=False):
                    pool.wait_ge(S["u1_maxed"], 16 * w + 16)
                    if not first:
                        pool.wait_ge(S["u1_mt"], w)
                    neg = nm[:, par, :, :]
                    p.tensor_tensor(mp[:, :, 0, :], neg, bc(one[:, :], [P, TB, MU], 2), ALU.mult).then_inc(S["u1_sp"], 1)
                    pool.wait_ge(S["u1_sp"], 3 * w + 1)
                    p.tensor_tensor(nmr[:, :, :], neg, mp[:, :, 0, :], ALU.subtract).then_inc(S["u1_sp"], 1)
                    pool.wait_ge(S["u1_sp"], 3 * w + 2)
                    p.tensor_tensor(mp[:, :, 1, :], nmr[:, :, :], bc(one[:, :], [P, TB, MU], 2), ALU.mult).then_inc(S["u1_sp"], 1)
                    pool.wait_ge(S["u1_sp"], 3 * w + 3)
                    p.tensor_tensor(mp[:, :, 2, :], nmr[:, :, :], mp[:, :, 1, :], ALU.subtract).then_inc(S["u1_split"], 1)

                def unit(i4, u4, first=False, last=False):
                    if last and u4 == 3:
                        return
                    u = 4 * i4 + u4
                    if not (first and u4 == 0):
                        stage_v(u + 1, (u4 + 1) % 2, 2 * i4 + (u4 + 1) // 2, False)
                    split_maxima(u + 1, (u4 + 1) % 2)
                pool.wait_ge(S["a1_v"], T)
                stage_v(0, 0, 0, True)
                stage_v(1, 1, 0, True)
                split_maxima(0, 0, True)
                for u4 in range(4):
                    unit(0, u4, first=True)
                with pool.Fori(1, 3) as i4:
                    for u4 in range(4):
                        unit(i4, u4)
                for u4 in range(4):
                    unit(3, u4, last=True)

            attn0()
            dispatch(0)
            experts(0)
            attn1()
            dispatch(1)
            experts(1)


def kernel(**inputs):
    import numpy as np
    import concourse.bacc as bacc
    from concourse.bass_utils import run_bass_kernel_spmd as run

    def rows(a):
        return np.ascontiguousarray(a.reshape(-1, 128, a.shape[-1]).transpose(1, 0, 2))

    i = {k: np.asarray(v) for k, v in inputs.items()}
    f = np.float32
    arrays = {"x": i["L0_attn_x"].reshape(B * N, D)}
    lora_a = i["L0_ffn_lora_A"].reshape(LE * RANK, D)
    arrays["wf"] = rows(np.concatenate([i["L0_ffn_weight"].T, lora_a.T, i["L0_ffn_router_w"].T], 1))
    arrays["lb"] = i["L0_ffn_lora_B"].transpose(0, 2, 1).reshape(LE * RANK, D)
    arrays["wa0"] = rows(np.concatenate([i["L0_attn_w_qkv"], i["L0_attn_w_out"]], 1))
    arrays["ln_scale"], arrays["ln_bias"] = i["L0_attn_ln_scale"], i["L0_attn_ln_bias"]
    arrays["wa1"] = rows(np.concatenate([i["L1_attn_Wq"].T, i["L1_attn_Wk"].T, i["L1_attn_Wv"].T, i["L1_attn_Wo"].T], 1))
    for short, name in (("lq1", "lambda_q1"), ("lk1", "lambda_k1"), ("lq2", "lambda_q2"), ("lk2", "lambda_k2"),
                        ("subln", "subln_weight")):
        arrays[short] = i["L1_attn_" + name]
    arrays["gw"] = rows(i["L1_ffn_gate_w"].T)
    w13 = np.concatenate([i["L1_ffn_w1"], i["L1_ffn_w3"]], 2)
    arrays["w13"] = w13.reshape(NE, C, P, 2 * INTER).transpose(2, 0, 1, 3).reshape(P, -1)
    arrays["w2"] = i["L1_ffn_w2"].reshape(NE, 2, IH, D).transpose(0, 2, 1, 3).reshape(NE * IH, 2 * D)
    arrays["sw13"] = rows(np.concatenate([i["L1_ffn_sw1"], i["L1_ffn_sw3"]], 1))
    arrays["sw2"] = rows(np.concatenate([i["L1_ffn_sw2"], np.zeros((3 * P - SI, D), f)], 0))
    arrays["ident"] = np.eye(P, dtype=f)
    arrays["mask"] = np.triu(np.ones((P, P), f))
    arrays["trif"] = np.triu(np.ones((P, P), f), 1)
    arrays["slot0"] = np.tile(np.arange(NE, dtype=f) * CAP + 1, (P, 1))
    arrays["tok"] = np.arange(B * N, dtype=f).reshape(T, P).T
    empty = np.zeros((P, 2, ROW), f)
    empty[:, :, D + 1] = B * N + np.arange(2 * P).reshape(2, P).T
    arrays["empty"] = empty
    inv = (f(1.0) / f(10000.0) ** (np.arange(0, HD, 2, dtype=f) / f(HD))).astype(f)
    angle = np.arange(N, dtype=f)[:, None] * inv[None, :]
    c, s = np.cos(angle), np.sin(angle)
    arrays["rope_c"] = rows(np.concatenate([c, c], 1))
    arrays["rope_s"] = rows(np.concatenate([-s, s], 1))
    arrays = {k: np.ascontiguousarray(v) for k, v in arrays.items()}

    nc = bacc.Bacc("TRN2", target_bir_lowering=False, num_devices=1)
    d = {k: nc.dram_tensor(k + "_dram", v.shape, F32, kind="ExternalInput").ap() for k, v in arrays.items()}
    out = nc.dram_tensor("out_dram", (B, N, D), F32, kind="ExternalOutput").ap()
    macaron_kernel(nc, d, out)
    r = run(nc, [{k + "_dram": v for k, v in arrays.items()}], core_ids=[0])
    return r.results[0]["out_dram"]
```

```python
from contextlib import ExitStack

import concourse.bass as bass
from concourse import mybir

F32 = mybir.dt.float32
BF16 = mybir.dt.bfloat16
U32 = mybir.dt.uint32
ALU = mybir.AluOpType
ACT = mybir.ActivationFunctionType
AX_X = mybir.AxisListType.X

P = 128
B, N, D = 2, 512, 256
T = B * N // P
TB = N // P
C = D // P
EPS = 1e-5
LE, RANK = 8, 16
FW = D + LE * RANK + LE
LPAD = 14
HD = 16
MU = 4
RUNS = [(0, 3, 0, 1), (3, 3, 0, 2), (6, 2, 0, 0)]
KPARTS = 5
LAMBDA_INIT = 0.8 - 0.6 * 2.718281828459045 ** (-0.3 * 12)
SCALE1 = 8.0 ** -0.5
NE, TOPK, CAP, INTER = 32, 6, 256, 176
IH = INTER // 2
EPAD = NE + 2
SI = 2 * INTER
ROW = D + 2
SLOTS = NE * CAP
NB = 4
SKIP = 65536.0


class Chain:

    def __init__(self, eng, sem):
        self.eng, self.sem, self.n = eng, sem, 0

    def link(self, ins):
        ins.then_inc(self.sem, 1)
        self.n += 1
        self.eng.wait_ge(self.sem, self.n)


def macaron_kernel(nc, d, out):
    ctx = ExitStack()
    with ctx:
        def sb(name, shape, dt=F32):
            return ctx.enter_context(nc.sbuf_tensor(name, shape, dt))

        def sem(name):
            return ctx.enter_context(nc.semaphore(name))

        parts = [nc.dram_tensor(f"parts{n}", [2, B, D // w, KPARTS, w, N], BF16, kind="Internal").ap()
                 for n, w in enumerate((HD, HD // 2))]
        xbuf = [nc.dram_tensor(f"xbuf{n}", [SLOTS, ROW], F32, kind="Internal").ap() for n in range(2)]
        y_dram = [nc.dram_tensor(f"y{n}", [B * N + 2 * P, D], F32, kind="Internal").ap() for n in range(2)]

        X = sb("X", [P, T, D])
        XN = sb("XN", [P, T, D])
        XT = sb("XT", [P, C, B * N])
        V = sb("V", [P, T, D])
        W13 = sb("W13", [P, NE * C * 2 * INTER])
        WF = sb("WF", [P, C, FW])
        LB = sb("LB", [P, D])
        WA = sb("WA", [P, C, 4 * D])
        SW13 = V[:, :, :].rearrange("p t d -> p (t d)")[:, 0:C * 2 * SI].rearrange("p (c n) -> p c n", c=C)
        SW2 = sb("SW2", [P, 3, D])
        GW = sb("GW", [P, C, NE])
        stack_mem = sb("stack_mem", [P, 8192])
        e_mem = sb("e_mem", [P, 4096])
        VA = sb("VA", [P, 2, TB, MU, 32])
        OS = sb("OS", [P, 2, N])
        ident = sb("ident", [P, P])
        trif = sb("trif", [P, P])
        identb = sb("identb", [P, P], BF16)
        mask = sb("mask", [P, P])
        tri = sb("tri", [P, P], BF16)
        ones = sb("ones", [P, P], BF16)
        slot0 = sb("slot0", [P, NE])
        tok = sb("tok", [P, T])
        empty = sb("empty", [P, 2, ROW])
        rope_c = sb("rope_c", [P, TB, HD])
        rope_s = sb("rope_s", [P, TB, HD])
        lnsb = sb("lnsb", [P, 2])
        subw = sb("subw", [P, 1])
        lamv = sb("lamv", [P, 4, 8])
        lam = sb("lam", [P, 8])
        st = sb("st", [P, T, 6])
        mv = sb("mv", [P, T, 2])
        rv = sb("rv", [P, T])
        rstd = sb("rstd", [P, T])
        m4 = sb("m4", [P, 4])
        el = sb("el", [P, 4, LE])
        ep = sb("ep", [P, 4, LPAD])
        v8 = sb("v8", [P, T, 8])
        rep = sb("rep", [P, 4, 8])
        rpl = sb("rpl", [P, 4, LPAD])
        g4 = sb("g4", [P, 4, LE])
        s4 = sb("s4", [P, 4])
        hs1 = sb("hs1", [P, 2, 32])
        hs2 = sb("hs2", [P, 2, 32])
        hs3 = sb("hs3", [P, 2, 32])
        hs4 = sb("hs4", [P, 2, 32])
        rec = sb("rec", [P, 2, TB, MU])
        amap = sb("amap", [P, TB, MU, HD])
        nm = sb("nm", [P, 2, TB, MU])
        nmr = sb("nmr", [P, TB, MU])
        one = sb("one", [P, 1])
        turn = sb("turn", [P, 1])
        mp = sb("mp", [P, TB, 3, MU], BF16)
        mr = sb("mr", [3 * MU, N], BF16)
        m8 = sb("m8", [P, T])
        rs8 = sb("rs8", [P, T])
        pe_ = sb("pe", [P, T, EPAD])
        rep8 = sb("rep8", [P, T, 8])
        mkb = sb("mkb", [P, T, NE], BF16)
        s8 = sb("s8", [P, T, 8])
        s8z = sb("s8z", [P, T, 8])
        idx = sb("idx", [P, T, 8], U32)
        junk = sb("junk", [P, TOPK, NE])
        meta_w = sb("meta_w", [P, NB, 2])
        meta_i = sb("meta_i", [P, NB, 2], U32)
        PS = ctx.enter_context(nc.psum_tensor("PS", [P, 8, 512], F32))

        KS = [stack_mem[:, 2048 * r:2048 * r + 1024].bitcast(BF16).rearrange("p (m t) -> p m t", m=MU) for r in range(4)]
        QS = [stack_mem[:, 2048 * r + 1024:2048 * r + 2048].bitcast(BF16).rearrange("p (m t) -> p m t", m=MU) for r in range(4)]
        E = [e_mem[:, 2048 * r:2048 * r + 2048].rearrange("p (m t) -> p m t", m=MU) for r in range(2)]
        Y4 = [stack_mem[:, 512 * r:512 * r + 512] for r in range(4)]
        SQ = [stack_mem[:, 2048 + 512 * r:2560 + 512 * r] for r in range(2)]
        R1 = [stack_mem[:, 3072 + 512 * r:3584 + 512 * r] for r in range(2)]
        xn_mem = XN[:, :, :].rearrange("p t d -> p (t d)")
        PT = [[mem.bitcast(BF16).rearrange("p (x t) -> p x t", x=4) for mem in three] for three in (
            (stack_mem[:, 4096:5120], stack_mem[:, 5120:6144], stack_mem[:, 6144:7168]),
            (xn_mem[:, 0:1024], xn_mem[:, 1024:2048], e_mem[:, 2048:3072]))]
        FULL = [e_mem[:, 3072 + 512 * r:3584 + 512 * r] for r in range(2)]
        EJ = [mem.rearrange("p (m t) -> p m t", m=MU) for mem in
              (stack_mem[:, 0:2048], stack_mem[:, 2048:4096], e_mem[:, 0:2048], e_mem[:, 2048:4096])]
        RT1 = [e_mem[:, 512 * r:512 * r + 512] for r in range(2)]
        RT2 = [e_mem[:, 1024 + 512 * r:1536 + 512 * r] for r in range(2)]
        ZS = e_mem[:, 2048:2048 + 512]
        ZF = e_mem[:, 2560:2560 + 512]
        Z = ZF.rearrange("p (t e r) -> p t e r", t=4, e=LE)
        at = [0]

        def take(mem, n):
            at[0] += n
            return mem[:, at[0] - n:at[0]]

        SRC = [take(stack_mem, TOPK * ROW).rearrange("p (k r) -> p k r", k=TOPK) for _ in range(2)]
        at[0] = 0
        XB = [take(stack_mem, 2 * ROW).rearrange("p (s r) -> p s r", s=2) for _ in range(NB)]
        W2E = [take(stack_mem, 512)[0:IH, :].rearrange("p (i n) -> p i n", i=2) for _ in range(NB)]
        XBT = [take(stack_mem, 512).rearrange("p (c s) -> p c s", c=C) for _ in range(2)]
        OB = [take(stack_mem, 512).rearrange("p (s n) -> p s n", s=2) for _ in range(NB)]
        at[0] = 0
        HSH = [take(e_mem, SI) for _ in range(2)]
        GSH = [take(e_mem, SI) for _ in range(2)]
        GTS = take(e_mem, 3 * P).rearrange("p (k t) -> p k t", k=3)
        GT = [take(e_mem, 512)[0:IH, :].rearrange("p (i s) -> p i s", i=2) for _ in range(2)]
        rpe = take(e_mem, T * EPAD).rearrange("p (t e) -> p t e", t=T)
        mk = take(e_mem, T * NE).rearrange("p (t e) -> p t e", t=T)
        wt = take(e_mem, T * NE).rearrange("p (t e) -> p t e", t=T)
        at[0] = 0
        HE = [[take(e_mem, INTER) for _ in range(2)] for _ in range(2)]
        GE = [[take(e_mem, INTER) for _ in range(2)] for _ in range(2)]
        rms = stack_mem[:, 0:4 * P].rearrange("p (k h) -> p k h", k=4)
        POS = PS[:, 5, 0:T * NE].rearrange("p (t e) -> p t e", t=T)
        MT = PS[0:3 * MU, 7, 0:N // 2].bitcast(BF16)
        LOG = PS[:, 4, 0:T * NE].rearrange("p (t e) -> p t e", t=T)

        STORED = 16 * C * (3 + KPARTS)
        STACK = 16 * 2 * len(RUNS)

        RING = [(start + x) % 3 for start in (0, 1, 2, 1) for x in range(16)]
        LAST = [next(k for k in range(1, 8) if RING[y - k] == RING[y]) for y in range(64)]

        names = """x_in0 x_in1 x_in2 x_in3 ffw_in attn0_in attn1_in shared_in w13_in const_in lam_in
        pool_const init_rows dve_self act_self pool_self final_store
        ln_var ln_rstd xn_ready xt_psum xt_ready
        ff_psum ff_shift ff_exp ff_z ff_zt_psum ff_zt ff_out ff_done
        a0_proj a0_v a0_rope a0_sum a0_mean a0_center a0_square a0_var a0_rstd a0_norm
        sp_psum sp_high sp_rest sp_parts sp_stored0 sp_stored1
        u0_scores u0_square u0_e u0_av u0_os u0_ot u0_rows u0_va
        att_ready wo_psum res_done
        a1_v_psum a1_v u1_max u1_maxed u1_split u1_mt u1_mr u1_mrow u1_scores u1_exp u1_av u1_os u1_ot u1_rows u1_va lam_sum lam_exp
        rms_in rms_var rms_rstd
        g_logits g_shift g_exp g_mask g_pos g_weight g_copy g_scatter0 g_scatter1
        s_h s_silu s_g s_gt_psum s_gt s_out s_y y_stored
        e_xb0 e_xb1 e_xb2 e_xb3 e_w20 e_w21 e_w22 e_w23 e_meta e_xbt_psum e_xbt e_h e_silu e_g e_gt_psum e_gt e_out e_ob y_added stack_pad pool_turn sw13_in u0_masked u0_rec u1_rec u1_diff sp_mid u1_sp a0_full""".split()
        S = {n: sem(n) for n in names}
        stk = [sem(f"stack_in{r}") for r in range(4)]

        block = ctx.enter_context(nc.Block())

        def bc(ap, shape, dim):
            return ap.unsqueeze(dim).broadcast_to(shape)

        LN_TURN = [0, 1, 3, 4, 5, 7]

        @block.sync
        def _(sp):
            def load_x(src):
                for q in range(4):
                    sp.dma_start(X[:, 2 * q:2 * q + 2, :], src[2 * P * q:2 * P * (q + 1), :].rearrange("(t p) d -> p t d", p=P))\
                        .then_inc(S[f"x_in{q}"], 16)

            load_x(d["x"])
            for dst, src in ((ident, "ident"), (mask, "mask"), (trif, "trif"), (slot0, "slot0"), (tok, "tok")):
                sp.dma_start(dst[:, :], d[src]).then_inc(S["const_in"], 16)
            sp.dma_start(WF[:, :, :], d["wf"]).then_inc(S["ffw_in"], 16)
            sp.dma_start(LB[:, :], d["lb"]).then_inc(S["ffw_in"], 16)
            for dst, src in ((rope_c, "rope_c"), (rope_s, "rope_s"), (empty, "empty")):
                sp.dma_start(dst[:, :, :], d[src]).then_inc(S["const_in"], 16)
            sp.dma_start(WA[:, :, :], d["wa0"]).then_inc(S["attn0_in"], 16)
            for j, name in enumerate(("ln_scale", "ln_bias")):
                sp.dma_start(lnsb[:, j:j + 1], bc(d[name], [P // HD, HD], 0)).then_inc(S["attn0_in"], 16)
            sp.dma_start(SW2[:, :, :], d["sw2"]).then_inc(S["shared_in"], 16)
            sp.dma_start(GW[:, :, :], d["gw"]).then_inc(S["shared_in"], 16)
            for j, name in enumerate(("lq1", "lk1", "lq2", "lk2")):
                sp.dma_start(lamv[:, j, :], bc(d[name], [P, 8], 0)).then_inc(S["lam_in"], 16)
            sp.dma_start(subw[:, :], bc(d["subln"], [P // HD, HD], 0)).then_inc(S["lam_in"], 16)
            sp.wait_ge(S["const_in"], 16 * 8)
            for n in range(2):
                for s in range(2):
                    sp.dma_start(xbuf[n].rearrange("(e s p) r -> p e s r", s=2, p=P)[:, :, s, :],
                                 bc(empty[:, s, :], [P, NE, ROW], 1)).then_inc(S["init_rows"], 16)
                sp.dma_start(y_dram[n][B * N:, :].rearrange("(s p) d -> p s d", p=P), empty[:, :, 0:D])\
                    .then_inc(S["init_rows"], 16)
            q = NE * C * 2 * INTER // 4
            for j in range(4):
                sp.dma_start(W13[:, j * q:(j + 1) * q], d["w13"][:, j * q:(j + 1) * q]).then_inc(S["w13_in"], 16)

            def load_stack(n, slot, g, b):
                w = parts[n].shape[4]
                for first, count, cq, ck in RUNS:
                    for dst, x, c in ((QS, 0, cq), (KS, 1, ck)):
                        src = parts[n][x, b, bass.ds(g * MU, MU), c:c + count, :, :]
                        sp.dma_start(dst[slot][w * first:w * (first + count), :, :],
                                     src.rearrange("m c i t -> (c i) m t")).then_inc(stk[slot], 16)

            def first_stacks(n, units):
                w = parts[n].shape[4]
                for b in range(B):
                    sp.wait_ge(S["sp_parts"], T * n + 4 * (b + 1))
                    for h in range(C):
                        maps = slice(h * (P // w), (h + 1) * (P // w))
                        for x in range(2):
                            for slot in range(KPARTS if x else 3):
                                sp.dma_start(parts[n][x, b, maps, slot, :, :], PT[b][slot % 3][:, 2 * x + h, :])\
                                    .then_inc(S[f"sp_stored{b}"], 16)
                    sp.wait_ge(S[f"sp_stored{b}"], STORED * (n + 1))
                    for slot, g in units[b]:
                        load_stack(n, slot, g, b)

            def experts(n):
                def load(e, k, first=False):
                    if not (first and n == 0):
                        sp.wait_ge(S["e_meta"], n * NE + e - NB + 1)
                        sp.wait_ge(S["e_xbt_psum"], n * NE + e - NB + 1)
                        sp.wait_ge(S["e_out"], n * NE + e - NB + 1)
                    sp.dma_start(XB[k], xbuf[n][bass.ds(e * CAP, CAP), :].rearrange("(s p) r -> p s r", p=P))\
                        .then_inc(S[f"e_xb{k}"], 16)
                    sp.dma_start(W2E[k], d["w2"][bass.ds(e * IH, IH), :].rearrange("p (i n) -> p i n", i=2))\
                        .then_inc(S[f"e_w2{k}"], 16)
                for r in range(2):
                    sp.wait_ge(S[f"g_scatter{r}"], (n + 1) * 4 * TOPK * 16)
                for k in range(NB):
                    load(k, k, True)
                with sp.Fori(1, NE // NB) as h:
                    for k in range(NB):
                        load(NB * h + k, k)

            def store_tiles(n):
                for t in range(T):
                    sp.wait_ge(S["s_y"], n * T + t + 1)
                    sp.dma_start(y_dram[n][t * P:(t + 1) * P, :], X[:, t, :]).then_inc(S["y_stored"], 16)

            first_stacks(0, [[(2, 0)], [(3, 0)]])
            with sp.Fori(1, 4) as g:
                for b in range(B):
                    sp.wait_ge(S["u0_scores"], 16 * g + 8 * b - 8)
                    load_stack(0, 2 + b, g, b)
            sp.wait_ge(S["wo_psum"], 4)
            sp.dma_start(SW13, d["sw13"]).then_inc(S["sw13_in"], 16)
            sp.dma_start(WA[:, :, :], d["wa1"]).then_inc(S["attn1_in"], 16)
            store_tiles(0)
            experts(0)
            sp.wait_ge(S["y_added"], 16 * 2 * NE)
            load_x(y_dram[0])
            def max_rows(u, slot):
                sp.wait_ge(S["u1_mr"], u + 1)
                sp.dma_start(QS[slot][64:67, :, :], mr[:, :]).then_inc(S["u1_mrow"], 16)
            first_stacks(1, [[(0, 0), (2, 1)], [(1, 0), (3, 1)]])
            max_rows(0, 0)
            max_rows(1, 1)
            with sp.Fori(0, 3) as i:
                for r in range(4):
                    sp.wait_ge(S["u1_scores"], 64 * i + 16 * r + 16)
                    load_stack(1, r, 2 * i + 2 + r // 2, r % 2)
                    max_rows(4 * i + r + 2, (r + 2) % 4)
            max_rows(14, 2)
            max_rows(15, 3)
            sp.wait_ge(S["wo_psum"], 8)
            sp.dma_start(SW13, d["sw13"]).then_inc(S["sw13_in"], 16)
            store_tiles(1)
            experts(1)
            sp.wait_ge(S["y_added"], 16 * 2 * NE * 2)
            sp.dma_start(out.rearrange("b n d -> (b n) d"), y_dram[1][0:B * N, :]).then_inc(S["final_store"], 16)
            sp.wait_ge(S["final_store"], 16)


        @block.tensor
        def _(pe):
            mm = nc.tensor.matmul

            def transposes(turn, ready, value):
                for tt in range(4):
                    pe.wait_ge(ready, value(tt))
                    for c in range(C):
                        for h in range(2):
                            t = 2 * tt + h
                            o = c * 256 + h * P
                            last = nc.tensor.transpose(PS[:, tt, o:o + P], XN[:, t, c * P:(c + 1) * P], ident[:, :])
                    last.then_inc(S["xt_psum"], 1)

            def ln_transposes(n):
                transposes(LN_TURN[n], S["xn_ready"], lambda tt: T * n + 2 * tt + 2)

            def xt(c, t):
                return XT[:, c, t * P:(t + 1) * P]

            def ffn(n):
                ln_transposes(2 * n)
                for g in range(2):
                    if g:
                        pe.wait_ge(S["ff_done"], 2 * n + 1)
                    for i in range(4):
                        t = 4 * g + i
                        if i % 2 == 0:
                            pe.wait_ge(S["xt_ready"], 4 * LN_TURN[2 * n] + t // 2 + 1)
                        for c in range(C):
                            last = mm(PS[:, 4 + i, 0:FW], xt(c, t), WF[:, c, :], start=(c == 0), stop=(c == C - 1))
                    last.then_inc(S["ff_psum"], 1)
                    pe.wait_ge(S["ff_z"], 2 * n + g + 1)
                    pe.wait_ge(S["xt_ready"], 4 * LN_TURN[2 * n] + 4)
                    for i in range(4):
                        last = nc.tensor.transpose(PS[:, 0, i * P:(i + 1) * P], ZF[:, i * P:(i + 1) * P], ident[:, :])
                    last.then_inc(S["ff_zt_psum"], 1)
                    pe.wait_ge(S["ff_zt"], 2 * n + g + 1)
                    for i in range(4):
                        last = mm(PS[:, 4 + i, 0:D], ZS[:, i * P:(i + 1) * P], LB[:, :],
                                  start=False, stop=True, skip_group_check=True)
                    last.then_inc(S["ff_out"], 1)

            def attention_out(k):
                if k:
                    transposes(6, S["att_ready"], lambda tt: tt + 1)
                else:
                    transposes(2, S["u0_rows"], lambda tt: 8)
                for tt in range(4):
                    pe.wait_ge(S["xt_ready"], 4 * (2 + 4 * k) + tt + 1)
                    for h in range(2):
                        for c in range(C):
                            last = mm(PS[:, 4 + tt, h * D:(h + 1) * D], xt(c, 2 * tt + h), WA[:, c, 3 * D:],
                                      start=(c == 0), stop=(c == C - 1))
                    last.then_inc(S["wo_psum"], 1)

            def attn0():
                ln_transposes(1)
                pe.wait_ge(S["attn0_in"], 48)
                for s in range(T + 3):
                    if s < T:
                        pe.wait_ge(S["xt_ready"], 4 + s // 2 + 1)
                        if s >= 2:
                            pe.wait_ge(S["a0_rope"], s - 1)
                            pe.wait_ge(S["a0_v"], s - 1)
                        for o, lo, hi in ((4, 0, 2 * D), (5, 2 * D, 3 * D)):
                            for c in range(C):
                                last = mm(PS[:, o + 2 * (s % 2), 0:hi - lo], xt(c, s), WA[:, c, lo:hi],
                                          start=(c == 0), stop=(c == C - 1))
                        last.then_inc(S["a0_proj"], 1)
                    t = s - 3
                    if t >= 0:
                        pe.wait_ge(S["a0_norm"], t + 1)
                        pe.wait_ge(S["xt_ready"], 8)
                        if t >= 2:
                            pe.wait_ge(S["a0_full"], t - 1)
                        for x in range(4):
                            last = nc.tensor.transpose(PS[:, t % 2, x * P:(x + 1) * P], Y4[t % 4][:, x * P:(x + 1) * P],
                                                       ident[:, :])
                        last.then_inc(S["sp_psum"], 1)

                def av(u, b, j):
                    pe.wait_ge(S["u0_e"], 4 * u + j + 1)
                    for m in range(MU):
                        last = mm(PS[32 * m:32 * m + 32, 4 + b, j * P:N], VA[:, b, j, m, :],
                                  EJ[j][:, m, 0:N - j * P], start=(j == 0), stop=(j == TB - 1),
                                  skip_group_check=True)
                    last.then_inc(S["u0_av"], 1)

                def turn_rows(u, b, fresh):
                    pe.wait_ge(S["u0_os"], u + 1)
                    if not fresh:
                        pe.wait_ge(S["u0_rows"], u - 1)
                    for i in range(TB):
                        last = nc.tensor.transpose(PS[:, 6 + b, i * P:(i + 1) * P], OS[:, b, i * P:(i + 1) * P], ident[:, :])
                    last.then_inc(S["u0_ot"], 1)

                def unit(g, b, first=False):
                    u = 2 * g + b
                    pe.wait_ge(stk[2 + b], STACK * (g + 1))
                    for j in range(TB):
                        for hp in range(2):
                            if not (first and b == 0 and j == 0):
                                pe.wait_ge(S["u0_square"], 8 * u + 2 * j + hp - 1)
                            elif hp == 0:
                                pe.wait_ge(S["a0_full"], T)
                                pe.wait_ge(S["a0_rope"], T)
                                pe.wait_ge(S["a0_v"], T)
                            for k in range(2):
                                m = 2 * hp + k
                                last = mm(PS[:, 2 * hp + k, 0:N - j * P], KS[2 + b][:, m, j * P:(j + 1) * P],
                                          QS[2 + b][:, m, j * P:N], start=True, stop=True)
                            last.then_inc(S["u0_scores"], 1)
                        if j == 3 and not (first and b == 0):
                            turn_rows(u - 1, 1 - b, first)
                        if j >= 2:
                            if j == 2:
                                pe.wait_ge(S["u0_va"], u + 1)
                                if not first:
                                    pe.wait_ge(S["u0_os"], u - 1)
                            av(u, b, j - 2)
                        elif not (first and b == 0):
                            av(u - 1, 1 - b, j + 2)
                unit(0, 0, True)
                unit(0, 1, True)
                with pe.Fori(1, 4) as g:
                    for b in range(B):
                        unit(g, b)
                av(7, 1, 2)
                av(7, 1, 3)
                turn_rows(7, 1, False)
                attention_out(0)

            def route(n):
                ln_transposes(3 + 2 * n)
                pe.wait_ge(S["shared_in"], 32)
                pe.wait_ge(S["sw13_in"], 16 * (n + 1))
                pe.wait_ge(S["xt_ready"], 4 * LN_TURN[3 + 2 * n] + 4)
                for t in range(T):
                    for c in range(C):
                        last = mm(LOG[:, t, :], xt(c, t), GW[:, c, :], start=(c == 0), stop=(c == C - 1))
                last.then_inc(S["g_logits"], 1)

            def positions(n):
                pe.wait_ge(S["g_mask"], n + 1)
                for t in range(T):
                    for k in range(t + 1):
                        last = mm(POS[:, t, :], (ones if k < t else tri)[:, :], mkb[:, k, :],
                                  start=(k == 0), stop=(k == t))
                last.then_inc(S["g_pos"], 1)

            def shared(n):
                def first_half(t):
                    q = n * T + t
                    for k in range(2):
                        if t >= 2:
                            pe.wait_ge(S["s_g"], q - 1)
                        for c in range(C):
                            last = mm(PS[:, 2 * k + t % 2, 0:SI], xt(c, t), SW13[:, c, k * SI:(k + 1) * SI],
                                      start=(c == 0), stop=(c == C - 1))
                    last.then_inc(S["s_h"], 1)

                def second_half(t):
                    q = n * T + t
                    pe.wait_ge(S["s_g"], q + 1)
                    if t >= 1:
                        pe.wait_ge(S["s_gt"], q)
                    for k in range(3):
                        w = min(P, SI - k * P)
                        last = nc.tensor.transpose(PS[0:w, 6, k * P:(k + 1) * P], GSH[t % 2][:, k * P:k * P + w], ident[:, :])
                    last.then_inc(S["s_gt_psum"], 1)
                    pe.wait_ge(S["s_gt"], q + 1)
                    if t >= 1:
                        pe.wait_ge(S["s_y"], q)
                    for k in range(3):
                        w = min(P, SI - k * P)
                        last = mm(PS[:, 7, 0:D], GTS[0:w, k, :], SW2[0:w, k, :], start=(k == 0), stop=(k == 2))
                    last.then_inc(S["s_out"], 1)
                first_half(0)
                first_half(1)
                positions(n)
                for t in range(T):
                    second_half(t)
                    if t + 2 < T:
                        first_half(t + 2)

            def experts(n):
                def turn_x(e, k, h, fresh=False):
                    pe.wait_ge(S[f"e_xb{k}"], 16 * (NE // NB) * n + 16 * (h + 1))
                    if not fresh:
                        pe.wait_ge(S["e_xbt"], NE * n + e - 1)
                    for c in range(C):
                        for s in range(2):
                            last = nc.tensor.transpose(PS[:, k % 2, c * 256 + s * P:c * 256 + (s + 1) * P],
                                                       XB[k][:, s, c * P:(c + 1) * P], ident[:, :])
                    last.then_inc(S["e_xbt_psum"], 1)

                def up(e, k, s, fresh):
                    if s == 0:
                        pe.wait_ge(S["e_xbt"], NE * n + e + 1)
                    if not fresh:
                        pe.wait_ge(S["e_g"], 2 * (NE * n + e) + s - 3)
                    for c in range(C):
                        last = mm(PS[:, 2 + 2 * (k % 2) + s, 0:2 * INTER], XBT[k % 2][:, c, s * P:(s + 1) * P],
                                  W13[:, bass.ds(e * (C * 2 * INTER) + c * 2 * INTER, 2 * INTER)],
                                  start=(c == 0), stop=(c == C - 1))
                    last.then_inc(S["e_h"], 1)

                def turn_g(e, k, fresh):
                    pe.wait_ge(S["e_g"], 2 * (NE * n + e) + 2)
                    if not fresh:
                        pe.wait_ge(S["e_gt"], NE * n + e)
                    for i in range(2):
                        for s in range(2):
                            last = nc.tensor.transpose(PS[0:IH, 6, (2 * i + s) * P:(2 * i + s + 1) * P],
                                                       GE[k % 2][s][:, i * IH:(i + 1) * IH], ident[:, :])
                    last.then_inc(S["e_gt_psum"], 1)

                def down(e, k, h, fresh):
                    pe.wait_ge(S["e_gt"], NE * n + e + 1)
                    pe.wait_ge(S[f"e_w2{k}"], 16 * (NE // NB) * n + 16 * (h + 1))
                    if not fresh:
                        pe.wait_ge(S["e_ob"], NE * n + e)
                    for s in range(2):
                        for i in range(2):
                            last = mm(PS[:, 7, s * D:(s + 1) * D], GT[k % 2][:, i, s * P:(s + 1) * P], W2E[k][:, i, :],
                                      start=(i == 0), stop=(i == 1))
                    last.then_inc(S["e_out"], 1)

                def step(e, k, h, first=False, last=False):
                    before, after = k - 1 if k else NB - 1, (k + 1) % NB
                    up(e, k, 0, first and k < 2)
                    if not (first and k == 0):
                        turn_g(e - 1, before, first and k == 1)
                    up(e, k, 1, first and k < 2)
                    if not (last and k == NB - 1):
                        turn_x(e + 1, after, h + (k + 1) // NB, first and k == 0)
                    if not (first and k == 0):
                        down(e - 1, before, h if k else h - 1, first and k == 1)
                pe.wait_ge(S["w13_in"], 64)
                pe.wait_ge(S["s_y"], T * (n + 1))
                turn_x(0, 0, 0, True)
                for k in range(NB):
                    step(k, k, 0, first=True)
                with pe.Fori(1, NE // NB - 1) as h:
                    for k in range(NB):
                        step(NB * h + k, k, h)
                for k in range(NB):
                    step(NE - NB + k, k, NE // NB - 1, last=True)
                turn_g(NE - 1, NB - 1, False)
                down(NE - 1, NB - 1, NE // NB - 1, False)

            def attn1():
                ln_transposes(4)
                pe.wait_ge(S["attn1_in"], 16)
                pe.wait_ge(S["xt_ready"], 4 * 5 + 4)
                for r in range(8):
                    b, x, half = r // 4, r // 2 % 2, r % 2
                    if r >= 2:
                        pe.wait_ge(S["sp_rest"], T + r - 1)
                    for c in range(C):
                        last = mm(PS[:, 4 + r % 2, :], WA[:, c, x * D + half * P:x * D + (half + 1) * P],
                                  XT[:, c, b * N:(b + 1) * N], start=(c == 0), stop=(c == C - 1))
                    last.then_inc(S["sp_psum"], 1)
                for t in range(T):
                    if t >= 2:
                        pe.wait_ge(S["a1_v"], t - 1)
                    for c in range(C):
                        last = mm(PS[:, 6 + t % 2, 0:D], xt(c, t), WA[:, c, 2 * D:3 * D], start=(c == 0), stop=(c == C - 1))
                    last.then_inc(S["a1_v_psum"], 1)

                def row_scores(w, slot, i4, x, start=False):
                    i, m = x // MU, x % MU
                    if x == 0:
                        pe.wait_ge(stk[slot], STACK * ((4 if slot >= 2 else 0) + i4 + 1))
                    y = 16 * slot + x
                    if not (start and y < LAST[y]):
                        pe.wait_ge(S["u1_maxed"], 16 * w + x - LAST[y] + 1)
                    mm(PS[:, 3 + RING[y], :], QS[slot][0:64, m, i * P:(i + 1) * P], KS[slot][0:64, m, :],
                       start=True, stop=True).then_inc(S["u1_max"], 1)

                def turn_maxima(w, first=False):
                    pe.wait_ge(S["u1_split"], w + 1)
                    if not first:
                        pe.wait_ge(S["u1_rows"], w - 2)
                    for i in range(TB):
                        last = nc.tensor.transpose(MT[:, i * P:(i + 1) * P], mp[:, i, :, :].rearrange("p c m -> p (c m)"),
                                                   identb[:, :])
                    last.then_inc(S["u1_mt"], 1)

                def av(u, b, j):
                    pe.wait_ge(S["u1_exp"], 16 * u + 4 * j + 4)
                    for m in range(MU):
                        last = mm(PS[32 * m:32 * m + 32, 6, :], VA[:, b, j, m // 2, :], E[j % 2][:, m, :],
                                  start=(j == 0), stop=(j == TB - 1), skip_group_check=True)
                    last.then_inc(S["u1_av"], 1)

                def turn_rows(u, b):
                    pe.wait_ge(S["u1_os"], u + 1)
                    for i in range(TB):
                        last = nc.tensor.transpose(PS[:, 7, i * P:(i + 1) * P], OS[:, b, i * P:(i + 1) * P], ident[:, :])
                    last.then_inc(S["u1_ot"], 1)

                def unit(i4, u4, first=False, last=False):
                    u = 4 * i4 + u4
                    final = last and u4 == 3
                    pe.wait_ge(S["u1_mrow"], 16 * u + 16)
                    pe.wait_ge(S["u1_va"], u + 1)
                    for j in range(TB):
                        if j == 1 and not final:
                            turn_maxima(u + 1, first and u4 < 2)
                        if j == 2 and not (first and u4 == 0):
                            if final:
                                pe.wait_ge(S["u1_rows"], u - 1)
                            else:
                                pe.wait_ge(S["u1_mr"], u + 2)
                            turn_rows(u - 1, (u4 + 1) % 2)
                        for m in range(MU):
                            y = 16 * u4 + 4 * j + m
                            if not (first and y < LAST[y]):
                                pe.wait_ge(S["u1_exp"], 16 * u + 4 * j + m - LAST[y] + 1)
                            mm(PS[:, RING[y], :], KS[u4][0:67, m, j * P:(j + 1) * P], QS[u4][0:67, m, :],
                               start=True, stop=True).then_inc(S["u1_scores"], 1)
                            if not (last and u4 > 1):
                                row_scores(u + 2, (u4 + 2) % 4, i4 + (u4 + 2) // 4, 4 * j + m)
                        if j:
                            if j == 1 and not (first and u4 == 0):
                                pe.wait_ge(S["u1_os"], u)
                            av(u, u4 % 2, j - 1)
                        elif not (first and u4 == 0):
                            av(u - 1, (u4 + 1) % 2, 3)
                pe.wait_ge(S["sp_rest"], T + 8)
                pe.wait_ge(S["a1_v"], T)
                for x in range(16):
                    row_scores(0, 0, 0, x, True)
                turn_maxima(0, True)
                for x in range(16):
                    row_scores(1, 1, 0, x, True)
                pe.wait_ge(S["stack_pad"], 1)
                for u4 in range(4):
                    unit(0, u4, first=True)
                with pe.Fori(1, 3) as i4:
                    for u4 in range(4):
                        unit(i4, u4)
                for u4 in range(4):
                    unit(3, u4, last=True)
                av(15, 1, 3)
                pe.wait_ge(S["u1_rows"], 15)
                turn_rows(15, 1)
                attention_out(1)

            pe.wait_ge(S["const_in"], 16 * 8)
            pe.wait_ge(S["pool_const"], 4)
            pe.wait_ge(S["ffw_in"], 32)
            ffn(0)
            attn0()
            ffn(1)
            route(0)
            shared(0)
            experts(0)
            attn1()
            route(1)
            shared(1)
            experts(1)

        @block.vector
        def _(dve):
            ch = Chain(dve, S["dve_self"])
            v = nc.vector

            def stats(q):
                for t in (2 * q, 2 * q + 1):
                    last = v.bn_stats(st[:, t, :], X[:, t, :])
                return last

            def layer_norm(n, loaded=0):
                for q in range(0 if loaded else 3, 4):
                    if loaded:
                        dve.wait_ge(S[f"x_in{q}"], 16 * loaded)
                    last = stats(q)
                ch.link(last)
                for t in range(T):
                    last = v.bn_aggr(mv[:, t, :], st[:, t, :])
                ch.link(last)
                ch.link(v.tensor_scalar(rv[:, :], mv[:, :, 1], EPS, None, ALU.add))
                v.reciprocal(rv[:, :], rv[:, :]).then_inc(S["ln_var"], 1)
                dve.wait_ge(S["ln_rstd"], n + 1)
                for t in range(T):
                    v.tensor_scalar(XN[:, t, :], X[:, t, :], mv[:, t, 0:1], rstd[:, t:t + 1],
                                    ALU.subtract, ALU.mult).then_inc(S["xn_ready"], 1)

            def ffn(n):
                layer_norm(2 * n, 0 if n else 1)
                if n == 0:
                    dve.wait_ge(S["pool_const"], 4)
                for g in range(2):
                    q = 2 * n + g
                    logits = PS[:, 4:8, D + LE * RANK:FW]
                    dve.wait_ge(S["ff_psum"], q + 1)
                    ch.link(v.tensor_reduce(m4[:, :], logits, AX_X, ALU.max))
                    v.tensor_tensor(el[:, :, :], logits, bc(m4[:, :], [P, 4, LE], 2), ALU.subtract)\
                        .then_inc(S["ff_shift"], 1)
                    dve.wait_ge(S["ff_exp"], q + 1)
                    for i in range(4):
                        last = v.max(out=v8[:, i, :], in_=ep[:, i, 0:LE])
                    ch.link(last)
                    ch.link(v.tensor_copy(rep[:, :, 0:2], v8[:, 0:4, 0:2]))
                    for i in range(4):
                        last = v.match_replace(rpl[:, i, :], rep[:, i, :], ep[:, i, :], 2.0)
                    ch.link(last)
                    ch.link(v.scalar_tensor_tensor(g4[:, :, :], rpl[:, :, 0:LE], 1.5, ep[:, :, 0:LE], ALU.is_gt, ALU.mult))
                    ch.link(v.tensor_reduce(s4[:, :], g4[:, :, :], AX_X, ALU.add))
                    ch.link(v.reciprocal(s4[:, :], s4[:, :]))
                    ch.link(v.scalar_tensor_tensor(g4[:, :, :], g4[:, :, :], 32.0 / RANK, bc(s4[:, :], [P, 4, LE], 2),
                                                   ALU.mult, ALU.mult))
                    v.tensor_tensor(Z, PS[:, 4:8, D:D + LE * RANK].rearrange("p t (e r) -> p t e r", e=LE),
                                    bc(g4[:, :, :], [P, 4, LE, RANK], 3), ALU.mult).then_inc(S["ff_z"], 1)
                    dve.wait_ge(S["ff_out"], q + 1)
                    x4 = X[:, 4 * g:4 * g + 4, :]
                    ins = v.scalar_tensor_tensor(x4, PS[:, 4:8, 0:D], 0.5, x4, ALU.mult, ALU.add)
                    ins.then_inc(S["ff_done"], 1)
                    dve.wait_ge(S["ff_done"], q + 1)
                    for pair in range(2 * g, 2 * g + 2 - g):
                        stats(pair)

            def attention_out(k):
                for tt in range(4):
                    dve.wait_ge(S["wo_psum"], 4 * k + tt + 1)
                    x2 = X[:, 2 * tt:2 * tt + 2, :]
                    v.tensor_tensor(x2, PS[:, 4 + tt, :].rearrange("p (t d) -> p t d", t=2), x2, ALU.add)\
                        .then_inc(S["res_done"], 1)
                    if tt:
                        dve.wait_ge(S["res_done"], 4 * k + tt)
                        stats(tt - 1)
                dve.wait_ge(S["res_done"], 4 * k + 4)

            def attn0():
                layer_norm(1)
                dve.wait_ge(S["const_in"], 16 * 8)
                for s in range(T + 3):
                    if s < T:
                        r, i = s % 2, s % TB
                        dve.wait_ge(S["a0_proj"], s + 1)
                        if s >= 2:
                            dve.wait_ge(S["a0_sum"], s - 1)
                        qk = PS[:, 4 + 2 * r, :].rearrange("p (h x e) -> p h x e", x=2, e=HD // 2)
                        t2 = RT2[r].rearrange("p (h x e) -> p h x e", x=2, e=HD // 2)
                        v.tensor_tensor(RT1[r].rearrange("p (h e) -> p h e", e=HD),
                                        PS[:, 4 + 2 * r, :].rearrange("p (h e) -> p h e", e=HD),
                                        bc(rope_c[:, i, :], [P, 32, HD], 1), ALU.mult)
                        for x in range(2):
                            last = v.tensor_tensor(t2[:, :, x, :], qk[:, :, 1 - x, :],
                                                   bc(rope_s[:, i, x * 8:x * 8 + 8], [P, 32, 8], 1), ALU.mult)
                        last.then_inc(S["a0_rope"], 1)
                    t = s - 1
                    if 0 <= t < T:
                        r = t % 2
                        dve.wait_ge(S["a0_sum"], t + 1)
                        if t >= 2:
                            dve.wait_ge(S["a0_center"], t - 1)
                        ch.link(v.tensor_reduce(hs1[:, r, :], Y4[t % 4].rearrange("p (h e) -> p h e", e=HD), AX_X, ALU.add))
                        v.tensor_scalar(hs2[:, r, :], hs1[:, r, :], 1.0 / HD, None, ALU.mult).then_inc(S["a0_mean"], 1)
                    t = s - 2
                    if 0 <= t < T:
                        r = t % 2
                        dve.wait_ge(S["a0_square"], t + 1)
                        ch.link(v.tensor_reduce(hs3[:, r, :], SQ[r].rearrange("p (h e) -> p h e", e=HD), AX_X, ALU.add))
                        ch.link(v.tensor_scalar(hs3[:, r, :], hs3[:, r, :], 1.0 / HD, EPS, ALU.mult, ALU.add))
                        v.reciprocal(hs3[:, r, :], hs3[:, r, :]).then_inc(S["a0_var"], 1)
                    t = s - 3
                    if 0 <= t < T:
                        rest(t, t % 2, FULL[t % 2].rearrange("p (x t) -> p x t", x=4),
                             PT[t // TB][0][:, :, (t % TB) * P:(t % TB + 1) * P], 4)
                    t = s - 2
                    if 0 <= t < T:
                        y = Y4[t % 4].rearrange("p (h e) -> p h e", e=HD)
                        dve.wait_ge(S["a0_rstd"], t + 1)
                        v.tensor_tensor(y, y, bc(hs4[:, t % 2, :], [P, 32, HD], 2), ALU.mult).then_inc(S["a0_norm"], 1)

                def powers(u, j):
                    dve.wait_ge(S["u0_square"], 8 * u + 2 * j + 2)
                    if j < TB - 1:
                        e = EJ[j][:, :, P:N - j * P]
                        v.tensor_tensor(e, e, e, ALU.mult)
                    dve.wait_ge(S["u0_masked"], 4 * u + j + 1)
                    e = EJ[j][:, :, 0:P]
                    v.tensor_tensor(e, e, e, ALU.mult).then_inc(S["u0_e"], 1)

                def rows(u, b, g):
                    dve.wait_ge(S["u0_ot"], u + 1)
                    ot = PS[:, 6 + b, :].rearrange("p (i m e) -> p i m e", i=TB, m=MU)
                    v.reciprocal(rec[:, b, :, :], ot[:, :, :, HD]).then_inc(S["u0_rec"], 1)
                    dve.wait_ge(S["u0_rec"], u + 1)
                    v.tensor_tensor(XN[:, TB * b:TB * b + TB, bass.ds(g * (MU * HD), MU * HD)]
                                    .rearrange("p i (m e) -> p i m e", m=MU), ot[:, :, :, 0:HD],
                                    bc(rec[:, b, :, :], [P, TB, MU, HD], 3), ALU.mult).then_inc(S["u0_rows"], 1)

                def unit(g, b, first=False):
                    for j in range(TB):
                        powers(2 * g + b, j)
                    if not (first and b == 0):
                        rows(2 * g + b - 1, 1 - b, g if b else g - 1)
                unit(0, 0, True)
                unit(0, 1, True)
                with dve.Fori(1, 4) as g:
                    for b in range(B):
                        unit(g, b)
                rows(7, 1, 3)
                attention_out(0)

            def rest(q, r, full, high, n):
                dve.wait_ge(S["sp_high"], q + 1)
                if q >= 2:
                    dve.wait_ge(S["sp_parts"], q - 1)
                v.tensor_tensor(R1[r].rearrange("p (x t) -> p x t", x=n), full, high, ALU.subtract)\
                    .then_inc(S["sp_rest"], 1)

            def route(n):
                layer_norm(3 + 2 * n)
                probs = pe_[:, :, 0:NE]
                dve.wait_ge(S["g_logits"], n + 1)
                ch.link(v.tensor_reduce(m8[:, :], LOG, AX_X, ALU.max))
                v.tensor_tensor(probs, LOG, bc(m8[:, :], [P, T, NE], 2), ALU.subtract).then_inc(S["g_shift"], 1)
                dve.wait_ge(S["g_exp"], n + 1)
                for t in range(T):
                    v.max(out=v8[:, t, :], in_=pe_[:, t, 0:NE])
                ch.link(v.tensor_reduce(rs8[:, :], probs, AX_X, ALU.add))
                v.reciprocal(rs8[:, :], rs8[:, :])
                ch.link(v.tensor_copy(rep8[:, :, 0:TOPK], v8[:, :, 0:TOPK]))
                for t in range(T):
                    last = v.match_replace(rpe[:, t, :], rep8[:, t, :], pe_[:, t, :], 2.0)
                ch.link(last)
                v.tensor_scalar(mkb[:, :, :], rpe[:, :, 0:NE], 1.5, None, ALU.is_gt).then_inc(S["g_mask"], 1)
                v.tensor_scalar(mk[:, :, :], rpe[:, :, 0:NE], 1.5, None, ALU.is_gt)
                ch.link(v.tensor_tensor(wt[:, :, :], probs, bc(rs8[:, :], [P, T, NE], 2), ALU.mult))

            def place(n):
                dve.wait_ge(S["g_pos"], n + 1)
                ch.link(v.scalar_tensor_tensor(mk[:, :, :], POS, float(CAP), mk[:, :, :], ALU.is_lt, ALU.mult))
                v.tensor_tensor(rpe[:, :, 0:NE], POS, bc(slot0[:, :], [P, T, NE], 1), ALU.add)
                ch.link(v.tensor_tensor(wt[:, :, :], wt[:, :, :], mk[:, :, :], ALU.mult))
                ch.link(v.tensor_tensor(mk[:, :, :], rpe[:, :, 0:NE], mk[:, :, :], ALU.mult))
                for t in range(T):
                    last = v.max(out=s8[:, t, :], in_=mk[:, t, :])
                ch.link(last)
                ch.link(v.tensor_scalar(s8z[:, :, :], s8[:, :, :], 0.0, SKIP, ALU.is_equal, ALU.mult))
                if n:
                    dve.wait_ge(S["g_scatter0"], 4 * TOPK * 16)
                    dve.wait_ge(S["g_scatter1"], 4 * TOPK * 16)
                ch.link(v.scalar_tensor_tensor(idx[:, :, :], s8[:, :, :], -1.0, s8z[:, :, :], ALU.add, ALU.add))

            def weights(n, t):
                src = SRC[t % 2]
                if t >= 2:
                    dve.wait_ge(S[f"g_scatter{t % 2}"], (n * 4 + t // 2) * TOPK * 16)
                v.tensor_copy(src[:, :, D + 1:D + 2], bc(tok[:, t:t + 1], [P, TOPK, 1], 1))
                for k in range(TOPK):
                    last = v.scalar_tensor_tensor(junk[:, k, :], mk[:, t, :], s8[:, t, k:k + 1], wt[:, t, :],
                                                  ALU.is_equal, ALU.mult, accum_out=src[:, k, D:D + 1])
                last.then_inc(S["g_weight"], 1)
                dve.wait_ge(S["g_weight"], n * T + t + 1)

            def shared(n):
                def gate(t):
                    q = n * T + t
                    dve.wait_ge(S["s_silu"], q + 1)
                    if t >= 2:
                        dve.wait_ge(S["s_gt_psum"], q - 1)
                    v.tensor_tensor(GSH[t % 2], HSH[t % 2], PS[:, 2 + t % 2, 0:SI], ALU.mult).then_inc(S["s_g"], 1)

                def add(t):
                    dve.wait_ge(S["s_out"], n * T + t + 1)
                    v.scalar_tensor_tensor(X[:, t, :], PS[:, 7, 0:D], 0.5, X[:, t, :], ALU.mult, ALU.add)\
                        .then_inc(S["s_y"], 1)
                gate(0)
                place(n)
                weights(n, 0)
                gate(1)
                weights(n, 1)
                for t in range(T):
                    add(t)
                    if t + 2 < T:
                        gate(t + 2)
                        weights(n, t + 2)

            def experts(n):
                def turned(e, k, fresh=False):
                    dve.wait_ge(S["e_xbt_psum"], NE * n + e + 1)
                    if not fresh:
                        dve.wait_ge(S["e_h"], 2 * (NE * n + e) - 2)
                    v.tensor_copy(XBT[k % 2], PS[:, k % 2, :].rearrange("p (c s) -> p c s", c=C)).then_inc(S["e_xbt"], 1)

                def step(e, k, h, first=False, last=False):
                    dve.wait_ge(S[f"e_xb{k}"], 16 * (NE // NB) * n + 16 * (h + 1))
                    if not first:
                        dve.wait_ge(S["y_added"], 32 * (NE * n + e) - 32 * (NB - 1))
                        dve.wait_ge(S["e_ob"], NE * n + e - NB + 1)
                    v.tensor_scalar(meta_w[:, k, :], XB[k][:, :, D], 0.5, None, ALU.mult)
                    v.tensor_copy(meta_i[:, k, :], XB[k][:, :, D + 1]).then_inc(S["e_meta"], 1)
                    for s in range(2):
                        dve.wait_ge(S["e_silu"], 2 * (NE * n + e) + s + 1)
                        if not (first and k < 2):
                            dve.wait_ge(S["e_gt_psum"], NE * n + e - 1)
                        v.tensor_tensor(GE[k % 2][s], HE[k % 2][s], PS[:, 2 + 2 * (k % 2) + s, INTER:2 * INTER], ALU.mult)\
                            .then_inc(S["e_g"], 1)
                    if not (last and k == NB - 1):
                        turned(e + 1, k + 1, first and k == 0)
                turned(0, 0, True)
                for k in range(NB):
                    step(k, k, 0, first=True)
                with dve.Fori(1, NE // NB - 1) as h:
                    for k in range(NB):
                        step(NB * h + k, k, h)
                for k in range(NB):
                    step(NE - NB + k, k, NE // NB - 1, last=True)

            def attn1():
                layer_norm(4, 2)
                dve.wait_ge(S["lam_in"], 80)
                ch.link(v.tensor_tensor(lam[:, :], lamv[:, 0, :], lamv[:, 1, :], ALU.mult))
                ch.link(v.tensor_reduce(m4[:, 0:1], lam[:, :], AX_X, ALU.add))
                ch.link(v.tensor_tensor(lam[:, :], lamv[:, 2, :], lamv[:, 3, :], ALU.mult))
                v.tensor_reduce(m4[:, 1:2], lam[:, :], AX_X, ALU.add).then_inc(S["lam_sum"], 1)
                dve.wait_ge(S["lam_exp"], 1)
                ch.link(v.scalar_tensor_tensor(lam[:, 0:1], lam[:, 2:3], -LAMBDA_INIT, lam[:, 1:2], ALU.add, ALU.subtract))
                ch.link(v.tensor_scalar(subw[:, :], subw[:, :], 1.0 - LAMBDA_INIT, None, ALU.mult))
                for r in range(8):
                    x = r % 4
                    rest(T + r, r % 2, PS[:, 4 + r % 2:5 + r % 2, :], PT[r // 4][0][:, x:x + 1, :], 1)

                def maximum(w, slot, x, fresh=False):
                    if x == 0 and not fresh:
                        dve.wait_ge(S["u1_split"], w - 1)
                    dve.wait_ge(S["u1_max"], 16 * w + x + 1)
                    v.tensor_reduce(nm[:, slot % 2, x // MU, x % MU:x % MU + 1], PS[:, 3 + RING[16 * slot + x], :],
                                    AX_X, ALU.max, negate=True).then_inc(S["u1_maxed"], 1)

                def squares(b, g0, g1):
                    t0, t1, h0, h1 = TB * b, TB * b + TB, 2 * g0, 2 * g1
                    x = XN[:, t0:t1, h0 * HD:h1 * HD]
                    size = TB * (h1 - h0) * HD
                    a, b_ = (stack_mem[:, o:o + size].rearrange("p (t d) -> p t d", t=TB) for o in (512, 1536))
                    ch.link(v.tensor_scalar(a, x, 4e18, -4e18, ALU.min, ALU.max))
                    v.tensor_tensor(a, a, a, ALU.mult)
                    ch.link(v.tensor_scalar(b_, x, 2.0 ** -40, 1e18, ALU.mult, ALU.min))
                    ch.link(v.tensor_scalar(b_, b_, -1e18, None, ALU.max))
                    ch.link(v.tensor_tensor(b_, b_, b_, ALU.mult))
                    for k, sq in enumerate((a, b_)):
                        last = v.tensor_reduce(rms[:, k, :].rearrange("p (t h) -> p t h", t=T)[:, t0:t1, h0:h1],
                                               sq.rearrange("p t (h e) -> p t h e", e=HD), AX_X, ALU.add)
                    ch.link(last)

                def rows(u, b, g):
                    dve.wait_ge(S["u1_ot"], u + 1)
                    ot = PS[:, 7, :].rearrange("p (i m e) -> p i m e", i=TB, m=MU)
                    v.reciprocal(rec[:, b, :, :], ot[:, :, :, HD]).then_inc(S["u1_rec"], 1)
                    dve.wait_ge(S["u1_rec"], u + 1)
                    v.tensor_tensor(amap[:, :, :, :], ot[:, :, :, 0:HD], bc(rec[:, b, :, :], [P, TB, MU, HD], 3), ALU.mult)\
                        .then_inc(S["u1_rows"], 1)
                    dve.wait_ge(S["u1_rows"], u + 1)
                    two = amap[:, :, :, :].rearrange("p i (h x) e -> p i h x e", x=2)
                    v.scalar_tensor_tensor(XN[:, TB * b:TB * b + TB, bass.ds(g * 32, 32)]
                                           .rearrange("p i (h e) -> p i h e", h=2),
                                           two[:, :, :, 1, :], lam[:, 0:1], two[:, :, :, 0, :], ALU.mult, ALU.add)\
                        .then_inc(S["u1_diff"], 1)

                def unit(i4, u4, first=False, last=False):
                    u = 4 * i4 + u4
                    for j in range(TB):
                        if not (last and u4 > 1):
                            for k in range(4):
                                maximum(u + 2, (u4 + 2) % 4, 4 * j + k)
                        if j == 2 and not (first and u4 == 0):
                            rows(u - 1, (u4 + 1) % 2, 2 * i4 + (u4 - 1) // 2)
                            if last and u4 > 1:
                                dve.wait_ge(S["u1_diff"], u)
                                squares(*((1, 0, 7) if u4 == 2 else (0, 0, 8)))
                for x in range(16):
                    maximum(0, 0, x, True)
                for x in range(16):
                    maximum(1, 1, x, True)
                for u4 in range(4):
                    unit(0, u4, first=True)
                with dve.Fori(1, 3) as i4:
                    for u4 in range(4):
                        unit(i4, u4)
                for u4 in range(4):
                    unit(3, u4, last=True)
                rows(15, 1, 7)
                dve.wait_ge(S["u1_diff"], 16)
                squares(1, 7, 8)
                flat = XN[:, :, :].rearrange("p t d -> p (t d)")
                v.tensor_scalar(rms[:, 2, :], rms[:, 1, :], 3.4028235e38 * 2.0 ** -80, None, ALU.is_le)
                v.tensor_scalar(rms[:, 0, :], rms[:, 0, :], 1.0 / HD, EPS, ALU.mult, ALU.add)
                ch.link(v.tensor_scalar(rms[:, 1, :], rms[:, 1, :], 1.0 / HD, 1e-30, ALU.mult, ALU.add))
                v.reciprocal(rms[:, 0:2, :], rms[:, 0:2, :]).then_inc(S["rms_var"], 1)
                dve.wait_ge(S["rms_rstd"], 1)
                ch.link(v.scalar_tensor_tensor(rms[:, 3, :], rms[:, 1, :], 2.0 ** -40, rms[:, 0, :], ALU.mult, ALU.min))
                ch.link(v.tensor_tensor(rms[:, 3, :], rms[:, 3, :], rms[:, 2, :], ALU.mult))
                x3 = flat.rearrange("p (h e) -> p h e", e=HD)
                for q in range(4):
                    h = slice(32 * q, 32 * q + 32)
                    v.tensor_tensor(x3[:, h, :], x3[:, h, :], bc(rms[:, 3, h], [P, 32, HD], 2), ALU.mult)\
                        .then_inc(S["att_ready"], 1)
                attention_out(1)

            ffn(0)
            attn0()
            ffn(1)
            route(0)
            shared(0)
            experts(0)
            attn1()
            route(1)
            shared(1)
            experts(1)

        @block.scalar
        def _(act):
            act_fn = nc.scalar.activation

            def evacuate_xt(turn, scale=1.0):
                for tt in range(4):
                    act.wait_ge(S["xt_psum"], 4 * turn + tt + 1)
                    act_fn(XT[:, :, tt * 256:(tt + 1) * 256], PS[:, tt, :].rearrange("p (c t) -> p c t", c=C), ACT.Copy,
                           scale=scale).then_inc(S["xt_ready"], 1)

            def layer_norm(n):
                act.wait_ge(S["ln_var"], n + 1)
                act_fn(rstd[:, :], rv[:, :], ACT.Sqrt).then_inc(S["ln_rstd"], 1)
                evacuate_xt(LN_TURN[n])

            def ffn(n):
                layer_norm(2 * n)
                for g in range(2):
                    q = 2 * n + g
                    act.wait_ge(S["ff_shift"], q + 1)
                    act_fn(ep[:, :, 0:LE], el[:, :, :], ACT.Exp).then_inc(S["ff_exp"], 1)
                    act.wait_ge(S["ff_zt_psum"], q + 1)
                    act_fn(ZS, PS[:, 0, :], ACT.Copy).then_inc(S["ff_zt"], 1)

            def split_high(q, dst, full):
                act_fn(dst, full, ACT.Copy).then_inc(S["sp_high"], 1)

            def split_mid(q, r, dst, n):
                act.wait_ge(S["sp_rest"], q + 1)
                act_fn(dst, R1[r].rearrange("p (x t) -> p x t", x=n), ACT.Copy).then_inc(S["sp_mid"], 1)

            def attn0():
                layer_norm(1)
                act.wait_ge(S["attn0_in"], 48)
                for s in range(T + 4):
                    if s < T:
                        act.wait_ge(S["a0_proj"], s + 1)
                        act_fn(V[:, s, :], PS[:, 5 + 2 * (s % 2), 0:D], ACT.Copy).then_inc(S["a0_v"], 1)
                    t = s - 3
                    if 0 <= t < T:
                        act.wait_ge(S["sp_psum"], t + 1)
                        if t >= 2:
                            act.wait_ge(S["sp_rest"], t - 1)
                        act_fn(FULL[t % 2], PS[:, t % 2, :], ACT.Identity, bias=lnsb[:, 1:2], scale=lnsb[:, 0:1])\
                            .then_inc(S["a0_full"], 1)
                        act.wait_ge(S["a0_full"], t + 1)
                        split_high(t, PT[t // TB][0][:, :, (t % TB) * P:(t % TB + 1) * P],
                                   FULL[t % 2].rearrange("p (x t) -> p x t", x=4))
                    t = s - 1
                    if 0 <= t < T:
                        act.wait_ge(S["a0_center"], t + 1)
                        if t >= 2:
                            act.wait_ge(S["a0_var"], t - 1)
                        act_fn(SQ[t % 2], Y4[t % 4], ACT.Square).then_inc(S["a0_square"], 1)
                    t = s - 2
                    if 0 <= t < T:
                        act.wait_ge(S["a0_var"], t + 1)
                        if t >= 2:
                            act.wait_ge(S["a0_norm"], t - 1)
                        act_fn(hs4[:, t % 2, :], hs3[:, t % 2, :], ACT.Sqrt).then_inc(S["a0_rstd"], 1)
                    t = s - 4
                    if 0 <= t < T:
                        split_mid(t, t % 2, PT[t // TB][1][:, :, (t % TB) * P:(t % TB + 1) * P], 4)

                def output(u, b, fresh):
                    act.wait_ge(S["u0_av"], 4 * u + 4)
                    if not fresh:
                        act.wait_ge(S["u0_ot"], u - 1)
                    act_fn(OS[:, b, :], PS[:, 4 + b, :], ACT.Copy).then_inc(S["u0_os"], 1)

                def unit(g, b, first=False):
                    u = 2 * g + b
                    for j in range(TB):
                        if first and b == 0 and j == 1:
                            act.wait_ge(S["sp_parts"], T)
                        if first and b == 0 and j == 3:
                            act.wait_ge(S["sp_stored1"], STORED)
                        for hp in range(2):
                            act.wait_ge(S["u0_scores"], 8 * u + 2 * j + hp + 1)
                            if not (first and b == 0):
                                act.wait_ge(S["u0_av"], 4 * u + j - 3)
                            act_fn(EJ[j][:, 2 * hp:2 * hp + 2, 0:N - j * P], PS[:, 2 * hp:2 * hp + 2, 0:N - j * P],
                                   ACT.Square).then_inc(S["u0_square"], 1)
                        if j == 2 and not (first and b == 0):
                            output(u - 1, 1 - b, first)
                unit(0, 0, True)
                unit(0, 1, True)
                with act.Fori(1, 4) as g:
                    for b in range(B):
                        unit(g, b)
                output(7, 1, False)
                evacuate_xt(2)

            def route(n):
                layer_norm(3 + 2 * n)
                act.wait_ge(S["g_shift"], n + 1)
                act_fn(pe_[:, :, 0:NE], pe_[:, :, 0:NE], ACT.Exp).then_inc(S["g_exp"], 1)

            def shared(n):
                def copy_rows(t):
                    if t >= 2:
                        act.wait_ge(S[f"g_scatter{t % 2}"], (n * 4 + t // 2) * TOPK * 16)
                    act_fn(SRC[t % 2][:, :, 0:D], bc(XN[:, t, :], [P, TOPK, D], 1), ACT.Copy).then_inc(S["g_copy"], 1)

                def silu(t):
                    q = n * T + t
                    act.wait_ge(S["s_h"], q + 1)
                    if t >= 2:
                        act.wait_ge(S["s_g"], q - 1)
                    act_fn(HSH[t % 2], PS[:, t % 2, 0:SI], ACT.Silu).then_inc(S["s_silu"], 1)
                silu(0)
                silu(1)
                copy_rows(0)
                copy_rows(1)
                for t in range(T):
                    q = n * T + t
                    act.wait_ge(S["s_gt_psum"], q + 1)
                    if t:
                        act.wait_ge(S["s_out"], q)
                    act_fn(GTS[:, 0:2, :], PS[:, 6, 0:2 * P].rearrange("p (k t) -> p k t", k=2), ACT.Copy)
                    act_fn(GTS[0:SI - 2 * P, 2, :], PS[0:SI - 2 * P, 6, 2 * P:3 * P], ACT.Copy).then_inc(S["s_gt"], 1)
                    if t + 2 < T:
                        silu(t + 2)
                        copy_rows(t + 2)

            def experts(n):
                def turned_g(e, k, fresh):
                    act.wait_ge(S["e_gt_psum"], NE * n + e + 1)
                    if not fresh:
                        act.wait_ge(S["e_out"], NE * n + e - 1)
                    act_fn(GT[k % 2], PS[0:IH, 6, :].rearrange("p (i s) -> p i s", i=2), ACT.Copy).then_inc(S["e_gt"], 1)

                def weigh(e, k, fresh):
                    act.wait_ge(S["e_out"], NE * n + e + 1)
                    act.wait_ge(S["e_meta"], NE * n + e + 1)
                    if not fresh:
                        act.wait_ge(S["y_added"], 32 * (NE * n + e) - 32 * (NB - 1))
                    for s in range(2):
                        last = act_fn(OB[k][:, s, :], PS[:, 7, s * D:(s + 1) * D], ACT.Copy, scale=meta_w[:, k, s:s + 1])
                    last.then_inc(S["e_ob"], 1)

                def step(e, k, first=False):
                    before = k - 1 if k else NB - 1
                    for s in range(2):
                        act.wait_ge(S["e_h"], 2 * (NE * n + e) + s + 1)
                        if not (first and k < 2):
                            act.wait_ge(S["e_g"], 2 * (NE * n + e) + s - 3)
                        act_fn(HE[k % 2][s], PS[:, 2 + 2 * (k % 2) + s, 0:INTER], ACT.Silu).then_inc(S["e_silu"], 1)
                        if not (first and k == 0):
                            if s == 0:
                                turned_g(e - 1, before, first and k < 3)
                            else:
                                weigh(e - 1, before, first)
                for k in range(NB):
                    step(k, k, True)
                with act.Fori(1, NE // NB) as h:
                    for k in range(NB):
                        step(NB * h + k, k)
                turned_g(NE - 1, NB - 1, False)
                weigh(NE - 1, NB - 1, False)

            def attn1():
                layer_norm(4)
                act.wait_ge(S["lam_sum"], 1)
                act_fn(lam[:, 1:3], m4[:, 0:2], ACT.Exp).then_inc(S["lam_exp"], 1)
                for r in range(9):
                    if r < 8:
                        act.wait_ge(S["sp_psum"], T + r + 1)
                        split_high(T + r, PT[r // 4][0][:, r % 4:r % 4 + 1, :], PS[:, 4 + r % 2:5 + r % 2, :])
                    if r:
                        split_mid(T + r - 1, (r - 1) % 2, PT[(r - 1) // 4][1][:, (r - 1) % 4:(r - 1) % 4 + 1, :], 1)
                for t in range(T):
                    act.wait_ge(S["a1_v_psum"], t + 1)
                    act_fn(V[:, t, :], PS[:, 6 + t % 2, 0:D], ACT.Copy).then_inc(S["a1_v"], 1)

                def max_rows(w, first=False):
                    act.wait_ge(S["u1_mt"], w + 1)
                    if not first:
                        act.wait_ge(S["u1_mrow"], 16 * w)
                    act_fn(mr[:, :], MT, ACT.Copy).then_inc(S["u1_mr"], 1)

                def output(u, b, fresh=False):
                    act.wait_ge(S["u1_av"], 4 * u + 4)
                    if not fresh:
                        act.wait_ge(S["u1_ot"], u - 1)
                    act_fn(OS[:, b, :], PS[:, 6, :], ACT.Copy).then_inc(S["u1_os"], 1)

                def unit(i4, u4, first=False, last=False):
                    u = 4 * i4 + u4
                    for j in range(TB):
                        if not (first and u4 == 0 and j < 2):
                            act.wait_ge(S["u1_av"], 4 * u + j - 1)
                        for m in range(MU):
                            act.wait_ge(S["u1_scores"], 16 * u + 4 * j + m + 1)
                            act_fn(E[j % 2][:, m, :], PS[:, RING[16 * u4 + 4 * j + m], :], ACT.Exp, scale=SCALE1)\
                                .then_inc(S["u1_exp"], 1)
                            if j == 1 and m == 1 and not (last and u4 == 3):
                                max_rows(u + 1)
                        if j == 0 and not (first and u4 == 0):
                            output(u - 1, (u4 + 1) % 2, first and u4 <= 2)
                max_rows(0, True)
                for u4 in range(4):
                    unit(0, u4, first=True)
                with act.Fori(1, 3) as i4:
                    for u4 in range(4):
                        unit(i4, u4)
                for u4 in range(4):
                    unit(3, u4, last=True)
                output(15, 1)
                act.wait_ge(S["rms_var"], 1)
                act_fn(rms[:, 0:2, :], rms[:, 0:2, :], ACT.Sqrt).then_inc(S["rms_rstd"], 1)
                evacuate_xt(6, subw[:, 0:1])

            ffn(0)
            attn0()
            ffn(1)
            route(0)
            shared(0)
            experts(0)
            attn1()
            route(1)
            shared(1)
            experts(1)

        @block.gpsimd
        def _(pool):
            ch = Chain(pool, S["pool_self"])
            p = nc.gpsimd
            p.memset(ep[:, :, LE:LPAD], -1.0)
            p.memset(rep[:, :, 2:8], -1.0)
            p.memset(pe_[:, :, NE:EPAD], -1.0)
            p.memset(rep8[:, :, TOPK:8], -1.0)
            ch.link(p.memset(VA[:, :, :, :, :], 0.0))
            pool.wait_ge(S["const_in"], 16 * 8)
            p.tensor_copy(identb[:, :], ident[:, :])
            p.tensor_copy(tri[:, :], trif[:, :])
            p.memset(ones[:, :], 1.0)
            p.memset(one[:, :], 1.0)
            p.memset(VA[:, :, :, :, HD:HD + 1], 1.0).then_inc(S["pool_const"], 4)

            def split_low(q, r, mid, low, n):
                pool.wait_ge(S["sp_mid"], q + 1)
                p.tensor_tensor(low, R1[r].rearrange("p (x t) -> p x t", x=n), mid, ALU.subtract).then_inc(S["sp_parts"], 1)

            def attn0():
                for s in range(T + 4):
                    if s < T:
                        r = s % 2
                        pool.wait_ge(S["a0_rope"], s + 1)
                        if s >= 4:
                            pool.wait_ge(S["sp_psum"], s - 3)
                        p.tensor_tensor(Y4[s % 4], RT1[r], RT2[r], ALU.add).then_inc(S["a0_sum"], 1)
                    t = s - 1
                    if 0 <= t < T:
                        y = Y4[t % 4].rearrange("p (h e) -> p h e", e=HD)
                        pool.wait_ge(S["a0_mean"], t + 1)
                        p.tensor_tensor(y, y, bc(hs2[:, t % 2, :], [P, 32, HD], 2), ALU.subtract).then_inc(S["a0_center"], 1)
                    t = s - 4
                    if 0 <= t < T:
                        cols = slice((t % TB) * P, (t % TB + 1) * P)
                        split_low(t, t % 2, PT[t // TB][1][:, :, cols], PT[t // TB][2][:, :, cols], 4)
                pool.wait_ge(S["a0_v"], T)

                def unit(g, b, first=False):
                    u = 2 * g + b
                    if not first:
                        pool.wait_ge(S["u0_av"], 4 * u - 4)
                    src = V[:, TB * b:TB * b + TB, bass.ds(g * (MU * HD), MU * HD)].rearrange("p i (m e) -> p i m e", m=MU)
                    p.tensor_tensor(VA[:, b, :, :, 0:HD], src, one[:, :].unsqueeze(2).unsqueeze(3)
                                    .broadcast_to([P, TB, MU, HD]), ALU.mult).then_inc(S["u0_va"], 1)
                    for j in range(TB):
                        pool.wait_ge(S["u0_square"], 8 * u + 2 * j + 2)
                        diag = EJ[j][:, :, 0:P]
                        p.tensor_tensor(diag, diag, bc(mask[:, :], [P, MU, P], 1), ALU.mult).then_inc(S["u0_masked"], 1)
                unit(0, 0, True)
                unit(0, 1, True)
                with pool.Fori(1, 4) as g:
                    for b in range(B):
                        unit(g, b)

            def dispatch(n):
                pool.wait_ge(S["init_rows"], 96)
                for t in range(T):
                    pool.wait_ge(S["g_weight"], n * T + t + 1)
                    pool.wait_ge(S["g_copy"], n * T + t + 1)
                    for k in range(TOPK):
                        p.indirect_dma_start(xbuf[n], bass.IndirectOffsetOnAxis(ap=idx[:, t, k:k + 1], axis=0),
                                             SRC[t % 2][:, k, :], None, bounds_check=SLOTS - 1, oob_is_err=False)\
                            .then_inc(S[f"g_scatter{t % 2}"], 16)

            def experts(n):
                def add(e, k, first=False):
                    if not (first and n == 0):
                        pool.wait_ge(S["pool_turn"], NE * n + e)
                    pool.wait_ge(S["e_ob"], NE * n + e + 1)
                    if not first:
                        pool.wait_ge(S["y_added"], 32 * (NE * n + e))
                    p.tensor_tensor(turn[:, :], one[:, :], one[:, :], ALU.mult).then_inc(S["pool_turn"], 1)
                    for s in range(2):
                        p.indirect_dma_start(y_dram[n], bass.IndirectOffsetOnAxis(ap=meta_i[:, k, s:s + 1], axis=0),
                                             OB[k][:, s, :], None, bounds_check=B * N + 2 * P - 1, oob_is_err=True,
                                             compute_op=ALU.add).then_inc(S["y_added"], 16)
                pool.wait_ge(S["y_stored"], 16 * T * (n + 1))
                for k in range(NB):
                    add(k, k, k == 0)
                with pool.Fori(1, NE // NB) as h:
                    for k in range(NB):
                        add(NB * h + k, k)

            def attn1():
                for r in range(8):
                    x = r % 4
                    split_low(T + r, r % 2, PT[r // 4][1][:, x:x + 1, :], PT[r // 4][2][:, x:x + 1, :], 1)
                pool.wait_ge(S["sp_parts"], 2 * T)
                for r in range(4):
                    if r == 2:
                        pool.wait_ge(S["sp_stored0"], 2 * STORED)
                    last = p.memset(KS[r][64:96, :, :], 1.0)
                last.then_inc(S["stack_pad"], 1)
                pool.wait_ge(S["stack_pad"], 1)

                def stage_v(u, b, g, fresh):
                    if not fresh:
                        pool.wait_ge(S["u1_av"], 4 * u - 4)
                    src = V[:, TB * b:TB * b + TB, bass.ds(g * 32, 32)].rearrange("p i (m e) -> p i m e", m=2)
                    p.tensor_tensor(VA[:, b, :, 0:2, 0:HD], src, one[:, :].unsqueeze(2).unsqueeze(3).broadcast_to([P, TB, 2, HD]), ALU.mult).then_inc(S["u1_va"], 1)

                def split_maxima(w, par, first=False):
                    pool.wait_ge(S["u1_maxed"], 16 * w + 16)
                    if not first:
                        pool.wait_ge(S["u1_mt"], w)
                    neg = nm[:, par, :, :]
                    p.tensor_tensor(mp[:, :, 0, :], neg, bc(one[:, :], [P, TB, MU], 2), ALU.mult).then_inc(S["u1_sp"], 1)
                    pool.wait_ge(S["u1_sp"], 3 * w + 1)
                    p.tensor_tensor(nmr[:, :, :], neg, mp[:, :, 0, :], ALU.subtract).then_inc(S["u1_sp"], 1)
                    pool.wait_ge(S["u1_sp"], 3 * w + 2)
                    p.tensor_tensor(mp[:, :, 1, :], nmr[:, :, :], bc(one[:, :], [P, TB, MU], 2), ALU.mult).then_inc(S["u1_sp"], 1)
                    pool.wait_ge(S["u1_sp"], 3 * w + 3)
                    p.tensor_tensor(mp[:, :, 2, :], nmr[:, :, :], mp[:, :, 1, :], ALU.subtract).then_inc(S["u1_split"], 1)

                def unit(i4, u4, first=False, last=False):
                    if last and u4 == 3:
                        return
                    u = 4 * i4 + u4
                    split_maxima(u + 1, (u4 + 1) % 2)
                    if not (first and u4 == 0):
                        stage_v(u + 1, (u4 + 1) % 2, 2 * i4 + (u4 + 1) // 2, False)
                pool.wait_ge(S["a1_v"], T)
                stage_v(0, 0, 0, True)
                stage_v(1, 1, 0, True)
                split_maxima(0, 0, True)
                for u4 in range(4):
                    unit(0, u4, first=True)
                with pool.Fori(1, 3) as i4:
                    for u4 in range(4):
                        unit(i4, u4)
                for u4 in range(4):
                    unit(3, u4, last=True)

            attn0()
            dispatch(0)
            experts(0)
            attn1()
            dispatch(1)
            experts(1)


def kernel(**inputs):
    import numpy as np
    import concourse.bacc as bacc
    from concourse.bass_utils import run_bass_kernel_spmd as run

    def rows(a):
        return np.ascontiguousarray(a.reshape(-1, 128, a.shape[-1]).transpose(1, 0, 2))

    i = {k: np.asarray(v) for k, v in inputs.items()}
    f = np.float32
    arrays = {"x": i["L0_attn_x"].reshape(B * N, D)}
    lora_a = i["L0_ffn_lora_A"].reshape(LE * RANK, D)
    arrays["wf"] = rows(np.concatenate([i["L0_ffn_weight"].T, lora_a.T, i["L0_ffn_router_w"].T], 1))
    arrays["lb"] = i["L0_ffn_lora_B"].transpose(0, 2, 1).reshape(LE * RANK, D)
    arrays["wa0"] = rows(np.concatenate([i["L0_attn_w_qkv"], i["L0_attn_w_out"]], 1))
    arrays["ln_scale"], arrays["ln_bias"] = i["L0_attn_ln_scale"], i["L0_attn_ln_bias"]
    arrays["wa1"] = rows(np.concatenate([i["L1_attn_Wq"].T, i["L1_attn_Wk"].T, i["L1_attn_Wv"].T, i["L1_attn_Wo"].T], 1))
    for short, name in (("lq1", "lambda_q1"), ("lk1", "lambda_k1"), ("lq2", "lambda_q2"), ("lk2", "lambda_k2"),
                        ("subln", "subln_weight")):
        arrays[short] = i["L1_attn_" + name]
    arrays["gw"] = rows(i["L1_ffn_gate_w"].T)
    w13 = np.concatenate([i["L1_ffn_w1"], i["L1_ffn_w3"]], 2)
    arrays["w13"] = w13.reshape(NE, C, P, 2 * INTER).transpose(2, 0, 1, 3).reshape(P, -1)
    arrays["w2"] = i["L1_ffn_w2"].reshape(NE, 2, IH, D).transpose(0, 2, 1, 3).reshape(NE * IH, 2 * D)
    arrays["sw13"] = rows(np.concatenate([i["L1_ffn_sw1"], i["L1_ffn_sw3"]], 1))
    arrays["sw2"] = rows(np.concatenate([i["L1_ffn_sw2"], np.zeros((3 * P - SI, D), f)], 0))
    arrays["ident"] = np.eye(P, dtype=f)
    arrays["mask"] = np.triu(np.ones((P, P), f))
    arrays["trif"] = np.triu(np.ones((P, P), f), 1)
    arrays["slot0"] = np.tile(np.arange(NE, dtype=f) * CAP + 1, (P, 1))
    arrays["tok"] = np.arange(B * N, dtype=f).reshape(T, P).T
    empty = np.zeros((P, 2, ROW), f)
    empty[:, :, D + 1] = B * N + np.arange(2 * P).reshape(2, P).T
    arrays["empty"] = empty
    inv = (f(1.0) / f(10000.0) ** (np.arange(0, HD, 2, dtype=f) / f(HD))).astype(f)
    angle = np.arange(N, dtype=f)[:, None] * inv[None, :]
    c, s = np.cos(angle), np.sin(angle)
    arrays["rope_c"] = rows(np.concatenate([c, c], 1))
    arrays["rope_s"] = rows(np.concatenate([-s, s], 1))
    arrays = {k: np.ascontiguousarray(v) for k, v in arrays.items()}

    nc = bacc.Bacc("TRN2", target_bir_lowering=False, num_devices=1)
    d = {k: nc.dram_tensor(k + "_dram", v.shape, F32, kind="ExternalInput").ap() for k, v in arrays.items()}
    out = nc.dram_tensor("out_dram", (B, N, D), F32, kind="ExternalOutput").ap()
    macaron_kernel(nc, d, out)
    r = run(nc, [{k + "_dram": v for k, v in arrays.items()}], core_ids=[0])
    return r.results[0]["out_dram"]
```

```python
from contextlib import ExitStack

import concourse.bass as bass
from concourse import mybir

F32 = mybir.dt.float32
BF16 = mybir.dt.bfloat16
U32 = mybir.dt.uint32
ALU = mybir.AluOpType
ACT = mybir.ActivationFunctionType
AX_X = mybir.AxisListType.X

P = 128
B, N, D = 2, 512, 256
T = B * N // P
TB = N // P
C = D // P
EPS = 1e-5
LE, RANK = 8, 16
FW = D + LE * RANK + LE
LPAD = 14
HD = 16
MU = 4
RUNS = [(0, 3, 0, 1), (3, 3, 0, 2), (6, 2, 0, 0)]
KPARTS = 5
LAMBDA_INIT = 0.8 - 0.6 * 2.718281828459045 ** (-0.3 * 12)
SCALE1 = 8.0 ** -0.5
NE, TOPK, CAP, INTER = 32, 6, 256, 176
IH = INTER // 2
EPAD = NE + 2
SI = 2 * INTER
ROW = D + 1 + NE
SLOTS = NE * CAP
NB = 4
SKIP = 65536.0


class Chain:

    def __init__(self, eng, sem):
        self.eng, self.sem, self.n = eng, sem, 0

    def link(self, ins):
        ins.then_inc(self.sem, 1)
        self.n += 1
        self.eng.wait_ge(self.sem, self.n)


def macaron_kernel(nc, d, out):
    ctx = ExitStack()
    with ctx:
        def sb(name, shape, dt=F32):
            return ctx.enter_context(nc.sbuf_tensor(name, shape, dt))

        def sem(name):
            return ctx.enter_context(nc.semaphore(name))

        parts = [nc.dram_tensor(f"parts{n}", [2, B, D // w, KPARTS, w, N], BF16, kind="Internal").ap()
                 for n, w in enumerate((HD, HD // 2))]
        xbuf = nc.dram_tensor("xbuf", [SLOTS, ROW], F32, kind="Internal").ap()
        y_dram = [nc.dram_tensor(f"y{n}", [B * N + 2 * P, D], F32, kind="Internal").ap() for n in range(2)]

        X = sb("X", [P, T, D])
        XN = sb("XN", [P, T, D])
        XT = sb("XT", [P, C, B * N])
        V = sb("V", [P, T, D])
        W13 = sb("W13", [P, NE * C * 2 * INTER])
        WF = sb("WF", [P, C, FW])
        LB = sb("LB", [P, D])
        WA = sb("WA", [P, C, 4 * D])
        SW13 = V[:, :, :].rearrange("p t d -> p (t d)")[:, 0:C * 2 * SI].rearrange("p (c n) -> p c n", c=C)
        SW2 = sb("SW2", [P, 3, D])
        GW = sb("GW", [P, C, NE])
        stack_mem = sb("stack_mem", [P, 8192])
        e_mem = sb("e_mem", [P, 4096])
        VA = sb("VA", [P, 2, TB, MU, 32])
        OS = sb("OS", [P, 2, N])
        ident = sb("ident", [P, P])
        trif = sb("trif", [P, P])
        identb = sb("identb", [P, P], BF16)
        mask = sb("mask", [P, P])
        tri = sb("tri", [P, P], BF16)
        ones = sb("ones", [P, P], BF16)
        slot0 = sb("slot0", [P, NE])
        tok = sb("tok", [P, T])
        empty = sb("empty", [P, 2, ROW])
        rope_c = sb("rope_c", [P, TB, HD])
        rope_s = sb("rope_s", [P, TB, HD])
        lnsb = sb("lnsb", [P, 2])
        subw = sb("subw", [P, 1])
        lamv = sb("lamv", [P, 4, 8])
        lam = sb("lam", [P, 8])
        st = sb("st", [P, T, 6])
        mv = sb("mv", [P, T, 2])
        rv = sb("rv", [P, T])
        rstd = sb("rstd", [P, T])
        m4 = sb("m4", [P, 4])
        el = sb("el", [P, 4, LE])
        ep = sb("ep", [P, 4, LPAD])
        v8 = sb("v8", [P, T, 8])
        rep = sb("rep", [P, 4, 8])
        rpl = sb("rpl", [P, 4, LPAD])
        g4 = sb("g4", [P, 4, LE])
        s4 = sb("s4", [P, 4])
        hs1 = sb("hs1", [P, 2, 32])
        hs2 = sb("hs2", [P, 2, 32])
        hs3 = sb("hs3", [P, 2, 32])
        hs4 = sb("hs4", [P, 2, 32])
        rec = sb("rec", [P, 2, TB, MU])
        amap = sb("amap", [P, TB, MU, HD])
        nm = sb("nm", [P, 2, TB, MU])
        nmr = sb("nmr", [P, TB, MU])
        one = sb("one", [P, 1])
        turn = sb("turn", [P, 1])
        mp = sb("mp", [P, TB, 3, MU], BF16)
        mr = sb("mr", [3 * MU, N], BF16)
        m8 = sb("m8", [P, T])
        rs8 = sb("rs8", [P, T])
        pe_ = sb("pe", [P, T, EPAD])
        rep8 = sb("rep8", [P, T, 8])
        mkb = sb("mkb", [P, T, NE], BF16)
        s8 = sb("s8", [P, T, 8])
        s8z = sb("s8z", [P, T, 8])
        idx = sb("idx", [P, T, 8], U32)
        meta_w = sb("meta_w", [P, NB, 2])
        meta_i = sb("meta_i", [P, NB, 2], U32)
        PS = ctx.enter_context(nc.psum_tensor("PS", [P, 8, 512], F32))

        KS = [stack_mem[:, 2048 * r:2048 * r + 1024].bitcast(BF16).rearrange("p (m t) -> p m t", m=MU) for r in range(4)]
        QS = [stack_mem[:, 2048 * r + 1024:2048 * r + 2048].bitcast(BF16).rearrange("p (m t) -> p m t", m=MU) for r in range(4)]
        E = [e_mem[:, 2048 * r:2048 * r + 2048].rearrange("p (m t) -> p m t", m=MU) for r in range(2)]
        Y4 = [stack_mem[:, 512 * r:512 * r + 512] for r in range(4)]
        SQ = [stack_mem[:, 2048 + 512 * r:2560 + 512 * r] for r in range(2)]
        R1 = [stack_mem[:, 3072 + 512 * r:3584 + 512 * r] for r in range(2)]
        xn_mem = XN[:, :, :].rearrange("p t d -> p (t d)")
        PT = [[[mem.bitcast(BF16).rearrange("p (x t) -> p x t", x=4) for mem in three] for three in two] for two in (
            [[W13[:, 1024 * (3 * b + c):1024 * (3 * b + c + 1)] for c in range(3)] for b in range(B)],
            [[stack_mem[:, 4096:5120], stack_mem[:, 5120:6144], stack_mem[:, 6144:7168]],
             [xn_mem[:, 0:1024], xn_mem[:, 1024:2048], e_mem[:, 2048:3072]]])]

        def qk_part(r):
            x, h = r % 2, r // 4
            return slice(2 * x + h, 2 * x + h + 1)

        FULL = [e_mem[:, 3072 + 512 * r:3584 + 512 * r] for r in range(2)]
        EJ = [mem.rearrange("p (m t) -> p m t", m=MU) for mem in
              (stack_mem[:, 0:2048], stack_mem[:, 2048:4096], e_mem[:, 0:2048], e_mem[:, 2048:4096])]
        RT1 = [e_mem[:, 512 * r:512 * r + 512] for r in range(2)]
        RT2 = [e_mem[:, 1024 + 512 * r:1536 + 512 * r] for r in range(2)]
        FF_BANK = (4, 0)
        ZS = [e_mem[:, 512 * g:512 * g + 512] for g in range(2)]
        ZF = [e_mem[:, 1024 + 512 * g:1536 + 512 * g] for g in range(2)]
        at = [0]

        def take(mem, n):
            at[0] += n
            return mem[:, at[0] - n:at[0]]

        SRC = take(stack_mem, T * ROW).rearrange("p (t r) -> p t r", t=T)
        at[0] = 0
        XB = [take(stack_mem, 2 * ROW).rearrange("p (s r) -> p s r", s=2) for _ in range(NB)]
        W2E = [take(stack_mem, 512)[0:IH, :].rearrange("p (i n) -> p i n", i=2) for _ in range(NB)]
        XBT = [take(stack_mem, 512).rearrange("p (c s) -> p c s", c=C) for _ in range(2)]
        OB = [take(stack_mem, 512).rearrange("p (s n) -> p s n", s=2) for _ in range(NB)]
        at[0] = 0
        HSH = [take(e_mem, SI) for _ in range(2)]
        GSH = [take(e_mem, SI) for _ in range(2)]
        GTS = take(e_mem, 3 * P).rearrange("p (k t) -> p k t", k=3)
        GT = [take(e_mem, 512)[0:IH, :].rearrange("p (i s) -> p i s", i=2) for _ in range(2)]
        rpe = take(e_mem, T * EPAD).rearrange("p (t e) -> p t e", t=T)
        mk = take(e_mem, T * NE).rearrange("p (t e) -> p t e", t=T)
        wt = take(e_mem, T * NE).rearrange("p (t e) -> p t e", t=T)
        at[0] = 0
        HE = [[take(e_mem, INTER) for _ in range(2)] for _ in range(2)]
        GE = [[take(e_mem, INTER) for _ in range(2)] for _ in range(2)]
        rms = stack_mem[:, 0:4 * P].rearrange("p (k h) -> p k h", k=4)
        LOG = [PS[:, 4 + h, 0:TB * NE].rearrange("p (t e) -> p t e", t=TB) for h in range(2)]
        POS = [PS[:, 6 + h, 0:TB * NE].rearrange("p (t e) -> p t e", t=TB) for h in range(2)]
        MT = PS[0:3 * MU, 7, 0:N // 2].bitcast(BF16)

        STORED = 16 * (3 + KPARTS)
        STACK = 16 * 2 * len(RUNS)

        RING = [(start + x) % 3 for start in (0, 1, 2, 1) for x in range(16)]
        LAST = [next(k for k in range(1, 8) if RING[y - k] == RING[y]) for y in range(64)]

        names = """ident_in x_in0 x_in1 x_in2 x_in3 ffw_in attn0_in attn1_in shared_in sw13_in w13_in const_in lam_in
        pool_const init_rows dve_self pool_self final_store
        ln_var ln_rstd xn_ready xt_psum xt_ready
        ff_psum ff_shift ff_exp ff_z ff_zt_psum ff_zt ff_out ff_done
        a0_proj a0_v a0_rope a0_sum a0_mean a0_center a0_square a0_var a0_rstd a0_norm a0_full
        sp_psum sp_high sp_rest sp_mid sp_parts sp_stored00 sp_stored01 sp_stored10 sp_stored11
        u0_scores u0_square u0_masked u0_e u0_av u0_os u0_ot u0_rec u0_rows u0_va
        att_ready wo_psum res_done
        a1_v_psum a1_v stack_pad lam_sum lam_exp rms_var rms_rstd
        u1_max u1_maxed u1_sp u1_split u1_mt u1_mr u1_mrow
        u1_scores u1_exp u1_av u1_os u1_ot u1_rec u1_rows u1_diff u1_va
        g_logits g_shift g_exp g_mask g_pos g_weight g_copy g_scatter0 g_scatter1
        s_h s_silu s_g s_gt_psum s_gt s_out s_y y_stored
        e_xb0 e_xb1 e_xb2 e_xb3 e_w20 e_w21 e_w22 e_w23 e_meta e_xbt_psum e_xbt
        e_h e_silu e_g e_gt_psum e_gt e_out e_ob pool_turn y_added""".split()
        S = {n: sem(n) for n in names}
        stk = [sem(f"stack_in{r}") for r in range(4)]

        block = ctx.enter_context(nc.Block())

        def bc(ap, shape, dim):
            return ap.unsqueeze(dim).broadcast_to(shape)

        LN_TURN = [0, 1, 3, 4, 5, 7]

        @block.sync
        def _(sp):
            def load_x(src):
                for q in range(4):
                    sp.dma_start(X[:, 2 * q:2 * q + 2, :], src[2 * P * q:2 * P * (q + 1), :].rearrange("(t p) d -> p t d", p=P))\
                        .then_inc(S[f"x_in{q}"], 16)

            load_x(d["x"])
            sp.dma_start(ident[:, :], d["ident"]).then_inc(S["ident_in"], 16)
            sp.dma_start(WF[:, :, :], d["wf"]).then_inc(S["ffw_in"], 16)
            sp.dma_start(LB[:, :], d["lb"]).then_inc(S["ffw_in"], 16)
            for dst, src in ((mask, "mask"), (trif, "trif"), (slot0, "slot0"), (tok, "tok")):
                sp.dma_start(dst[:, :], d[src]).then_inc(S["const_in"], 16)
            for dst, src in ((rope_c, "rope_c"), (rope_s, "rope_s"), (empty, "empty")):
                sp.dma_start(dst[:, :, :], d[src]).then_inc(S["const_in"], 16)
            sp.dma_start(WA[:, :, :], d["wa0"]).then_inc(S["attn0_in"], 16)
            for j, name in enumerate(("ln_scale", "ln_bias")):
                sp.dma_start(lnsb[:, j:j + 1], bc(d[name], [P // HD, HD], 0)).then_inc(S["attn0_in"], 16)
            sp.dma_start(SW2[:, :, :], d["sw2"]).then_inc(S["shared_in"], 16)
            sp.dma_start(GW[:, :, :], d["gw"]).then_inc(S["shared_in"], 16)
            for j, name in enumerate(("lq1", "lk1", "lq2", "lk2")):
                sp.dma_start(lamv[:, j, :], bc(d[name], [P, 8], 0)).then_inc(S["lam_in"], 16)
            sp.dma_start(subw[:, :], bc(d["subln"], [P // HD, HD], 0)).then_inc(S["lam_in"], 16)
            slots = xbuf.rearrange("(e s p) r -> p e s r", s=2, p=P)
            sp.wait_ge(S["const_in"], 16 * 7)
            for s in range(2):
                sp.dma_start(slots[:, :, s, :], bc(empty[:, s, :], [P, NE, ROW], 1)).then_inc(S["init_rows"], 16)
            for n in range(2):
                sp.dma_start(y_dram[n][B * N:, :].rearrange("(s p) d -> p s d", p=P), empty[:, :, 0:D])\
                    .then_inc(S["init_rows"], 16)

            def load_stack(n, slot, g, b):
                w = parts[n].shape[4]
                for first, count, cq, ck in RUNS:
                    for dst, x, c in ((QS, 0, cq), (KS, 1, ck)):
                        src = parts[n][x, b, bass.ds(g * MU, MU), c:c + count, :, :]
                        sp.dma_start(dst[slot][w * first:w * (first + count), :, :],
                                     src.rearrange("m c i t -> (c i) m t")).then_inc(stk[slot], 16)

            def store_parts(n, b, h, ready):
                w = parts[n].shape[4]
                maps = slice(h * (P // w), (h + 1) * (P // w))
                sp.wait_ge(S["sp_parts"], T * n + ready)
                for x in range(2):
                    for slot in range(KPARTS if x else 3):
                        sp.dma_start(parts[n][x, b, maps, slot, :, :], PT[n][b][slot % 3][:, 2 * x + h, :])\
                            .then_inc(S[f"sp_stored{b}{h}"], 16)

            def parts_stored(n, b, h):
                sp.wait_ge(S[f"sp_stored{b}{h}"], STORED * (n + 1))

            def experts(n):
                def load(e, k, first=False):
                    if not (first and n == 0):
                        sp.wait_ge(S["e_meta"], n * NE + e - NB + 1)
                        sp.wait_ge(S["e_xbt_psum"], n * NE + e - NB + 1)
                        sp.wait_ge(S["e_out"], n * NE + e - NB + 1)
                    sp.dma_start(XB[k], xbuf[bass.ds(e * CAP, CAP), :].rearrange("(s p) r -> p s r", p=P))\
                        .then_inc(S[f"e_xb{k}"], 16)
                    sp.dma_start(W2E[k], d["w2"][bass.ds(e * IH, IH), :].rearrange("p (i n) -> p i n", i=2))\
                        .then_inc(S[f"e_w2{k}"], 16)
                for r in range(2):
                    sp.wait_ge(S[f"g_scatter{r}"], (n + 1) * 4 * TOPK * 16)
                for k in range(NB):
                    load(k, k, True)
                with sp.Fori(1, NE // NB) as h:
                    for k in range(NB):
                        load(NB * h + k, k)

            def store_tiles(n):
                for t in range(T):
                    sp.wait_ge(S["s_y"], n * T + t + 1)
                    sp.dma_start(y_dram[n][t * P:(t + 1) * P, :], X[:, t, :]).then_inc(S["y_stored"], 16)

            for b in range(B):
                store_parts(0, b, 0, TB * (b + 1))
                parts_stored(0, b, 0)
                load_stack(0, 2 + b, 0, b)
                store_parts(0, b, 1, TB * (b + 1))
            for b in range(B):
                parts_stored(0, b, 1)
            with sp.Fori(1, 4) as g:
                for b in range(B):
                    sp.wait_ge(S["u0_scores"], 16 * g + 8 * b - 8)
                    load_stack(0, 2 + b, g, b)
            q = NE * C * 2 * INTER // 4
            for j in range(4):
                sp.dma_start(W13[:, j * q:(j + 1) * q], d["w13"][:, j * q:(j + 1) * q]).then_inc(S["w13_in"], 16)
            sp.wait_ge(S["wo_psum"], 4)
            sp.dma_start(SW13, d["sw13"]).then_inc(S["sw13_in"], 16)
            sp.dma_start(WA[:, :, :], d["wa1"]).then_inc(S["attn1_in"], 16)
            store_tiles(0)
            experts(0)
            sp.wait_ge(S["y_added"], 16 * 2 * NE)
            load_x(y_dram[0])
            for s in range(2):
                sp.dma_start(slots[:, :, s, D:], bc(empty[:, s, D:], [P, NE, ROW - D], 1)).then_inc(S["init_rows"], 16)

            def max_rows(u, slot):
                sp.wait_ge(S["u1_mr"], u + 1)
                sp.dma_start(QS[slot][64:67, :, :], mr[:, :]).then_inc(S["u1_mrow"], 16)
            store_parts(1, 0, 0, 2)
            parts_stored(1, 0, 0)
            load_stack(1, 0, 0, 0)
            store_parts(1, 1, 0, 4)
            store_parts(1, 0, 1, 6)
            sp.wait_ge(S["sp_parts"], 2 * T)
            parts_stored(1, 1, 0)
            load_stack(1, 1, 0, 1)
            store_parts(1, 1, 1, 8)
            parts_stored(1, 0, 1)
            load_stack(1, 2, 1, 0)
            parts_stored(1, 1, 1)
            load_stack(1, 3, 1, 1)
            max_rows(0, 0)
            max_rows(1, 1)
            with sp.Fori(0, 3) as i:
                for r in range(4):
                    sp.wait_ge(S["u1_scores"], 64 * i + 16 * r + 16)
                    load_stack(1, r, 2 * i + 2 + r // 2, r % 2)
                    max_rows(4 * i + r + 2, (r + 2) % 4)
            max_rows(14, 2)
            max_rows(15, 3)
            sp.wait_ge(S["wo_psum"], 8)
            sp.dma_start(SW13, d["sw13"]).then_inc(S["sw13_in"], 16)
            store_tiles(1)
            experts(1)
            sp.wait_ge(S["y_added"], 16 * 2 * NE * 2)
            sp.dma_start(out.rearrange("b n d -> (b n) d"), y_dram[1][0:B * N, :]).then_inc(S["final_store"], 16)
            sp.wait_ge(S["final_store"], 16)


        @block.tensor
        def _(pe):
            mm = nc.tensor.matmul

            def transposes(turn, ready, value):
                for tt in range(4):
                    pe.wait_ge(ready, value(tt))
                    for c in range(C):
                        for h in range(2):
                            t = 2 * tt + h
                            o = c * 256 + h * P
                            last = nc.tensor.transpose(PS[:, tt, o:o + P], XN[:, t, c * P:(c + 1) * P], ident[:, :])
                    last.then_inc(S["xt_psum"], 1)

            def ln_transposes(n):
                transposes(LN_TURN[n], S["xn_ready"], lambda tt: T * n + 2 * tt + 2)

            def xt(c, t):
                return XT[:, c, t * P:(t + 1) * P]

            def ffn(n):
                ln_transposes(2 * n)
                if n == 0:
                    pe.wait_ge(S["ffw_in"], 32)
                ready = 4 * LN_TURN[2 * n]
                for g, bank in enumerate(FF_BANK):
                    if g:
                        pe.wait_ge(S["xt_ready"], ready + 4)
                    for i in range(4):
                        t = 4 * g + i
                        if i % 2 == 0 and not g:
                            pe.wait_ge(S["xt_ready"], ready + t // 2 + 1)
                        for c in range(C):
                            last = mm(PS[:, bank + i, 0:FW], xt(c, t), WF[:, c, :], start=(c == 0), stop=(c == C - 1))
                    last.then_inc(S["ff_psum"], 1)
                for g, bank in enumerate(FF_BANK):
                    pe.wait_ge(S["ff_z"], 2 * n + g + 1)
                    for i in range(4):
                        last = nc.tensor.transpose(PS[:, bank + i, D:D + P], ZF[g][:, i * P:(i + 1) * P], ident[:, :])
                    last.then_inc(S["ff_zt_psum"], 1)
                    pe.wait_ge(S["ff_zt"], 2 * n + g + 1)
                    for i in range(4):
                        last = mm(PS[:, bank + i, 0:D], ZS[g][:, i * P:(i + 1) * P], LB[:, :],
                                  start=True, stop=True)
                    last.then_inc(S["ff_out"], 1)

            def attention_out(k):
                if k:
                    transposes(6, S["att_ready"], lambda tt: tt + 1)
                else:
                    transposes(2, S["u0_rows"], lambda tt: 8)
                for tt in range(4):
                    pe.wait_ge(S["xt_ready"], 4 * (2 + 4 * k) + tt + 1)
                    for h in range(2):
                        for c in range(C):
                            last = mm(PS[:, 4 + tt, h * D:(h + 1) * D], xt(c, 2 * tt + h), WA[:, c, 3 * D:],
                                      start=(c == 0), stop=(c == C - 1))
                    last.then_inc(S["wo_psum"], 1)

            def attn0():
                ln_transposes(1)
                pe.wait_ge(S["attn0_in"], 48)
                pe.wait_ge(S["pool_const"], 4)
                for s in range(T + 3):
                    if s < T:
                        pe.wait_ge(S["xt_ready"], 4 + s // 2 + 1)
                        if s >= 2:
                            pe.wait_ge(S["a0_rope"], s - 1)
                            pe.wait_ge(S["a0_v"], s - 1)
                        for o, lo, hi in ((4, 0, 2 * D), (5, 2 * D, 3 * D)):
                            for c in range(C):
                                last = mm(PS[:, o + 2 * (s % 2), 0:hi - lo], xt(c, s), WA[:, c, lo:hi],
                                          start=(c == 0), stop=(c == C - 1))
                        last.then_inc(S["a0_proj"], 1)
                    t = s - 3
                    if t >= 0:
                        pe.wait_ge(S["a0_norm"], t + 1)
                        pe.wait_ge(S["xt_ready"], 8)
                        if t >= 2:
                            pe.wait_ge(S["a0_full"], t - 1)
                        for x in range(4):
                            last = nc.tensor.transpose(PS[:, t % 2, x * P:(x + 1) * P], Y4[t % 4][:, x * P:(x + 1) * P],
                                                       ident[:, :])
                        last.then_inc(S["sp_psum"], 1)

                def av(u, b, j):
                    pe.wait_ge(S["u0_e"], 4 * u + j + 1)
                    for m in range(MU):
                        last = mm(PS[32 * m:32 * m + 32, 4 + b, j * P:N], VA[:, b, j, m, :],
                                  EJ[j][:, m, 0:N - j * P], start=(j == 0), stop=(j == TB - 1),
                                  skip_group_check=True)
                    last.then_inc(S["u0_av"], 1)

                def turn_rows(u, b, fresh):
                    pe.wait_ge(S["u0_os"], u + 1)
                    if not fresh:
                        pe.wait_ge(S["u0_rows"], u - 1)
                    for i in range(TB):
                        last = nc.tensor.transpose(PS[:, 6 + b, i * P:(i + 1) * P], OS[:, b, i * P:(i + 1) * P], ident[:, :])
                    last.then_inc(S["u0_ot"], 1)

                def unit(g, b, first=False):
                    u = 2 * g + b
                    pe.wait_ge(stk[2 + b], STACK * (g + 1))
                    for j in range(TB):
                        for hp in range(2):
                            if not (first and b == 0 and j == 0):
                                pe.wait_ge(S["u0_square"], 8 * u + 2 * j + hp - 1)
                            elif hp == 0:
                                pe.wait_ge(S["a0_full"], T)
                                pe.wait_ge(S["a0_rope"], T)
                                pe.wait_ge(S["a0_v"], T)
                            for k in range(2):
                                m = 2 * hp + k
                                last = mm(PS[:, 2 * hp + k, 0:N - j * P], KS[2 + b][:, m, j * P:(j + 1) * P],
                                          QS[2 + b][:, m, j * P:N], start=True, stop=True)
                            last.then_inc(S["u0_scores"], 1)
                        if j == 3 and not (first and b == 0):
                            turn_rows(u - 1, 1 - b, first)
                        if j == 3:
                            pe.wait_ge(S["u0_va"], u + 1)
                            if not first:
                                pe.wait_ge(S["u0_os"], u - 1)
                            av(u, b, 0)
                        elif not (first and b == 0):
                            av(u - 1, 1 - b, j + 1)
                unit(0, 0, True)
                unit(0, 1, True)
                with pe.Fori(1, 4) as g:
                    for b in range(B):
                        unit(g, b)
                for j in range(1, TB):
                    av(7, 1, j)
                turn_rows(7, 1, False)
                attention_out(0)

            def route(n):
                ln_transposes(3 + 2 * n)
                pe.wait_ge(S["shared_in"], 32)
                pe.wait_ge(S["sw13_in"], 16 * (n + 1))
                for t in range(T):
                    if t % 2 == 0:
                        pe.wait_ge(S["xt_ready"], 4 * LN_TURN[3 + 2 * n] + t // 2 + 1)
                    for c in range(C):
                        last = mm(LOG[t // TB][:, t % TB, :], xt(c, t), GW[:, c, :], start=(c == 0), stop=(c == C - 1))
                    if t % TB == TB - 1:
                        last.then_inc(S["g_logits"], 1)

            def positions(n, h):
                pe.wait_ge(S["g_mask"], 2 * n + h + 1)
                for i in range(TB):
                    t = TB * h + i
                    for k in range(t + 1):
                        last = mm(POS[h][:, i, :], (ones if k < t else tri)[:, :], mkb[:, k, :],
                                  start=(k == 0), stop=(k == t))
                last.then_inc(S["g_pos"], 1)

            def shared(n):
                def first_half(t):
                    q = n * T + t
                    for k in range(2):
                        if t >= 2:
                            pe.wait_ge(S["s_g"], q - 1)
                        for c in range(C):
                            last = mm(PS[:, 2 * k + t % 2, 0:SI], xt(c, t), SW13[:, c, k * SI:(k + 1) * SI],
                                      start=(c == 0), stop=(c == C - 1))
                    last.then_inc(S["s_h"], 1)

                def second_half(t):
                    q = n * T + t
                    pe.wait_ge(S["s_g"], q + 1)
                    if t >= 1:
                        pe.wait_ge(S["s_gt"], q)
                    for k in range(3):
                        w = min(P, SI - k * P)
                        last = nc.tensor.transpose(PS[0:w, 6, k * P:(k + 1) * P], GSH[t % 2][:, k * P:k * P + w], ident[:, :])
                    last.then_inc(S["s_gt_psum"], 1)
                    pe.wait_ge(S["s_gt"], q + 1)
                    if t >= 1:
                        pe.wait_ge(S["s_y"], q)
                    for k in range(3):
                        w = min(P, SI - k * P)
                        last = mm(PS[:, 7, 0:D], GTS[0:w, k, :], SW2[0:w, k, :], start=(k == 0), stop=(k == 2))
                    last.then_inc(S["s_out"], 1)
                positions(n, 0)
                first_half(0)
                first_half(1)
                positions(n, 1)
                for t in range(T):
                    second_half(t)
                    if t + 2 < T:
                        first_half(t + 2)

            def experts(n):
                def turn_x(e, k, h, fresh=False):
                    pe.wait_ge(S[f"e_xb{k}"], 16 * (NE // NB) * n + 16 * (h + 1))
                    if not fresh:
                        pe.wait_ge(S["e_xbt"], NE * n + e - 1)
                    for c in range(C):
                        for s in range(2):
                            last = nc.tensor.transpose(PS[:, k % 2, c * 256 + s * P:c * 256 + (s + 1) * P],
                                                       XB[k][:, s, c * P:(c + 1) * P], ident[:, :])
                    last.then_inc(S["e_xbt_psum"], 1)

                def up(e, k, s, fresh):
                    if s == 0:
                        pe.wait_ge(S["e_xbt"], NE * n + e + 1)
                    if not fresh:
                        pe.wait_ge(S["e_g"], 2 * (NE * n + e) + s - 3)
                    for c in range(C):
                        last = mm(PS[:, 2 + 2 * (k % 2) + s, 0:2 * INTER], XBT[k % 2][:, c, s * P:(s + 1) * P],
                                  W13[:, bass.ds(e * (C * 2 * INTER) + c * 2 * INTER, 2 * INTER)],
                                  start=(c == 0), stop=(c == C - 1))
                    last.then_inc(S["e_h"], 1)

                def turn_g(e, k, fresh):
                    pe.wait_ge(S["e_g"], 2 * (NE * n + e) + 2)
                    if not fresh:
                        pe.wait_ge(S["e_gt"], NE * n + e)
                    for i in range(2):
                        for s in range(2):
                            last = nc.tensor.transpose(PS[0:IH, 6, (2 * i + s) * P:(2 * i + s + 1) * P],
                                                       GE[k % 2][s][:, i * IH:(i + 1) * IH], ident[:, :])
                    last.then_inc(S["e_gt_psum"], 1)

                def down(e, k, h, fresh):
                    pe.wait_ge(S["e_gt"], NE * n + e + 1)
                    pe.wait_ge(S[f"e_w2{k}"], 16 * (NE // NB) * n + 16 * (h + 1))
                    if not fresh:
                        pe.wait_ge(S["e_ob"], NE * n + e)
                    for s in range(2):
                        for i in range(2):
                            last = mm(PS[:, 7, s * D:(s + 1) * D], GT[k % 2][:, i, s * P:(s + 1) * P], W2E[k][:, i, :],
                                      start=(i == 0), stop=(i == 1))
                    last.then_inc(S["e_out"], 1)

                def step(e, k, h, first=False, last=False):
                    before, after = k - 1 if k else NB - 1, (k + 1) % NB
                    up(e, k, 0, first and k < 2)
                    if not (first and k == 0):
                        turn_g(e - 1, before, first and k == 1)
                    up(e, k, 1, first and k < 2)
                    if not (last and k == NB - 1):
                        turn_x(e + 1, after, h + (k + 1) // NB, first and k == 0)
                    if not (first and k == 0):
                        down(e - 1, before, h if k else h - 1, first and k == 1)
                pe.wait_ge(S["w13_in"], 64)
                pe.wait_ge(S["s_y"], T * (n + 1))
                turn_x(0, 0, 0, True)
                for k in range(NB):
                    step(k, k, 0, first=True)
                with pe.Fori(1, NE // NB - 1) as h:
                    for k in range(NB):
                        step(NB * h + k, k, h)
                for k in range(NB):
                    step(NE - NB + k, k, NE // NB - 1, last=True)
                turn_g(NE - 1, NB - 1, False)
                down(NE - 1, NB - 1, NE // NB - 1, False)

            def attn1():
                ln_transposes(4)
                pe.wait_ge(S["attn1_in"], 16)
                pe.wait_ge(S["xt_ready"], 4 * 5 + 4)
                for r in range(8):
                    half, b, x = r // 4, r // 2 % 2, r % 2
                    if r >= 2:
                        pe.wait_ge(S["sp_rest"], T + r - 1)
                    for c in range(C):
                        last = mm(PS[:, 4 + r % 2, :], WA[:, c, x * D + half * P:x * D + (half + 1) * P],
                                  XT[:, c, b * N:(b + 1) * N], start=(c == 0), stop=(c == C - 1))
                    last.then_inc(S["sp_psum"], 1)

                def project_v(t):
                    if t >= 2:
                        pe.wait_ge(S["a1_v"], t - 1)
                    for c in range(C):
                        last = mm(PS[:, t % 2, 0:D], xt(c, t), WA[:, c, 2 * D:3 * D], start=(c == 0), stop=(c == C - 1))
                    last.then_inc(S["a1_v_psum"], 1)

                def row_scores(w, slot, i4, x, start=False):
                    i, m = x // MU, x % MU
                    if x == 0:
                        pe.wait_ge(stk[slot], STACK * ((4 if slot >= 2 else 0) + i4 + 1))
                    y = 16 * slot + x
                    if not (start and y < LAST[y]):
                        pe.wait_ge(S["u1_maxed"], 16 * w + x - LAST[y] + 1)
                    mm(PS[:, 3 + RING[y], :], QS[slot][0:64, m, i * P:(i + 1) * P], KS[slot][0:64, m, :],
                       start=True, stop=True).then_inc(S["u1_max"], 1)

                def turn_maxima(w, first=False):
                    pe.wait_ge(S["u1_split"], w + 1)
                    if not first:
                        pe.wait_ge(S["u1_rows"], w - 2)
                    for i in range(TB):
                        last = nc.tensor.transpose(MT[:, i * P:(i + 1) * P], mp[:, i, :, :].rearrange("p c m -> p (c m)"),
                                                   identb[:, :])
                    last.then_inc(S["u1_mt"], 1)

                def av(u, b, j):
                    pe.wait_ge(S["u1_exp"], 16 * u + 4 * j + 4)
                    for m in range(MU):
                        last = mm(PS[32 * m:32 * m + 32, 6, :], VA[:, b, j, m // 2, :], E[j % 2][:, m, :],
                                  start=(j == 0), stop=(j == TB - 1), skip_group_check=True)
                    last.then_inc(S["u1_av"], 1)

                def turn_rows(u, b):
                    pe.wait_ge(S["u1_os"], u + 1)
                    for i in range(TB):
                        last = nc.tensor.transpose(PS[:, 7, i * P:(i + 1) * P], OS[:, b, i * P:(i + 1) * P], ident[:, :])
                    last.then_inc(S["u1_ot"], 1)

                def unit(i4, u4, first=False, last=False):
                    u = 4 * i4 + u4
                    final = last and u4 == 3
                    pe.wait_ge(S["u1_mrow"], 16 * u + 16)
                    pe.wait_ge(S["u1_va"], u + 1)
                    for j in range(TB):
                        if j == 1 and not final:
                            turn_maxima(u + 1, first and u4 < 2)
                        for m in range(MU):
                            y = 16 * u4 + 4 * j + m
                            if not (first and y < LAST[y]):
                                pe.wait_ge(S["u1_exp"], 16 * u + 4 * j + m - LAST[y] + 1)
                            mm(PS[:, RING[y], :], KS[u4][0:67, m, j * P:(j + 1) * P], QS[u4][0:67, m, :],
                               start=True, stop=True).then_inc(S["u1_scores"], 1)
                            if not (last and u4 > 1):
                                row_scores(u + 2, (u4 + 2) % 4, i4 + (u4 + 2) // 4, 4 * j + m)
                            if m == 2 and j:
                                if j == 1 and not (first and u4 == 0):
                                    pe.wait_ge(S["u1_os"], u)
                                av(u, u4 % 2, j - 1)
                            elif m == 2 and not (first and u4 == 0):
                                av(u - 1, (u4 + 1) % 2, 3)
                        if j == 2 and not (first and u4 == 0):
                            if final:
                                pe.wait_ge(S["u1_rows"], u - 1)
                            else:
                                pe.wait_ge(S["u1_mr"], u + 2)
                            turn_rows(u - 1, (u4 + 1) % 2)
                pe.wait_ge(S["sp_rest"], T + 8)
                for x in range(16):
                    row_scores(0, 0, 0, x, True)
                turn_maxima(0, True)
                for x in range(16):
                    row_scores(1, 1, 0, x, True)
                    if x % 2:
                        project_v(x // 2)
                pe.wait_ge(S["a1_v"], T)
                pe.wait_ge(S["stack_pad"], 1)
                for u4 in range(4):
                    unit(0, u4, first=True)
                with pe.Fori(1, 3) as i4:
                    for u4 in range(4):
                        unit(i4, u4)
                for u4 in range(4):
                    unit(3, u4, last=True)
                av(15, 1, 3)
                pe.wait_ge(S["u1_rows"], 15)
                turn_rows(15, 1)
                attention_out(1)

            pe.wait_ge(S["ident_in"], 16)
            ffn(0)
            attn0()
            ffn(1)
            route(0)
            shared(0)
            experts(0)
            attn1()
            route(1)
            shared(1)
            experts(1)

        @block.vector
        def _(dve):
            ch = Chain(dve, S["dve_self"])
            v = nc.vector

            def stats(q):
                for t in (2 * q, 2 * q + 1):
                    last = v.bn_stats(st[:, t, :], X[:, t, :])
                return last

            def layer_norm(n, loaded=0):
                for q in range(0 if loaded else 3, 4):
                    if loaded:
                        dve.wait_ge(S[f"x_in{q}"], 16 * loaded)
                    last = stats(q)
                ch.link(last)
                for t in range(T):
                    last = v.bn_aggr(mv[:, t, :], st[:, t, :])
                ch.link(last)
                ch.link(v.tensor_scalar(rv[:, :], mv[:, :, 1], EPS, None, ALU.add))
                v.reciprocal(rv[:, :], rv[:, :]).then_inc(S["ln_var"], 1)
                dve.wait_ge(S["ln_rstd"], n + 1)
                for t in range(T):
                    v.tensor_scalar(XN[:, t, :], X[:, t, :], mv[:, t, 0:1], rstd[:, t:t + 1],
                                    ALU.subtract, ALU.mult).then_inc(S["xn_ready"], 1)

            def ffn(n):
                layer_norm(2 * n, 0 if n else 1)
                if n == 0:
                    dve.wait_ge(S["pool_const"], 4)
                for g, bank in enumerate(FF_BANK):
                    q = 2 * n + g
                    logits = PS[:, bank:bank + 4, D + LE * RANK:FW]
                    dve.wait_ge(S["ff_psum"], q + 1)
                    ch.link(v.tensor_reduce(m4[:, :], logits, AX_X, ALU.max))
                    v.tensor_tensor(el[:, :, :], logits, bc(m4[:, :], [P, 4, LE], 2), ALU.subtract)\
                        .then_inc(S["ff_shift"], 1)
                    dve.wait_ge(S["ff_exp"], q + 1)
                    for i in range(4):
                        last = v.max(out=v8[:, i, :], in_=ep[:, i, 0:LE])
                    ch.link(last)
                    ch.link(v.tensor_copy(rep[:, :, 0:2], v8[:, 0:4, 0:2]))
                    for i in range(4):
                        last = v.match_replace(rpl[:, i, :], rep[:, i, :], ep[:, i, :], 2.0)
                    ch.link(last)
                    ch.link(v.scalar_tensor_tensor(g4[:, :, :], rpl[:, :, 0:LE], 1.5, ep[:, :, 0:LE], ALU.is_gt, ALU.mult))
                    ch.link(v.tensor_reduce(s4[:, :], g4[:, :, :], AX_X, ALU.add))
                    ch.link(v.reciprocal(s4[:, :], s4[:, :]))
                    ch.link(v.scalar_tensor_tensor(g4[:, :, :], g4[:, :, :], 32.0 / RANK, bc(s4[:, :], [P, 4, LE], 2),
                                                   ALU.mult, ALU.mult))
                    v.tensor_tensor(ZF[g].rearrange("p (t e r) -> p t e r", t=4, e=LE),
                                    PS[:, bank:bank + 4, D:D + LE * RANK].rearrange("p t (e r) -> p t e r", e=LE),
                                    bc(g4[:, :, :], [P, 4, LE, RANK], 3), ALU.mult)
                    x4 = X[:, 4 * g:4 * g + 4, :]
                    v.scalar_tensor_tensor(x4, PS[:, bank:bank + 4, 0:D], 0.5, x4, ALU.mult, ALU.add)\
                        .then_inc(S["ff_z"], 1)
                for g, bank in enumerate(FF_BANK):
                    q = 2 * n + g
                    dve.wait_ge(S["ff_out"], q + 1)
                    dve.wait_ge(S["ff_z"], q + 1)
                    x4 = X[:, 4 * g:4 * g + 4, :]
                    v.scalar_tensor_tensor(x4, PS[:, bank:bank + 4, 0:D], 0.5, x4, ALU.mult, ALU.add)\
                        .then_inc(S["ff_done"], 1)
                    dve.wait_ge(S["ff_done"], q + 1)
                    for pair in range(2 * g, 2 * g + 2 - g):
                        stats(pair)

            def attention_out(k):
                for tt in range(4):
                    dve.wait_ge(S["wo_psum"], 4 * k + tt + 1)
                    x2 = X[:, 2 * tt:2 * tt + 2, :]
                    v.tensor_tensor(x2, PS[:, 4 + tt, :].rearrange("p (t d) -> p t d", t=2), x2, ALU.add)\
                        .then_inc(S["res_done"], 1)
                    if tt:
                        dve.wait_ge(S["res_done"], 4 * k + tt)
                        stats(tt - 1)
                dve.wait_ge(S["res_done"], 4 * k + 4)

            def attn0():
                layer_norm(1)
                dve.wait_ge(S["const_in"], 16 * 7)
                for s in range(T + 3):
                    if s < T:
                        r, i = s % 2, s % TB
                        dve.wait_ge(S["a0_proj"], s + 1)
                        if s >= 2:
                            dve.wait_ge(S["a0_sum"], s - 1)
                        qk = PS[:, 4 + 2 * r, :].rearrange("p (h x e) -> p h x e", x=2, e=HD // 2)
                        t2 = RT2[r].rearrange("p (h x e) -> p h x e", x=2, e=HD // 2)
                        v.tensor_tensor(RT1[r].rearrange("p (h e) -> p h e", e=HD),
                                        PS[:, 4 + 2 * r, :].rearrange("p (h e) -> p h e", e=HD),
                                        bc(rope_c[:, i, :], [P, 32, HD], 1), ALU.mult)
                        for x in range(2):
                            last = v.tensor_tensor(t2[:, :, x, :], qk[:, :, 1 - x, :],
                                                   bc(rope_s[:, i, x * 8:x * 8 + 8], [P, 32, 8], 1), ALU.mult)
                        last.then_inc(S["a0_rope"], 1)
                    t = s - 1
                    if 0 <= t < T:
                        r = t % 2
                        dve.wait_ge(S["a0_sum"], t + 1)
                        if t >= 2:
                            dve.wait_ge(S["a0_center"], t - 1)
                        ch.link(v.tensor_reduce(hs1[:, r, :], Y4[t % 4].rearrange("p (h e) -> p h e", e=HD), AX_X, ALU.add))
                        v.tensor_scalar(hs2[:, r, :], hs1[:, r, :], 1.0 / HD, None, ALU.mult).then_inc(S["a0_mean"], 1)
                    t = s - 2
                    if 0 <= t < T:
                        r = t % 2
                        dve.wait_ge(S["a0_square"], t + 1)
                        ch.link(v.tensor_reduce(hs3[:, r, :], SQ[r].rearrange("p (h e) -> p h e", e=HD), AX_X, ALU.add))
                        ch.link(v.tensor_scalar(hs3[:, r, :], hs3[:, r, :], 1.0 / HD, EPS, ALU.mult, ALU.add))
                        v.reciprocal(hs3[:, r, :], hs3[:, r, :]).then_inc(S["a0_var"], 1)
                    t = s - 3
                    if 0 <= t < T:
                        rest(t, t % 2, FULL[t % 2].rearrange("p (x t) -> p x t", x=4),
                             PT[0][t // TB][0][:, :, (t % TB) * P:(t % TB + 1) * P], 4)
                    t = s - 2
                    if 0 <= t < T:
                        y = Y4[t % 4].rearrange("p (h e) -> p h e", e=HD)
                        dve.wait_ge(S["a0_rstd"], t + 1)
                        v.tensor_tensor(y, y, bc(hs4[:, t % 2, :], [P, 32, HD], 2), ALU.mult).then_inc(S["a0_norm"], 1)

                def powers(u, j):
                    dve.wait_ge(S["u0_square"], 8 * u + 2 * j + 2)
                    if j < TB - 1:
                        e = EJ[j][:, :, P:N - j * P]
                        v.tensor_tensor(e, e, e, ALU.mult)
                    dve.wait_ge(S["u0_masked"], 4 * u + j + 1)
                    e = EJ[j][:, :, 0:P]
                    v.tensor_tensor(e, e, e, ALU.mult).then_inc(S["u0_e"], 1)

                def rows(u, b, g):
                    dve.wait_ge(S["u0_ot"], u + 1)
                    ot = PS[:, 6 + b, :].rearrange("p (i m e) -> p i m e", i=TB, m=MU)
                    v.reciprocal(rec[:, b, :, :], ot[:, :, :, HD]).then_inc(S["u0_rec"], 1)
                    dve.wait_ge(S["u0_rec"], u + 1)
                    v.tensor_tensor(XN[:, TB * b:TB * b + TB, bass.ds(g * (MU * HD), MU * HD)]
                                    .rearrange("p i (m e) -> p i m e", m=MU), ot[:, :, :, 0:HD],
                                    bc(rec[:, b, :, :], [P, TB, MU, HD], 3), ALU.mult).then_inc(S["u0_rows"], 1)

                def unit(g, b, first=False):
                    for j in range(TB):
                        powers(2 * g + b, j)
                    if not (first and b == 0):
                        rows(2 * g + b - 1, 1 - b, g if b else g - 1)
                unit(0, 0, True)
                unit(0, 1, True)
                with dve.Fori(1, 4) as g:
                    for b in range(B):
                        unit(g, b)
                rows(7, 1, 3)
                attention_out(0)

            def rest(q, r, full, high, n):
                dve.wait_ge(S["sp_high"], q + 1)
                if q >= 2:
                    dve.wait_ge(S["sp_parts"], q - 1)
                v.tensor_tensor(R1[r].rearrange("p (x t) -> p x t", x=n), full, high, ALU.subtract)\
                    .then_inc(S["sp_rest"], 1)

            def route(n):
                layer_norm(3 + 2 * n)
                for h in range(2):
                    choose(n, h)
                    place(n, h)

            def choose(n, h):
                t4 = slice(TB * h, TB * h + TB)
                probs = pe_[:, t4, 0:NE]
                dve.wait_ge(S["g_logits"], 2 * n + h + 1)
                ch.link(v.tensor_reduce(m8[:, t4], LOG[h], AX_X, ALU.max))
                v.tensor_tensor(probs, LOG[h], bc(m8[:, t4], [P, TB, NE], 2), ALU.subtract).then_inc(S["g_shift"], 1)
                dve.wait_ge(S["g_exp"], 2 * n + h + 1)
                for t in range(TB * h, TB * h + TB):
                    v.max(out=v8[:, t, :], in_=pe_[:, t, 0:NE])
                ch.link(v.tensor_reduce(rs8[:, t4], probs, AX_X, ALU.add))
                v.reciprocal(rs8[:, t4], rs8[:, t4])
                ch.link(v.tensor_copy(rep8[:, t4, 0:TOPK], v8[:, t4, 0:TOPK]))
                for t in range(TB * h, TB * h + TB):
                    last = v.match_replace(rpe[:, t, :], rep8[:, t, :], pe_[:, t, :], 2.0)
                ch.link(last)
                v.tensor_scalar(mkb[:, t4, :], rpe[:, t4, 0:NE], 1.5, None, ALU.is_gt).then_inc(S["g_mask"], 1)
                v.tensor_scalar(mk[:, t4, :], rpe[:, t4, 0:NE], 1.5, None, ALU.is_gt)
                ch.link(v.tensor_tensor(wt[:, t4, :], probs, bc(rs8[:, t4], [P, TB, NE], 2), ALU.mult))

            def place(n, h):
                t4 = slice(TB * h, TB * h + TB)
                dve.wait_ge(S["g_pos"], 2 * n + h + 1)
                ch.link(v.scalar_tensor_tensor(mk[:, t4, :], POS[h], float(CAP), mk[:, t4, :], ALU.is_lt, ALU.mult))
                v.tensor_tensor(rpe[:, t4, 0:NE], POS[h], bc(slot0[:, :], [P, TB, NE], 1), ALU.add)
                ch.link(v.tensor_tensor(wt[:, t4, :], wt[:, t4, :], mk[:, t4, :], ALU.mult))
                ch.link(v.tensor_tensor(mk[:, t4, :], rpe[:, t4, 0:NE], mk[:, t4, :], ALU.mult))
                for t in range(TB * h, TB * h + TB):
                    last = v.max(out=s8[:, t, :], in_=mk[:, t, :])
                ch.link(last)
                ch.link(v.tensor_scalar(s8z[:, t4, :], s8[:, t4, :], 0.0, SKIP, ALU.is_equal, ALU.mult))
                if n:
                    dve.wait_ge(S["g_scatter0"], 4 * TOPK * 16)
                    dve.wait_ge(S["g_scatter1"], 4 * TOPK * 16)
                ch.link(v.scalar_tensor_tensor(idx[:, t4, :], s8[:, t4, :], -1.0, s8z[:, t4, :], ALU.add, ALU.add))
                v.tensor_copy(SRC[:, t4, D:D + 1], tok[:, t4].unsqueeze(2))
                v.tensor_copy(SRC[:, t4, D + 1:ROW], wt[:, t4, :]).then_inc(S["g_weight"], 1)

            def shared(n):
                def gate(t):
                    q = n * T + t
                    dve.wait_ge(S["s_silu"], q + 1)
                    if t >= 2:
                        dve.wait_ge(S["s_gt_psum"], q - 1)
                    v.tensor_tensor(GSH[t % 2], HSH[t % 2], PS[:, 2 + t % 2, 0:SI], ALU.mult).then_inc(S["s_g"], 1)

                def add(t):
                    dve.wait_ge(S["s_out"], n * T + t + 1)
                    v.scalar_tensor_tensor(X[:, t, :], PS[:, 7, 0:D], 0.5, X[:, t, :], ALU.mult, ALU.add)\
                        .then_inc(S["s_y"], 1)
                gate(0)
                gate(1)
                for t in range(T):
                    add(t)
                    if t + 2 < T:
                        gate(t + 2)

            def experts(n):
                def turned(e, k, fresh=False):
                    dve.wait_ge(S["e_xbt_psum"], NE * n + e + 1)
                    if not fresh:
                        dve.wait_ge(S["e_h"], 2 * (NE * n + e) - 2)
                    v.tensor_copy(XBT[k % 2], PS[:, k % 2, :].rearrange("p (c s) -> p c s", c=C)).then_inc(S["e_xbt"], 1)

                def step(e, k, h, first=False, last=False):
                    dve.wait_ge(S[f"e_xb{k}"], 16 * (NE // NB) * n + 16 * (h + 1))
                    if not first:
                        dve.wait_ge(S["y_added"], 32 * (NE * n + e) - 32 * (NB - 1))
                        dve.wait_ge(S["e_ob"], NE * n + e - NB + 1)
                    v.tensor_scalar(meta_w[:, k, :], XB[k][:, :, bass.ds(D + 1 + e, 1)].rearrange("p s o -> p (s o)"),
                                    0.5, None, ALU.mult)
                    v.tensor_copy(meta_i[:, k, :], XB[k][:, :, D]).then_inc(S["e_meta"], 1)
                    for s in range(2):
                        dve.wait_ge(S["e_silu"], 2 * (NE * n + e) + s + 1)
                        if not (first and k < 2):
                            dve.wait_ge(S["e_gt_psum"], NE * n + e - 1)
                        v.tensor_tensor(GE[k % 2][s], HE[k % 2][s], PS[:, 2 + 2 * (k % 2) + s, INTER:2 * INTER], ALU.mult)\
                            .then_inc(S["e_g"], 1)
                    if not (last and k == NB - 1):
                        turned(e + 1, k + 1, first and k == 0)
                turned(0, 0, True)
                for k in range(NB):
                    step(k, k, 0, first=True)
                with dve.Fori(1, NE // NB - 1) as h:
                    for k in range(NB):
                        step(NB * h + k, k, h)
                for k in range(NB):
                    step(NE - NB + k, k, NE // NB - 1, last=True)

            def attn1():
                layer_norm(4, 2)
                dve.wait_ge(S["lam_in"], 80)
                ch.link(v.tensor_tensor(lam[:, :], lamv[:, 0, :], lamv[:, 1, :], ALU.mult))
                ch.link(v.tensor_reduce(m4[:, 0:1], lam[:, :], AX_X, ALU.add))
                ch.link(v.tensor_tensor(lam[:, :], lamv[:, 2, :], lamv[:, 3, :], ALU.mult))
                v.tensor_reduce(m4[:, 1:2], lam[:, :], AX_X, ALU.add).then_inc(S["lam_sum"], 1)
                dve.wait_ge(S["lam_exp"], 1)
                ch.link(v.scalar_tensor_tensor(lam[:, 0:1], lam[:, 2:3], -LAMBDA_INIT, lam[:, 1:2], ALU.add, ALU.subtract))
                ch.link(v.tensor_scalar(subw[:, :], subw[:, :], 1.0 - LAMBDA_INIT, None, ALU.mult))
                for r in range(8):
                    rest(T + r, r % 2, PS[:, 4 + r % 2:5 + r % 2, :], PT[1][r // 2 % 2][0][:, qk_part(r), :], 1)

                def maximum(w, slot, x, fresh=False):
                    if x == 0 and not fresh:
                        dve.wait_ge(S["u1_split"], w - 1)
                    dve.wait_ge(S["u1_max"], 16 * w + x + 1)
                    v.tensor_reduce(nm[:, slot % 2, x // MU, x % MU:x % MU + 1], PS[:, 3 + RING[16 * slot + x], :],
                                    AX_X, ALU.max, negate=True).then_inc(S["u1_maxed"], 1)

                def squares(b, g0, g1):
                    t0, t1, h0, h1 = TB * b, TB * b + TB, 2 * g0, 2 * g1
                    x = XN[:, t0:t1, h0 * HD:h1 * HD]
                    size = TB * (h1 - h0) * HD
                    a, b_ = (stack_mem[:, o:o + size].rearrange("p (t d) -> p t d", t=TB) for o in (512, 1536))
                    ch.link(v.tensor_scalar(a, x, 4e18, -4e18, ALU.min, ALU.max))
                    v.tensor_tensor(a, a, a, ALU.mult)
                    ch.link(v.tensor_scalar(b_, x, 2.0 ** -40, 1e18, ALU.mult, ALU.min))
                    ch.link(v.tensor_scalar(b_, b_, -1e18, None, ALU.max))
                    ch.link(v.tensor_tensor(b_, b_, b_, ALU.mult))
                    for k, sq in enumerate((a, b_)):
                        last = v.tensor_reduce(rms[:, k, :].rearrange("p (t h) -> p t h", t=T)[:, t0:t1, h0:h1],
                                               sq.rearrange("p t (h e) -> p t h e", e=HD), AX_X, ALU.add)
                    ch.link(last)

                def rows(u, b, g):
                    dve.wait_ge(S["u1_ot"], u + 1)
                    ot = PS[:, 7, :].rearrange("p (i m e) -> p i m e", i=TB, m=MU)
                    v.reciprocal(rec[:, b, :, :], ot[:, :, :, HD]).then_inc(S["u1_rec"], 1)
                    dve.wait_ge(S["u1_rec"], u + 1)
                    v.tensor_tensor(amap[:, :, :, :], ot[:, :, :, 0:HD], bc(rec[:, b, :, :], [P, TB, MU, HD], 3), ALU.mult)\
                        .then_inc(S["u1_rows"], 1)
                    dve.wait_ge(S["u1_rows"], u + 1)
                    two = amap[:, :, :, :].rearrange("p i (h x) e -> p i h x e", x=2)
                    v.scalar_tensor_tensor(XN[:, TB * b:TB * b + TB, bass.ds(g * 32, 32)]
                                           .rearrange("p i (h e) -> p i h e", h=2),
                                           two[:, :, :, 1, :], lam[:, 0:1], two[:, :, :, 0, :], ALU.mult, ALU.add)\
                        .then_inc(S["u1_diff"], 1)

                def unit(i4, u4, first=False, last=False):
                    u = 4 * i4 + u4
                    for j in range(TB):
                        if not (last and u4 > 1):
                            for k in range(4):
                                maximum(u + 2, (u4 + 2) % 4, 4 * j + k)
                        if j == 2 and not (first and u4 == 0):
                            rows(u - 1, (u4 + 1) % 2, 2 * i4 + (u4 - 1) // 2)
                            if last and u4 > 1:
                                dve.wait_ge(S["u1_diff"], u)
                                squares(*((1, 0, 7) if u4 == 2 else (0, 0, 8)))
                for x in range(16):
                    maximum(0, 0, x, True)
                for x in range(16):
                    maximum(1, 1, x, True)
                for u4 in range(4):
                    unit(0, u4, first=True)
                with dve.Fori(1, 3) as i4:
                    for u4 in range(4):
                        unit(i4, u4)
                for u4 in range(4):
                    unit(3, u4, last=True)
                rows(15, 1, 7)
                dve.wait_ge(S["u1_diff"], 16)
                squares(1, 7, 8)
                flat = XN[:, :, :].rearrange("p t d -> p (t d)")
                v.tensor_scalar(rms[:, 2, :], rms[:, 1, :], 3.4028235e38 * 2.0 ** -80, None, ALU.is_le)
                v.tensor_scalar(rms[:, 0, :], rms[:, 0, :], 1.0 / HD, EPS, ALU.mult, ALU.add)
                ch.link(v.tensor_scalar(rms[:, 1, :], rms[:, 1, :], 1.0 / HD, 1e-30, ALU.mult, ALU.add))
                v.reciprocal(rms[:, 0:2, :], rms[:, 0:2, :]).then_inc(S["rms_var"], 1)
                dve.wait_ge(S["rms_rstd"], 1)
                ch.link(v.scalar_tensor_tensor(rms[:, 3, :], rms[:, 1, :], 2.0 ** -40, rms[:, 0, :], ALU.mult, ALU.min))
                ch.link(v.tensor_tensor(rms[:, 3, :], rms[:, 3, :], rms[:, 2, :], ALU.mult))
                x3 = flat.rearrange("p (h e) -> p h e", e=HD)
                for q in range(4):
                    h = slice(32 * q, 32 * q + 32)
                    v.tensor_tensor(x3[:, h, :], x3[:, h, :], bc(rms[:, 3, h], [P, 32, HD], 2), ALU.mult)\
                        .then_inc(S["att_ready"], 1)
                attention_out(1)

            ffn(0)
            attn0()
            ffn(1)
            route(0)
            shared(0)
            experts(0)
            attn1()
            route(1)
            shared(1)
            experts(1)

        @block.scalar
        def _(act):
            act_fn = nc.scalar.activation

            def evacuate_xt(turn, scale=1.0):
                for tt in range(4):
                    act.wait_ge(S["xt_psum"], 4 * turn + tt + 1)
                    act_fn(XT[:, :, tt * 256:(tt + 1) * 256], PS[:, tt, :].rearrange("p (c t) -> p c t", c=C), ACT.Copy,
                           scale=scale).then_inc(S["xt_ready"], 1)

            def layer_norm(n):
                act.wait_ge(S["ln_var"], n + 1)
                act_fn(rstd[:, :], rv[:, :], ACT.Sqrt).then_inc(S["ln_rstd"], 1)
                evacuate_xt(LN_TURN[n])

            def ffn(n):
                layer_norm(2 * n)
                for g in range(2):
                    act.wait_ge(S["ff_shift"], 2 * n + g + 1)
                    act_fn(ep[:, :, 0:LE], el[:, :, :], ACT.Exp).then_inc(S["ff_exp"], 1)
                for g, bank in enumerate(FF_BANK):
                    act.wait_ge(S["ff_zt_psum"], 2 * n + g + 1)
                    act_fn(ZS[g].rearrange("p (i t) -> p i t", i=4), PS[:, bank:bank + 4, D:D + P], ACT.Copy)\
                        .then_inc(S["ff_zt"], 1)

            def split_high(q, dst, full):
                act_fn(dst, full, ACT.Copy).then_inc(S["sp_high"], 1)

            def split_mid(q, r, dst, n):
                act.wait_ge(S["sp_rest"], q + 1)
                act_fn(dst, R1[r].rearrange("p (x t) -> p x t", x=n), ACT.Copy).then_inc(S["sp_mid"], 1)

            def attn0():
                layer_norm(1)
                act.wait_ge(S["attn0_in"], 48)
                for s in range(T + 4):
                    if s < T:
                        act.wait_ge(S["a0_proj"], s + 1)
                        act_fn(V[:, s, :], PS[:, 5 + 2 * (s % 2), 0:D], ACT.Copy).then_inc(S["a0_v"], 1)
                    t = s - 3
                    if 0 <= t < T:
                        act.wait_ge(S["sp_psum"], t + 1)
                        if t >= 2:
                            act.wait_ge(S["sp_rest"], t - 1)
                        act_fn(FULL[t % 2], PS[:, t % 2, :], ACT.Identity, bias=lnsb[:, 1:2], scale=lnsb[:, 0:1])\
                            .then_inc(S["a0_full"], 1)
                        act.wait_ge(S["a0_full"], t + 1)
                        split_high(t, PT[0][t // TB][0][:, :, (t % TB) * P:(t % TB + 1) * P],
                                   FULL[t % 2].rearrange("p (x t) -> p x t", x=4))
                    t = s - 1
                    if 0 <= t < T:
                        act.wait_ge(S["a0_center"], t + 1)
                        if t >= 2:
                            act.wait_ge(S["a0_var"], t - 1)
                        act_fn(SQ[t % 2], Y4[t % 4], ACT.Square).then_inc(S["a0_square"], 1)
                    t = s - 2
                    if 0 <= t < T:
                        act.wait_ge(S["a0_var"], t + 1)
                        if t >= 2:
                            act.wait_ge(S["a0_norm"], t - 1)
                        act_fn(hs4[:, t % 2, :], hs3[:, t % 2, :], ACT.Sqrt).then_inc(S["a0_rstd"], 1)
                    t = s - 4
                    if 0 <= t < T:
                        split_mid(t, t % 2, PT[0][t // TB][1][:, :, (t % TB) * P:(t % TB + 1) * P], 4)

                def output(u, b, fresh):
                    act.wait_ge(S["u0_av"], 4 * u + 4)
                    if not fresh:
                        act.wait_ge(S["u0_ot"], u - 1)
                    act_fn(OS[:, b, :], PS[:, 4 + b, :], ACT.Copy).then_inc(S["u0_os"], 1)

                def unit(g, b, first=False):
                    u = 2 * g + b
                    for j in range(TB):
                        if first and b == 0 and j == 1:
                            act.wait_ge(S["sp_parts"], T)
                        for hp in range(2):
                            act.wait_ge(S["u0_scores"], 8 * u + 2 * j + hp + 1)
                            if not (first and b == 0):
                                act.wait_ge(S["u0_av"], 4 * u + j - 3)
                            act_fn(EJ[j][:, 2 * hp:2 * hp + 2, 0:N - j * P], PS[:, 2 * hp:2 * hp + 2, 0:N - j * P],
                                   ACT.Square).then_inc(S["u0_square"], 1)
                        if j == 2 and not (first and b == 0):
                            output(u - 1, 1 - b, first)
                unit(0, 0, True)
                unit(0, 1, True)
                with act.Fori(1, 4) as g:
                    for b in range(B):
                        unit(g, b)
                output(7, 1, False)
                evacuate_xt(2)

            def route(n):
                layer_norm(3 + 2 * n)
                for h in range(2):
                    probs = pe_[:, TB * h:TB * h + TB, 0:NE]
                    act.wait_ge(S["g_shift"], 2 * n + h + 1)
                    act_fn(probs, probs, ACT.Exp).then_inc(S["g_exp"], 1)
                    for t in range(TB * h, TB * h + TB):
                        act_fn(SRC[:, t, 0:D], XN[:, t, :], ACT.Copy).then_inc(S["g_copy"], 1)

            def shared(n):
                def silu(t):
                    q = n * T + t
                    act.wait_ge(S["s_h"], q + 1)
                    if t >= 2:
                        act.wait_ge(S["s_g"], q - 1)
                    act_fn(HSH[t % 2], PS[:, t % 2, 0:SI], ACT.Silu).then_inc(S["s_silu"], 1)
                silu(0)
                silu(1)
                for t in range(T):
                    q = n * T + t
                    act.wait_ge(S["s_gt_psum"], q + 1)
                    if t:
                        act.wait_ge(S["s_out"], q)
                    act_fn(GTS[:, 0:2, :], PS[:, 6, 0:2 * P].rearrange("p (k t) -> p k t", k=2), ACT.Copy)
                    act_fn(GTS[0:SI - 2 * P, 2, :], PS[0:SI - 2 * P, 6, 2 * P:3 * P], ACT.Copy).then_inc(S["s_gt"], 1)
                    if t + 2 < T:
                        silu(t + 2)

            def experts(n):
                def turned_g(e, k, fresh):
                    act.wait_ge(S["e_gt_psum"], NE * n + e + 1)
                    if not fresh:
                        act.wait_ge(S["e_out"], NE * n + e - 1)
                    act_fn(GT[k % 2], PS[0:IH, 6, :].rearrange("p (i s) -> p i s", i=2), ACT.Copy).then_inc(S["e_gt"], 1)

                def weigh(e, k, fresh):
                    act.wait_ge(S["e_out"], NE * n + e + 1)
                    act.wait_ge(S["e_meta"], NE * n + e + 1)
                    if not fresh:
                        act.wait_ge(S["y_added"], 32 * (NE * n + e) - 32 * (NB - 1))
                    for s in range(2):
                        last = act_fn(OB[k][:, s, :], PS[:, 7, s * D:(s + 1) * D], ACT.Copy, scale=meta_w[:, k, s:s + 1])
                    last.then_inc(S["e_ob"], 1)

                def step(e, k, first=False):
                    before = k - 1 if k else NB - 1
                    for s in range(2):
                        act.wait_ge(S["e_h"], 2 * (NE * n + e) + s + 1)
                        if not (first and k < 2):
                            act.wait_ge(S["e_g"], 2 * (NE * n + e) + s - 3)
                        act_fn(HE[k % 2][s], PS[:, 2 + 2 * (k % 2) + s, 0:INTER], ACT.Silu).then_inc(S["e_silu"], 1)
                        if not (first and k == 0):
                            if s == 0:
                                turned_g(e - 1, before, first and k < 3)
                            else:
                                weigh(e - 1, before, first)
                for k in range(NB):
                    step(k, k, True)
                with act.Fori(1, NE // NB) as h:
                    for k in range(NB):
                        step(NB * h + k, k)
                turned_g(NE - 1, NB - 1, False)
                weigh(NE - 1, NB - 1, False)

            def attn1():
                layer_norm(4)
                act.wait_ge(S["lam_sum"], 1)
                act_fn(lam[:, 1:3], m4[:, 0:2], ACT.Exp).then_inc(S["lam_exp"], 1)
                for r in range(9):
                    if r < 8:
                        act.wait_ge(S["sp_psum"], T + r + 1)
                        split_high(T + r, PT[1][r // 2 % 2][0][:, qk_part(r), :], PS[:, 4 + r % 2:5 + r % 2, :])
                    if r:
                        split_mid(T + r - 1, (r - 1) % 2, PT[1][(r - 1) // 2 % 2][1][:, qk_part(r - 1), :], 1)
                def max_rows(w, first=False):
                    act.wait_ge(S["u1_mt"], w + 1)
                    if not first:
                        act.wait_ge(S["u1_mrow"], 16 * w)
                    act_fn(mr[:, :], MT, ACT.Copy).then_inc(S["u1_mr"], 1)

                def output(u, b, fresh=False):
                    act.wait_ge(S["u1_av"], 4 * u + 4)
                    if not fresh:
                        act.wait_ge(S["u1_ot"], u - 1)
                    act_fn(OS[:, b, :], PS[:, 6, :], ACT.Copy).then_inc(S["u1_os"], 1)

                def unit(i4, u4, first=False, last=False):
                    u = 4 * i4 + u4
                    for j in range(TB):
                        if not (first and u4 == 0 and j < 2):
                            act.wait_ge(S["u1_av"], 4 * u + j - 1)
                        elif j == 1:
                            act.wait_ge(S["sp_stored10"], 2 * STORED)
                            act.wait_ge(S["sp_stored11"], 2 * STORED)
                        for m in range(MU):
                            act.wait_ge(S["u1_scores"], 16 * u + 4 * j + m + 1)
                            act_fn(E[j % 2][:, m, :], PS[:, RING[16 * u4 + 4 * j + m], :], ACT.Exp, scale=SCALE1)\
                                .then_inc(S["u1_exp"], 1)
                            if j == 1 and m == 3 and not (last and u4 == 3):
                                max_rows(u + 1)
                            if j == 0 and m == 3 and not (first and u4 == 0):
                                output(u - 1, (u4 + 1) % 2, first and u4 <= 2)
                max_rows(0, True)
                for t in range(T):
                    act.wait_ge(S["a1_v_psum"], t + 1)
                    act_fn(V[:, t, :], PS[:, t % 2, 0:D], ACT.Copy).then_inc(S["a1_v"], 1)
                for u4 in range(4):
                    unit(0, u4, first=True)
                with act.Fori(1, 3) as i4:
                    for u4 in range(4):
                        unit(i4, u4)
                for u4 in range(4):
                    unit(3, u4, last=True)
                output(15, 1)
                act.wait_ge(S["rms_var"], 1)
                act_fn(rms[:, 0:2, :], rms[:, 0:2, :], ACT.Sqrt).then_inc(S["rms_rstd"], 1)
                evacuate_xt(6, subw[:, 0:1])

            ffn(0)
            attn0()
            ffn(1)
            route(0)
            shared(0)
            experts(0)
            attn1()
            route(1)
            shared(1)
            experts(1)

        @block.gpsimd
        def _(pool):
            ch = Chain(pool, S["pool_self"])
            p = nc.gpsimd
            p.memset(ep[:, :, LE:LPAD], -1.0)
            p.memset(rep[:, :, 2:8], -1.0)
            p.memset(pe_[:, :, NE:EPAD], -1.0)
            p.memset(rep8[:, :, TOPK:8], -1.0)
            ch.link(p.memset(VA[:, :, :, :, :], 0.0))
            pool.wait_ge(S["const_in"], 16 * 7)
            pool.wait_ge(S["ident_in"], 16)
            p.tensor_copy(identb[:, :], ident[:, :])
            p.tensor_copy(tri[:, :], trif[:, :])
            p.memset(ones[:, :], 1.0)
            p.memset(one[:, :], 1.0)
            p.memset(VA[:, :, :, :, HD:HD + 1], 1.0).then_inc(S["pool_const"], 4)

            def split_low(q, r, mid, low, n):
                pool.wait_ge(S["sp_mid"], q + 1)
                p.tensor_tensor(low, R1[r].rearrange("p (x t) -> p x t", x=n), mid, ALU.subtract).then_inc(S["sp_parts"], 1)

            def attn0():
                for s in range(T + 4):
                    if s < T:
                        r = s % 2
                        pool.wait_ge(S["a0_rope"], s + 1)
                        if s >= 4:
                            pool.wait_ge(S["sp_psum"], s - 3)
                        p.tensor_tensor(Y4[s % 4], RT1[r], RT2[r], ALU.add).then_inc(S["a0_sum"], 1)
                    t = s - 1
                    if 0 <= t < T:
                        y = Y4[t % 4].rearrange("p (h e) -> p h e", e=HD)
                        pool.wait_ge(S["a0_mean"], t + 1)
                        p.tensor_tensor(y, y, bc(hs2[:, t % 2, :], [P, 32, HD], 2), ALU.subtract).then_inc(S["a0_center"], 1)
                    t = s - 4
                    if 0 <= t < T:
                        cols = slice((t % TB) * P, (t % TB + 1) * P)
                        split_low(t, t % 2, PT[0][t // TB][1][:, :, cols], PT[0][t // TB][2][:, :, cols], 4)
                pool.wait_ge(S["a0_v"], T)

                def unit(g, b, first=False):
                    u = 2 * g + b
                    if not first:
                        pool.wait_ge(S["u0_av"], 4 * u - 4)
                    src = V[:, TB * b:TB * b + TB, bass.ds(g * (MU * HD), MU * HD)].rearrange("p i (m e) -> p i m e", m=MU)
                    p.tensor_tensor(VA[:, b, :, :, 0:HD], src, one[:, :].unsqueeze(2).unsqueeze(3)
                                    .broadcast_to([P, TB, MU, HD]), ALU.mult).then_inc(S["u0_va"], 1)
                    for j in range(TB):
                        pool.wait_ge(S["u0_square"], 8 * u + 2 * j + 2)
                        diag = EJ[j][:, :, 0:P]
                        p.tensor_tensor(diag, diag, bc(mask[:, :], [P, MU, P], 1), ALU.mult).then_inc(S["u0_masked"], 1)
                unit(0, 0, True)
                unit(0, 1, True)
                with pool.Fori(1, 4) as g:
                    for b in range(B):
                        unit(g, b)

            def dispatch(n):
                pool.wait_ge(S["init_rows"], 64 + 32 * n)
                for t in range(T):
                    if t % TB == 0:
                        pool.wait_ge(S["g_weight"], 2 * n + t // TB + 1)
                    pool.wait_ge(S["g_copy"], n * T + t + 1)
                    for k in range(TOPK):
                        p.indirect_dma_start(xbuf, bass.IndirectOffsetOnAxis(ap=idx[:, t, k:k + 1], axis=0),
                                             SRC[:, t, :], None, bounds_check=SLOTS - 1, oob_is_err=False)\
                            .then_inc(S[f"g_scatter{t % 2}"], 16)

            def experts(n):
                def add(e, k, first=False):
                    if not (first and n == 0):
                        pool.wait_ge(S["pool_turn"], NE * n + e)
                    pool.wait_ge(S["e_ob"], NE * n + e + 1)
                    if not first:
                        pool.wait_ge(S["y_added"], 32 * (NE * n + e))
                    p.tensor_tensor(turn[:, :], one[:, :], one[:, :], ALU.mult).then_inc(S["pool_turn"], 1)
                    for s in range(2):
                        p.indirect_dma_start(y_dram[n], bass.IndirectOffsetOnAxis(ap=meta_i[:, k, s:s + 1], axis=0),
                                             OB[k][:, s, :], None, bounds_check=B * N + 2 * P - 1, oob_is_err=True,
                                             compute_op=ALU.add).then_inc(S["y_added"], 16)
                pool.wait_ge(S["y_stored"], 16 * T * (n + 1))
                for k in range(NB):
                    add(k, k, k == 0)
                with pool.Fori(1, NE // NB) as h:
                    for k in range(NB):
                        add(NB * h + k, k)

            def attn1():
                for r in range(8):
                    split_low(T + r, r % 2, PT[1][r // 2 % 2][1][:, qk_part(r), :], PT[1][r // 2 % 2][2][:, qk_part(r), :], 1)
                pool.wait_ge(S["sp_parts"], 2 * T)
                for r in range(4):
                    if r == 2:
                        pool.wait_ge(S["sp_stored00"], 2 * STORED)
                        pool.wait_ge(S["sp_stored01"], 2 * STORED)
                    last = p.memset(KS[r][64:96, :, :], 1.0)
                last.then_inc(S["stack_pad"], 1)
                pool.wait_ge(S["stack_pad"], 1)

                def stage_v(u, b, g, fresh):
                    if not fresh:
                        pool.wait_ge(S["u1_av"], 4 * u - 4)
                    src = V[:, TB * b:TB * b + TB, bass.ds(g * 32, 32)].rearrange("p i (m e) -> p i m e", m=2)
                    p.tensor_tensor(VA[:, b, :, 0:2, 0:HD], src, one[:, :].unsqueeze(2).unsqueeze(3).broadcast_to([P, TB, 2, HD]), ALU.mult).then_inc(S["u1_va"], 1)

                def split_maxima(w, par, first=False):
                    pool.wait_ge(S["u1_maxed"], 16 * w + 16)
                    if not first:
                        pool.wait_ge(S["u1_mt"], w)
                    neg = nm[:, par, :, :]
                    p.tensor_tensor(mp[:, :, 0, :], neg, bc(one[:, :], [P, TB, MU], 2), ALU.mult).then_inc(S["u1_sp"], 1)
                    pool.wait_ge(S["u1_sp"], 3 * w + 1)
                    p.tensor_tensor(nmr[:, :, :], neg, mp[:, :, 0, :], ALU.subtract).then_inc(S["u1_sp"], 1)
                    pool.wait_ge(S["u1_sp"], 3 * w + 2)
                    p.tensor_tensor(mp[:, :, 1, :], nmr[:, :, :], bc(one[:, :], [P, TB, MU], 2), ALU.mult).then_inc(S["u1_sp"], 1)
                    pool.wait_ge(S["u1_sp"], 3 * w + 3)
                    p.tensor_tensor(mp[:, :, 2, :], nmr[:, :, :], mp[:, :, 1, :], ALU.subtract).then_inc(S["u1_split"], 1)

                def unit(i4, u4, first=False, last=False):
                    if last and u4 == 3:
                        return
                    u = 4 * i4 + u4
                    split_maxima(u + 1, (u4 + 1) % 2)
                    if not (first and u4 == 0):
                        stage_v(u + 1, (u4 + 1) % 2, 2 * i4 + (u4 + 1) // 2, False)
                split_maxima(0, 0, True)
                pool.wait_ge(S["a1_v"], T)
                stage_v(0, 0, 0, True)
                stage_v(1, 1, 0, True)
                for u4 in range(4):
                    unit(0, u4, first=True)
                with pool.Fori(1, 3) as i4:
                    for u4 in range(4):
                        unit(i4, u4)
                for u4 in range(4):
                    unit(3, u4, last=True)

            attn0()
            dispatch(0)
            experts(0)
            attn1()
            dispatch(1)
            experts(1)


def kernel(**inputs):
    import numpy as np
    import concourse.bacc as bacc
    from concourse.bass_utils import run_bass_kernel_spmd as run

    def rows(a):
        return np.ascontiguousarray(a.reshape(-1, 128, a.shape[-1]).transpose(1, 0, 2))

    i = {k: np.asarray(v) for k, v in inputs.items()}
    f = np.float32
    arrays = {"x": i["L0_attn_x"].reshape(B * N, D)}
    lora_a = i["L0_ffn_lora_A"].reshape(LE * RANK, D)
    arrays["wf"] = rows(np.concatenate([i["L0_ffn_weight"].T, lora_a.T, i["L0_ffn_router_w"].T], 1))
    arrays["lb"] = i["L0_ffn_lora_B"].transpose(0, 2, 1).reshape(LE * RANK, D)
    arrays["wa0"] = rows(np.concatenate([i["L0_attn_w_qkv"], i["L0_attn_w_out"]], 1))
    arrays["ln_scale"], arrays["ln_bias"] = i["L0_attn_ln_scale"], i["L0_attn_ln_bias"]
    arrays["wa1"] = rows(np.concatenate([i["L1_attn_Wq"].T, i["L1_attn_Wk"].T, i["L1_attn_Wv"].T, i["L1_attn_Wo"].T], 1))
    for short, name in (("lq1", "lambda_q1"), ("lk1", "lambda_k1"), ("lq2", "lambda_q2"), ("lk2", "lambda_k2"),
                        ("subln", "subln_weight")):
        arrays[short] = i["L1_attn_" + name]
    arrays["gw"] = rows(i["L1_ffn_gate_w"].T)
    w13 = np.concatenate([i["L1_ffn_w1"], i["L1_ffn_w3"]], 2)
    arrays["w13"] = w13.reshape(NE, C, P, 2 * INTER).transpose(2, 0, 1, 3).reshape(P, -1)
    arrays["w2"] = i["L1_ffn_w2"].reshape(NE, 2, IH, D).transpose(0, 2, 1, 3).reshape(NE * IH, 2 * D)
    arrays["sw13"] = rows(np.concatenate([i["L1_ffn_sw1"], i["L1_ffn_sw3"]], 1))
    arrays["sw2"] = rows(np.concatenate([i["L1_ffn_sw2"], np.zeros((3 * P - SI, D), f)], 0))
    arrays["ident"] = np.eye(P, dtype=f)
    arrays["mask"] = np.triu(np.ones((P, P), f))
    arrays["trif"] = np.triu(np.ones((P, P), f), 1)
    arrays["slot0"] = np.tile(np.arange(NE, dtype=f) * CAP + 1, (P, 1))
    arrays["tok"] = np.arange(B * N, dtype=f).reshape(T, P).T
    empty = np.zeros((P, 2, ROW), f)
    empty[:, :, D] = B * N + np.arange(2 * P).reshape(2, P).T
    arrays["empty"] = empty
    inv = (f(1.0) / f(10000.0) ** (np.arange(0, HD, 2, dtype=f) / f(HD))).astype(f)
    angle = np.arange(N, dtype=f)[:, None] * inv[None, :]
    c, s = np.cos(angle), np.sin(angle)
    arrays["rope_c"] = rows(np.concatenate([c, c], 1))
    arrays["rope_s"] = rows(np.concatenate([-s, s], 1))
    arrays = {k: np.ascontiguousarray(v) for k, v in arrays.items()}

    nc = bacc.Bacc("TRN2", target_bir_lowering=False, num_devices=1)
    d = {k: nc.dram_tensor(k + "_dram", v.shape, F32, kind="ExternalInput").ap() for k, v in arrays.items()}
    out = nc.dram_tensor("out_dram", (B, N, D), F32, kind="ExternalOutput").ap()
    macaron_kernel(nc, d, out)
    r = run(nc, [{k + "_dram": v for k, v in arrays.items()}], core_ids=[0])
    return r.results[0]["out_dram"]
```
